# Optimizing a Trainium2 kernel written in Bass

```python
import numpy as np
import jax
import jax.numpy as jnp

def _softmax(x, axis=-1):
    return jax.nn.softmax(x, axis=axis)

def _gelu(x):
    return jax.nn.gelu(x, approximate=True)

def _silu(x):
    return jax.nn.silu(x)

def _sigmoid(x):
    return jax.nn.sigmoid(x)

def _layernorm(x, axis=-1, eps=1e-05):
    m = jnp.mean(x, axis=axis, keepdims=True)
    v = jnp.var(x, axis=axis, keepdims=True)
    return (x - m) / jnp.sqrt(v + eps)

def _scatter_add(tgt, idx, src, axis=0):
    return tgt.at[idx].add(src)

def _segment_sum(src, seg, n):
    return jax.ops.segment_sum(src, seg, n)
kernel_name = 'mk_prb_d4_jaxref_r8_6cdce6'

def setup_inputs(seed: int=0):
    np.random.seed(seed)
    _w = jnp.asarray

    def _L0_attn_setup():
        import jax, jax.numpy as jnp
        import numpy as np
        N_HEADS = 16
        N_KV_HEADS = 4
        MAX_TIMESCALE = 10000.0

        def rms_norm(x):
            var = jnp.mean(jnp.square(x.astype(jnp.float32)), axis=-1, keepdims=True)
            return (x * jax.lax.rsqrt(var + 1e-06)).astype(x.dtype)

        def rotate_half(x):
            x1, x2 = jnp.split(x, 2, axis=-1)
            return jnp.concatenate([-x2, x1], axis=-1)

        def sine_table(features, length):
            fraction = jnp.arange(0, features, 2, dtype=jnp.float32) / features
            inv_freq = 1.0 / MAX_TIMESCALE ** fraction
            sinusoid = jnp.arange(length, dtype=jnp.float32)[:, None] * inv_freq[None, :]
            sinusoid = jnp.concatenate([sinusoid, sinusoid], axis=-1)
            return (jnp.sin(sinusoid), jnp.cos(sinusoid))
        key = jax.random.key(seed)
        ks = jax.random.split(key, 5)
        B, T, C = (2, 128, 256)
        N, K = (N_HEADS, N_KV_HEADS)
        H = C // N
        init_std = np.sqrt(2.0 / (5.0 * C))
        wang_std = 2.0 / 24 / np.sqrt(N * H)
        x = jax.random.normal(ks[0], (B, T, C), dtype=jnp.float32)
        q_kernel = jax.random.normal(ks[1], (C, N * H), dtype=jnp.float32) * init_std
        k_kernel = jax.random.normal(ks[2], (C, K * H), dtype=jnp.float32) * init_std
        v_kernel = jax.random.normal(ks[3], (C, K * H), dtype=jnp.float32) * init_std
        out_kernel = jax.random.normal(ks[4], (N * H, C), dtype=jnp.float32) * wang_std
        return {'x': x, 'q_kernel': q_kernel, 'k_kernel': k_kernel, 'v_kernel': v_kernel, 'out_kernel': out_kernel}
    _L0_attn_in = _L0_attn_setup()

    def _L0_ffn_setup():
        import jax, jax.numpy as jnp
        import numpy as np
        TOP_K = 2
        key = jax.random.key(seed)
        ks = jax.random.split(key, 5)
        B, S, D, F, E = (2, 128, 256, 512, 8)
        scale_d = 1.0 / np.sqrt(D)
        scale_f = 1.0 / np.sqrt(F)
        return {'hidden_states': jax.random.normal(ks[0], (B, S, D), dtype=jnp.float32), 'router_w': jax.random.normal(ks[1], (D, E), dtype=jnp.float32) * scale_d, 'w1': jax.random.normal(ks[2], (E, D, F), dtype=jnp.float32) * scale_d, 'v1': jax.random.normal(ks[3], (E, D, F), dtype=jnp.float32) * scale_d, 'w2': jax.random.normal(ks[4], (E, F, D), dtype=jnp.float32) * scale_f}
    _L0_ffn_in = _L0_ffn_setup()

    def _L1_attn_setup():
        import jax, jax.numpy as jnp
        import numpy as np
        D_MODEL = 256
        N_HEADS = 16
        HEAD_DIM = D_MODEL // N_HEADS

        def _alibi_slopes(n_heads: int) -> jnp.ndarray:
            start = 2.0 ** (-8.0 / n_heads)
            return jnp.asarray([start * start ** i for i in range(n_heads)], dtype=jnp.float32)
        key = jax.random.key(seed)
        ks = jax.random.split(key, 9)
        B, S, D = (2, 256, D_MODEL)
        scale = 1.0 / np.sqrt(D)
        return {'x': jax.random.normal(ks[0], (B, S, D), dtype=jnp.float32), 'wq': jax.random.normal(ks[1], (D, D), dtype=jnp.float32) * scale, 'bq': jnp.zeros((D,), dtype=jnp.float32), 'wk': jax.random.normal(ks[2], (D, D), dtype=jnp.float32) * scale, 'bk': jnp.zeros((D,), dtype=jnp.float32), 'wv': jax.random.normal(ks[3], (D, D), dtype=jnp.float32) * scale, 'bv': jnp.zeros((D,), dtype=jnp.float32), 'wo': jax.random.normal(ks[4], (D, D), dtype=jnp.float32) * scale, 'bo': jnp.zeros((D,), dtype=jnp.float32)}
    _L1_attn_in = _L1_attn_setup()

    def _L1_ffn_setup():
        import jax, jax.numpy as jnp
        import numpy as np
        HIDDEN = 256
        INTER = 1024
        SCALE = 64.0

        def fwht(x):
            orig_shape = x.shape
            n = orig_shape[-1]
            x = x.reshape(-1, n)
            h = 1
            while h < n:
                x = x.reshape(-1, n // (2 * h), 2, h)
                a, b = (x[:, :, 0, :], x[:, :, 1, :])
                x = jnp.stack([a + b, a - b], axis=2).reshape(-1, n)
                h *= 2
            return (x / jnp.sqrt(jnp.asarray(n, x.dtype))).reshape(orig_shape)
        key = jax.random.key(seed)
        ks = jax.random.split(key, 8)
        inp = jax.random.normal(ks[0], (4, 256, HIDDEN), dtype=jnp.float32)
        SU_ug = jnp.where(jax.random.bernoulli(ks[1], 0.5, (HIDDEN,)), 1.0, -1.0).astype(jnp.float32)
        SU_dp = jnp.where(jax.random.bernoulli(ks[2], 0.5, (INTER,)), 1.0, -1.0).astype(jnp.float32)
        Wscale_ug = jax.random.uniform(ks[3], (2 * INTER,), jnp.float32, 0.5, 1.5)
        Wscale_dp = jax.random.uniform(ks[4], (HIDDEN,), jnp.float32, 0.5, 1.5)
        W_up = jax.random.normal(ks[5], (INTER, HIDDEN), dtype=jnp.float32) * 0.02
        W_gate = jax.random.normal(ks[6], (INTER, HIDDEN), dtype=jnp.float32) * 0.02
        W_down = jax.random.normal(ks[7], (HIDDEN, INTER), dtype=jnp.float32) * 0.02
        return {'input': inp, 'SU_ug': SU_ug, 'SU_dp': SU_dp, 'Wscale_ug': Wscale_ug, 'Wscale_dp': Wscale_dp, 'W_up': W_up, 'W_gate': W_gate, 'W_down': W_down}
    _L1_ffn_in = _L1_ffn_setup()

    def _L2_attn_setup():
        import jax, jax.numpy as jnp
        import numpy as np
        D_MODEL = 256
        N_HEADS = 16
        HEAD_DIM = D_MODEL // N_HEADS
        SCALE = HEAD_DIM ** (-0.5)
        key = jax.random.key(seed)
        ks = jax.random.split(key, 9)
        B, L, D = (4, 512, D_MODEL)
        s = 1.0 / np.sqrt(D)
        inp = {'x': jax.random.normal(ks[0], (B, L, D), dtype=jnp.float32)}
        inp['Wq'] = jax.random.normal(ks[1], (D, D), dtype=jnp.float32) * s
        inp['bq'] = jnp.zeros((D,), dtype=jnp.float32)
        inp['Wk'] = jax.random.normal(ks[2], (D, D), dtype=jnp.float32) * s
        inp['bk'] = jnp.zeros((D,), dtype=jnp.float32)
        inp['Wv'] = jax.random.normal(ks[3], (D, D), dtype=jnp.float32) * s
        inp['bv'] = jnp.zeros((D,), dtype=jnp.float32)
        inp['Wo'] = jax.random.normal(ks[4], (D, D), dtype=jnp.float32) * s
        inp['bo'] = jnp.zeros((D,), dtype=jnp.float32)
        return inp
    _L2_attn_in = _L2_attn_setup()

    def _L2_ffn_setup():
        import jax, jax.numpy as jnp
        import numpy as np
        B, S, H = (2, 256, 256)
        FFN = 128
        E = 8
        TOP_K = 2
        key = jax.random.key(seed)
        ks = jax.random.split(key, 5)
        scale = 0.02
        hidden_states = jax.random.normal(ks[0], (B, S, H), dtype=jnp.float32)
        Wg = jax.random.normal(ks[1], (E, H), dtype=jnp.float32) * scale
        W1 = jax.random.normal(ks[2], (E, FFN, H), dtype=jnp.float32) * scale
        W3 = jax.random.normal(ks[3], (E, FFN, H), dtype=jnp.float32) * scale
        W2 = jax.random.normal(ks[4], (E, H, FFN), dtype=jnp.float32) * scale
        bias = jnp.zeros((E,), dtype=jnp.float32)
        return {'hidden_states': hidden_states, 'Wg': Wg, 'W1': W1, 'W2': W2, 'W3': W3, 'bias': bias}
    _L2_ffn_in = _L2_ffn_setup()

    def _L3_attn_setup():
        import jax, jax.numpy as jnp
        import numpy as np
        from jax.scipy.linalg import solve_triangular
        EMB = 256
        NKH = 16
        NVH = 32
        DK = 128
        DV = 128
        KSZ = 4
        EPS = 1e-06
        CHUNK = 64
        KEY_DIM = NKH * DK
        VAL_DIM = NVH * DV
        CONV_DIM = 2 * KEY_DIM + VAL_DIM
        B, S = (1, 512)

        def _chunk_gated_delta_rule(q, k, v, g, beta):
            dt = q.dtype
            prec = jax.lax.Precision.HIGHEST
            q = jnp.transpose(q, (0, 2, 1, 3)).astype(jnp.float32)
            k = jnp.transpose(k, (0, 2, 1, 3)).astype(jnp.float32)
            v = jnp.transpose(v, (0, 2, 1, 3)).astype(jnp.float32)
            beta = jnp.transpose(beta, (0, 2, 1)).astype(jnp.float32)
            g = jnp.transpose(g, (0, 2, 1)).astype(jnp.float32)
            b, h, s, dk = k.shape
            dv = v.shape[-1]
            nc = s // CHUNK
            q = q * jax.lax.rsqrt(jnp.float32(dk))
            v_beta = v * beta[..., None]
            k_beta = k * beta[..., None]
            qc = q.reshape(b, h, nc, CHUNK, dk)
            kc = k.reshape(b, h, nc, CHUNK, dk)
            kbc = k_beta.reshape(b, h, nc, CHUNK, dk)
            vbc = v_beta.reshape(b, h, nc, CHUNK, dv)
            gc = g.reshape(b, h, nc, CHUNK)
            g_cum = jnp.cumsum(gc, axis=-1)
            g_diff = g_cum[..., :, None] - g_cum[..., None, :]
            decay = jnp.exp(jnp.tril(g_diff))
            tri_incl = jnp.triu(jnp.ones((CHUNK, CHUNK), bool), k=0)
            L = -jnp.matmul(kbc, jnp.swapaxes(kc, -1, -2), precision=prec) * decay
            L = jnp.where(tri_incl, 0.0, L)
            eye = jnp.eye(CHUNK, dtype=jnp.float32)
            attn = solve_triangular(eye - L, jnp.broadcast_to(eye, L.shape), lower=True)
            v_intra = jnp.matmul(attn, vbc, precision=prec)
            k_cumdecay = jnp.matmul(attn, kbc * jnp.exp(g_cum)[..., None], precision=prec)
            state0 = jnp.zeros((b, h, dk, dv), jnp.float32)
            tri_strict = jnp.triu(jnp.ones((CHUNK, CHUNK), bool), k=1)
            xs = tuple((jnp.moveaxis(t, 2, 0) for t in (qc, kc, v_intra, k_cumdecay, g_cum, decay)))

            def scan_body(state, x):
                q_i, k_i, v_i, kcd_i, g_i, dm_i = x
                a_i = jnp.matmul(q_i, jnp.swapaxes(k_i, -1, -2), precision=prec) * dm_i
                a_i = jnp.where(tri_strict, 0.0, a_i)
                v_new = v_i - jnp.matmul(kcd_i, state, precision=prec)
                out_i = jnp.matmul(q_i * jnp.exp(g_i)[..., None], state, precision=prec) + jnp.matmul(a_i, v_new, precision=prec)
                g_last = g_i[..., -1]
                new_state = state * jnp.exp(g_last)[..., None, None] + jnp.matmul(jnp.swapaxes(k_i * jnp.exp(g_last[..., None] - g_i)[..., None], -1, -2), v_new, precision=prec)
                return (new_state, out_i)
            _, out = jax.lax.scan(scan_body, state0, xs)
            out = jnp.moveaxis(out, 0, 2).reshape(b, h, s, dv)
            return jnp.transpose(out, (0, 2, 1, 3)).astype(dt)
        key = jax.random.key(seed)
        ks = jax.random.split(key, 7)
        s = 0.02
        return {'hidden_states': jax.random.normal(ks[0], (B, S, EMB), jnp.float32), 'W_qkvz': jax.random.normal(ks[1], (EMB, 2 * KEY_DIM + 2 * VAL_DIM), jnp.float32) * s, 'W_ba': jax.random.normal(ks[2], (EMB, 2 * NVH), jnp.float32) * s, 'conv_kernel': jax.random.normal(ks[3], (KSZ, 1, CONV_DIM), jnp.float32) * 0.1, 'A_log': jnp.log(jax.random.uniform(ks[4], (NVH,), jnp.float32, 1e-09, 16.0)), 'dt_bias': jnp.ones((NVH,), jnp.float32), 'norm_weight': jnp.ones((DV,), jnp.float32), 'W_out': jax.random.normal(ks[5], (VAL_DIM, EMB), jnp.float32) * s}
    _L3_attn_in = _L3_attn_setup()

    def _L3_ffn_setup():
        import jax, jax.numpy as jnp
        import numpy as np
        HIDDEN = 256
        INTER = 688
        LUT_SIZE = 16

        def _ghost_linear(x, idx, lut):
            w = lut[idx]
            return jnp.einsum('bsh,oh->bso', x, w)
        key = jax.random.key(seed)
        k_x, k_lut, k_g, k_u, k_d = jax.random.split(key, 5)
        x = jax.random.normal(k_x, (2, 512, HIDDEN), dtype=jnp.float32)
        lut = jax.random.normal(k_lut, (LUT_SIZE,), dtype=jnp.float32) * 0.02
        gate_idx = jax.random.randint(k_g, (INTER, HIDDEN), 0, LUT_SIZE, dtype=jnp.int32)
        up_idx = jax.random.randint(k_u, (INTER, HIDDEN), 0, LUT_SIZE, dtype=jnp.int32)
        down_idx = jax.random.randint(k_d, (HIDDEN, INTER), 0, LUT_SIZE, dtype=jnp.int32)
        return {'x': x, 'lut': lut, 'gate_idx': gate_idx, 'up_idx': up_idx, 'down_idx': down_idx}
    _L3_ffn_in = _L3_ffn_setup()
    _d = {'L0_attn_x': _L0_attn_in['x'], 'L0_attn_q_kernel': _L0_attn_in['q_kernel'], 'L0_attn_k_kernel': _L0_attn_in['k_kernel'], 'L0_attn_v_kernel': _L0_attn_in['v_kernel'], 'L0_attn_out_kernel': _L0_attn_in['out_kernel'], 'L0_ffn_router_w': _L0_ffn_in['router_w'], 'L0_ffn_w1': _L0_ffn_in['w1'], 'L0_ffn_v1': _L0_ffn_in['v1'], 'L0_ffn_w2': _L0_ffn_in['w2'], 'L1_attn_wq': _L1_attn_in['wq'], 'L1_attn_bq': _L1_attn_in['bq'], 'L1_attn_wk': _L1_attn_in['wk'], 'L1_attn_bk': _L1_attn_in['bk'], 'L1_attn_wv': _L1_attn_in['wv'], 'L1_attn_bv': _L1_attn_in['bv'], 'L1_attn_wo': _L1_attn_in['wo'], 'L1_attn_bo': _L1_attn_in['bo'], 'L1_ffn_SU_ug': _L1_ffn_in['SU_ug'], 'L1_ffn_SU_dp': _L1_ffn_in['SU_dp'], 'L1_ffn_Wscale_ug': _L1_ffn_in['Wscale_ug'], 'L1_ffn_Wscale_dp': _L1_ffn_in['Wscale_dp'], 'L1_ffn_W_up': _L1_ffn_in['W_up'], 'L1_ffn_W_gate': _L1_ffn_in['W_gate'], 'L1_ffn_W_down': _L1_ffn_in['W_down'], 'L2_attn_Wq': _L2_attn_in['Wq'], 'L2_attn_bq': _L2_attn_in['bq'], 'L2_attn_Wk': _L2_attn_in['Wk'], 'L2_attn_bk': _L2_attn_in['bk'], 'L2_attn_Wv': _L2_attn_in['Wv'], 'L2_attn_bv': _L2_attn_in['bv'], 'L2_attn_Wo': _L2_attn_in['Wo'], 'L2_attn_bo': _L2_attn_in['bo'], 'L2_ffn_Wg': _L2_ffn_in['Wg'], 'L2_ffn_W1': _L2_ffn_in['W1'], 'L2_ffn_W2': _L2_ffn_in['W2'], 'L2_ffn_W3': _L2_ffn_in['W3'], 'L2_ffn_bias': _L2_ffn_in['bias'], 'L3_attn_W_qkvz': _L3_attn_in['W_qkvz'], 'L3_attn_W_ba': _L3_attn_in['W_ba'], 'L3_attn_conv_kernel': _L3_attn_in['conv_kernel'], 'L3_attn_A_log': _L3_attn_in['A_log'], 'L3_attn_dt_bias': _L3_attn_in['dt_bias'], 'L3_attn_norm_weight': _L3_attn_in['norm_weight'], 'L3_attn_W_out': _L3_attn_in['W_out'], 'L3_ffn_lut': _L3_ffn_in['lut'], 'L3_ffn_gate_idx': _L3_ffn_in['gate_idx'], 'L3_ffn_up_idx': _L3_ffn_in['up_idx'], 'L3_ffn_down_idx': _L3_ffn_in['down_idx']}
    _x0 = _d['L0_attn_x']
    _d['L0_attn_x'] = jax.random.normal(jax.random.fold_in(jax.random.key(seed), 1), (2, 512, 256), dtype=_x0.dtype)
    del _x0
    return _d

def reference(L0_attn_x, L0_attn_q_kernel, L0_attn_k_kernel, L0_attn_v_kernel, L0_attn_out_kernel, L0_ffn_router_w, L0_ffn_w1, L0_ffn_v1, L0_ffn_w2, L1_attn_wq, L1_attn_bq, L1_attn_wk, L1_attn_bk, L1_attn_wv, L1_attn_bv, L1_attn_wo, L1_attn_bo, L1_ffn_SU_ug, L1_ffn_SU_dp, L1_ffn_Wscale_ug, L1_ffn_Wscale_dp, L1_ffn_W_up, L1_ffn_W_gate, L1_ffn_W_down, L2_attn_Wq, L2_attn_bq, L2_attn_Wk, L2_attn_bk, L2_attn_Wv, L2_attn_bv, L2_attn_Wo, L2_attn_bo, L2_ffn_Wg, L2_ffn_W1, L2_ffn_W2, L2_ffn_W3, L2_ffn_bias, L3_attn_W_qkvz, L3_attn_W_ba, L3_attn_conv_kernel, L3_attn_A_log, L3_attn_dt_bias, L3_attn_norm_weight, L3_attn_W_out, L3_ffn_lut, L3_ffn_gate_idx, L3_ffn_up_idx, L3_ffn_down_idx):

    def _L0_attn_ref(x, q_kernel, k_kernel, v_kernel, out_kernel):
        import jax, jax.numpy as jnp
        import numpy as np
        N_HEADS = 16
        N_KV_HEADS = 4
        MAX_TIMESCALE = 10000.0

        def rms_norm(x):
            var = jnp.mean(jnp.square(x.astype(jnp.float32)), axis=-1, keepdims=True)
            return (x * jax.lax.rsqrt(var + 1e-06)).astype(x.dtype)

        def rotate_half(x):
            x1, x2 = jnp.split(x, 2, axis=-1)
            return jnp.concatenate([-x2, x1], axis=-1)

        def sine_table(features, length):
            fraction = jnp.arange(0, features, 2, dtype=jnp.float32) / features
            inv_freq = 1.0 / MAX_TIMESCALE ** fraction
            sinusoid = jnp.arange(length, dtype=jnp.float32)[:, None] * inv_freq[None, :]
            sinusoid = jnp.concatenate([sinusoid, sinusoid], axis=-1)
            return (jnp.sin(sinusoid), jnp.cos(sinusoid))
        B, T, C = x.shape
        N, K = (N_HEADS, N_KV_HEADS)
        G = N // K
        H = C // N
        q = rms_norm(jnp.dot(x, q_kernel))
        k = rms_norm(jnp.dot(x, k_kernel))
        v = jnp.dot(x, v_kernel)
        q = q.reshape(B, T, K, G, H)
        k = k.reshape(B, T, K, H)
        v = v.reshape(B, T, K, H)
        sin, cos = sine_table(H, T)
        qcos = cos[None, :, None, None, :]
        qsin = sin[None, :, None, None, :]
        kcos = cos[None, :, None, :]
        ksin = sin[None, :, None, :]
        q = (q * qcos + rotate_half(q) * qsin).astype(x.dtype)
        k = (k * kcos + rotate_half(k) * ksin).astype(x.dtype)
        scale = jax.lax.rsqrt(jnp.array(H, dtype=jnp.float32)).astype(q.dtype)
        logits = jnp.einsum('btkgh,bskh->bkgts', q * scale, k)
        probs = jax.nn.softmax(logits.astype(jnp.float32), axis=-1).astype(logits.dtype)
        encoded = jnp.einsum('bkgts,bskh->btkgh', probs, v)
        encoded = encoded.reshape(B, T, N * H)
        return jnp.dot(encoded, out_kernel)

    def _L0_ffn_ref(hidden_states, router_w, w1, v1, w2):
        import jax, jax.numpy as jnp
        import numpy as np
        TOP_K = 2
        B, S, D = hidden_states.shape
        E = router_w.shape[1]
        x = hidden_states.reshape(-1, D)
        router_logits = x @ router_w
        routing_weights = jax.nn.softmax(router_logits.astype(jnp.float32), axis=-1)
        top_w, top_i = jax.lax.top_k(routing_weights, TOP_K)
        top_w = top_w / jnp.sum(top_w, axis=-1, keepdims=True)
        onehot = jax.nn.one_hot(top_i, E, dtype=top_w.dtype)
        expert_weights = jnp.einsum('tk,tke->te', top_w, onehot).astype(x.dtype)
        h1 = jnp.einsum('td,edf->etf', x, w1)
        g = jax.nn.silu(h1) * jnp.einsum('td,edf->etf', x, v1)
        out = jnp.einsum('etf,efd,te->td', g, w2, expert_weights)
        return out.reshape(B, S, D)

    def _L1_attn_ref(x, wq, bq, wk, bk, wv, bv, wo, bo):
        import jax, jax.numpy as jnp
        import numpy as np
        D_MODEL = 256
        N_HEADS = 16
        HEAD_DIM = D_MODEL // N_HEADS

        def _alibi_slopes(n_heads: int) -> jnp.ndarray:
            start = 2.0 ** (-8.0 / n_heads)
            return jnp.asarray([start * start ** i for i in range(n_heads)], dtype=jnp.float32)
        B, S, D = x.shape
        H, hd = (N_HEADS, HEAD_DIM)

        def heads(y):
            return y.reshape(B, S, H, hd).transpose(0, 2, 1, 3)
        q = heads(x @ wq + bq)
        k = heads(x @ wk + bk)
        v = heads(x @ wv + bv)
        scores = jnp.einsum('bhqd,bhkd->bhqk', q, k) / jnp.sqrt(jnp.float32(hd))
        pos = jnp.arange(S)
        rel = pos[None, :] - pos[:, None]
        slopes = _alibi_slopes(H)
        bias = slopes[:, None, None] * rel.astype(jnp.float32)
        causal = jnp.where(rel > 0, -jnp.inf, 0.0).astype(jnp.float32)
        scores = scores + (bias + causal)[None]
        attn = jax.nn.softmax(scores, axis=-1)
        out = jnp.einsum('bhqk,bhkd->bhqd', attn, v)
        out = out.transpose(0, 2, 1, 3).reshape(B, S, D)
        return out @ wo + bo

    def _L1_ffn_ref(input, SU_ug, SU_dp, Wscale_ug, Wscale_dp, W_up, W_gate, W_down):
        import jax, jax.numpy as jnp
        import numpy as np
        HIDDEN = 256
        INTER = 1024
        SCALE = 64.0

        def fwht(x):
            orig_shape = x.shape
            n = orig_shape[-1]
            x = x.reshape(-1, n)
            h = 1
            while h < n:
                x = x.reshape(-1, n // (2 * h), 2, h)
                a, b = (x[:, :, 0, :], x[:, :, 1, :])
                x = jnp.stack([a + b, a - b], axis=2).reshape(-1, n)
                h *= 2
            return (x / jnp.sqrt(jnp.asarray(n, x.dtype))).reshape(orig_shape)
        n = SU_ug.shape[0]
        x = input.reshape(-1, n)
        x = fwht(x * SU_ug) / SCALE
        x_up = x @ W_up.T * (Wscale_ug[:INTER] * SCALE)
        x_gate = x @ W_gate.T * (Wscale_ug[INTER:] * SCALE)
        x = jax.nn.silu(x_gate) * x_up
        x = fwht(x * SU_dp) / SCALE
        x = x @ W_down.T * (Wscale_dp * SCALE)
        return x.reshape(input.shape)

    def _L2_attn_ref(x, Wq, bq, Wk, bk, Wv, bv, Wo, bo):
        import jax, jax.numpy as jnp
        import numpy as np
        D_MODEL = 256
        N_HEADS = 16
        HEAD_DIM = D_MODEL // N_HEADS
        SCALE = HEAD_DIM ** (-0.5)
        B, L, D = x.shape
        H, Hd = (N_HEADS, HEAD_DIM)
        q = jnp.einsum('bld,ed->ble', x, Wq) + bq
        k = jnp.einsum('bld,ed->ble', x, Wk) + bk
        v = jnp.einsum('bld,ed->ble', x, Wv) + bv
        phi_q = jax.nn.elu(q) + 1.0
        phi_k = jax.nn.elu(k) + 1.0
        phi_q = phi_q.reshape(B, L, H, Hd)
        phi_k = phi_k.reshape(B, L, H, Hd)
        v = v.reshape(B, L, H, Hd)
        kv_sum = jnp.cumsum(phi_k * v, axis=1)
        context = (phi_q * kv_sum).reshape(B, L, D) * SCALE
        return jnp.einsum('bld,ed->ble', context, Wo) + bo

    def _L2_ffn_ref(hidden_states, Wg, W1, W2, W3, bias):
        import jax, jax.numpy as jnp
        import numpy as np
        B, S, H = (2, 256, 256)
        FFN = 128
        E = 8
        TOP_K = 2
        bsz, seq_len, hidden_dim = hidden_states.shape
        x = hidden_states.reshape(-1, hidden_dim)
        router_logits = x @ Wg.T
        routing_weights = jax.nn.sigmoid(router_logits.astype(jnp.float32))
        scores = routing_weights + bias
        _, top_k_index = jax.lax.top_k(scores, TOP_K)
        top_k_weights = jnp.take_along_axis(routing_weights, top_k_index, axis=1)
        top_k_weights = top_k_weights / top_k_weights.sum(axis=-1, keepdims=True)
        top_k_weights = top_k_weights.astype(x.dtype)
        one_hot = jax.nn.one_hot(top_k_index, Wg.shape[0], dtype=x.dtype)
        expert_w = jnp.einsum('tk,tke->te', top_k_weights, one_hot)
        h1 = jnp.einsum('th,efh->tef', x, W1)
        h3 = jnp.einsum('th,efh->tef', x, W3)
        g = jax.nn.silu(h1) * h3 * expert_w[:, :, None]
        out = jnp.einsum('tef,ehf->th', g, W2)
        return out.reshape(bsz, seq_len, hidden_dim)

    def _L3_attn_ref(hidden_states, W_qkvz, W_ba, conv_kernel, A_log, dt_bias, norm_weight, W_out):
        import jax, jax.numpy as jnp
        import numpy as np
        from jax.scipy.linalg import solve_triangular
        EMB = 256
        NKH = 16
        NVH = 32
        DK = 128
        DV = 128
        KSZ = 4
        EPS = 1e-06
        CHUNK = 64
        KEY_DIM = NKH * DK
        VAL_DIM = NVH * DV
        CONV_DIM = 2 * KEY_DIM + VAL_DIM
        B, S = (1, 512)

        def _chunk_gated_delta_rule(q, k, v, g, beta):
            dt = q.dtype
            prec = jax.lax.Precision.HIGHEST
            q = jnp.transpose(q, (0, 2, 1, 3)).astype(jnp.float32)
            k = jnp.transpose(k, (0, 2, 1, 3)).astype(jnp.float32)
            v = jnp.transpose(v, (0, 2, 1, 3)).astype(jnp.float32)
            beta = jnp.transpose(beta, (0, 2, 1)).astype(jnp.float32)
            g = jnp.transpose(g, (0, 2, 1)).astype(jnp.float32)
            b, h, s, dk = k.shape
            dv = v.shape[-1]
            nc = s // CHUNK
            q = q * jax.lax.rsqrt(jnp.float32(dk))
            v_beta = v * beta[..., None]
            k_beta = k * beta[..., None]
            qc = q.reshape(b, h, nc, CHUNK, dk)
            kc = k.reshape(b, h, nc, CHUNK, dk)
            kbc = k_beta.reshape(b, h, nc, CHUNK, dk)
            vbc = v_beta.reshape(b, h, nc, CHUNK, dv)
            gc = g.reshape(b, h, nc, CHUNK)
            g_cum = jnp.cumsum(gc, axis=-1)
            g_diff = g_cum[..., :, None] - g_cum[..., None, :]
            decay = jnp.exp(jnp.tril(g_diff))
            tri_incl = jnp.triu(jnp.ones((CHUNK, CHUNK), bool), k=0)
            L = -jnp.matmul(kbc, jnp.swapaxes(kc, -1, -2), precision=prec) * decay
            L = jnp.where(tri_incl, 0.0, L)
            eye = jnp.eye(CHUNK, dtype=jnp.float32)
            attn = solve_triangular(eye - L, jnp.broadcast_to(eye, L.shape), lower=True)
            v_intra = jnp.matmul(attn, vbc, precision=prec)
            k_cumdecay = jnp.matmul(attn, kbc * jnp.exp(g_cum)[..., None], precision=prec)
            state0 = jnp.zeros((b, h, dk, dv), jnp.float32)
            tri_strict = jnp.triu(jnp.ones((CHUNK, CHUNK), bool), k=1)
            xs = tuple((jnp.moveaxis(t, 2, 0) for t in (qc, kc, v_intra, k_cumdecay, g_cum, decay)))

            def scan_body(state, x):
                q_i, k_i, v_i, kcd_i, g_i, dm_i = x
                a_i = jnp.matmul(q_i, jnp.swapaxes(k_i, -1, -2), precision=prec) * dm_i
                a_i = jnp.where(tri_strict, 0.0, a_i)
                v_new = v_i - jnp.matmul(kcd_i, state, precision=prec)
                out_i = jnp.matmul(q_i * jnp.exp(g_i)[..., None], state, precision=prec) + jnp.matmul(a_i, v_new, precision=prec)
                g_last = g_i[..., -1]
                new_state = state * jnp.exp(g_last)[..., None, None] + jnp.matmul(jnp.swapaxes(k_i * jnp.exp(g_last[..., None] - g_i)[..., None], -1, -2), v_new, precision=prec)
                return (new_state, out_i)
            _, out = jax.lax.scan(scan_body, state0, xs)
            out = jnp.moveaxis(out, 0, 2).reshape(b, h, s, dv)
            return jnp.transpose(out, (0, 2, 1, 3)).astype(dt)
        b, s, _ = hidden_states.shape
        vk = NVH // NKH
        qkvz = hidden_states @ W_qkvz
        ba = hidden_states @ W_ba
        mixed = qkvz.reshape(b, s, NKH, 2 * DK + 2 * vk * DV)
        q, k, v_raw, z_raw = jnp.split(mixed, [DK, 2 * DK, 2 * DK + vk * DV], axis=3)
        value = v_raw.reshape(b, s, NVH, DV)
        z = z_raw.reshape(b, s, NVH, DV)
        mixed_ba = ba.reshape(b, s, NKH, 2 * vk)
        b_raw, a_raw = jnp.split(mixed_ba, [vk], axis=3)
        b_gate = b_raw.reshape(b, s, NVH)
        a_gate = a_raw.reshape(b, s, NVH)
        qkv = jnp.concatenate([q.reshape(b, s, -1), k.reshape(b, s, -1), value.reshape(b, s, -1)], axis=-1)
        x = jnp.pad(qkv, ((0, 0), (KSZ - 1, 0), (0, 0)))
        conv = jax.lax.conv_general_dilated(x, conv_kernel, (1,), 'VALID', dimension_numbers=('NWC', 'WIO', 'NWC'), feature_group_count=CONV_DIM)
        qkv_c = jax.nn.silu(conv.astype(jnp.float32)).astype(hidden_states.dtype)
        q_c, k_c, v_c = jnp.split(qkv_c, [KEY_DIM, 2 * KEY_DIM], axis=-1)
        query = q_c.reshape(b, s, NKH, DK)
        key = k_c.reshape(b, s, NKH, DK)
        value = v_c.reshape(b, s, NVH, DV)
        beta = jax.nn.sigmoid(b_gate)
        g = (-jnp.exp(A_log.astype(jnp.float32)) * jax.nn.softplus(a_gate.astype(jnp.float32) + dt_bias.astype(jnp.float32))).astype(hidden_states.dtype)
        query = jnp.repeat(query, vk, axis=2)
        key = jnp.repeat(key, vk, axis=2)
        core = _chunk_gated_delta_rule(query, key, value, g, beta)
        xf = core.astype(jnp.float32) * jax.nn.silu(z.astype(jnp.float32))
        var = jnp.mean(xf * xf, axis=-1, keepdims=True)
        xf = xf * jax.lax.rsqrt(var + EPS) * norm_weight
        out = xf.astype(hidden_states.dtype).reshape(b, s, VAL_DIM)
        return out @ W_out

    def _L3_ffn_ref(x, lut, gate_idx, up_idx, down_idx):
        import jax, jax.numpy as jnp
        import numpy as np
        HIDDEN = 256
        INTER = 688
        LUT_SIZE = 16

        def _ghost_linear(x, idx, lut):
            w = lut[idx]
            return jnp.einsum('bsh,oh->bso', x, w)
        gate = _ghost_linear(x, gate_idx, lut)
        up = _ghost_linear(x, up_idx, lut)
        h = jax.nn.silu(gate) * up
        return _ghost_linear(h, down_idx, lut)
    x = L0_attn_x
    xn = _layernorm(x, axis=-1)
    x = x + _L0_attn_ref(xn, L0_attn_q_kernel, L0_attn_k_kernel, L0_attn_v_kernel, L0_attn_out_kernel) + _L0_ffn_ref(xn, L0_ffn_router_w, L0_ffn_w1, L0_ffn_v1, L0_ffn_w2)
    xn = _layernorm(x, axis=-1)
    x = x + _L1_attn_ref(xn, L1_attn_wq, L1_attn_bq, L1_attn_wk, L1_attn_bk, L1_attn_wv, L1_attn_bv, L1_attn_wo, L1_attn_bo) + _L1_ffn_ref(xn, L1_ffn_SU_ug, L1_ffn_SU_dp, L1_ffn_Wscale_ug, L1_ffn_Wscale_dp, L1_ffn_W_up, L1_ffn_W_gate, L1_ffn_W_down)
    xn = _layernorm(x, axis=-1)
    x = x + _L2_attn_ref(xn, L2_attn_Wq, L2_attn_bq, L2_attn_Wk, L2_attn_bk, L2_attn_Wv, L2_attn_bv, L2_attn_Wo, L2_attn_bo) + _L2_ffn_ref(xn, L2_ffn_Wg, L2_ffn_W1, L2_ffn_W2, L2_ffn_W3, L2_ffn_bias)
    xn = _layernorm(x, axis=-1)
    x = x + _L3_attn_ref(xn, L3_attn_W_qkvz, L3_attn_W_ba, L3_attn_conv_kernel, L3_attn_A_log, L3_attn_dt_bias, L3_attn_norm_weight, L3_attn_W_out) + _L3_ffn_ref(xn, L3_ffn_lut, L3_ffn_gate_idx, L3_ffn_up_idx, L3_ffn_down_idx)
    return x

_drawn_inputs = setup_inputs


def setup_inputs(seed=0):
    import zlib

    import numpy as np

    out = dict(_drawn_inputs(seed))
    spreads = {'L1_attn_bq': (0.0, 0.1),
     'L1_attn_bk': (0.0, 0.1),
     'L1_attn_bv': (0.0, 0.1),
     'L1_attn_bo': (0.0, 0.1),
     'L2_attn_bq': (0.0, 0.1),
     'L2_attn_bk': (0.0, 0.1),
     'L2_attn_bv': (0.0, 0.1),
     'L2_attn_bo': (0.0, 0.1),
     'L2_ffn_bias': (0.0, 0.1),
     'L3_attn_dt_bias': (1.0, 0.2),
     'L3_attn_norm_weight': (1.0, 0.2)}
    factors = {}
    for name, (base, spread) in spreads.items():
        noise = np.random.default_rng([zlib.crc32(name.encode()), seed]).standard_normal(out[name].shape)
        drawn = base * np.exp(spread * noise) if base else spread * noise
        out[name] = jnp.asarray(drawn.astype(out[name].dtype))
    for name, factor in factors.items():
        out[name] = (out[name] * factor).astype(out[name].dtype)
    return out
```

```python
from contextlib import ExitStack

import numpy as np

import concourse.bass as bass
from concourse import mybir

F32 = mybir.dt.float32
I32 = mybir.dt.int32
U32 = mybir.dt.uint32
ALU = mybir.AluOpType
ACT = mybir.ActivationFunctionType
AX = mybir.AxisListType

P = 128
B, T, C = 2, 512, 256
N = B * T
KC = C // P
TT = N // P
NH, HD = 16, 16
HP = 32
HG = P // HP
NG = NH // HG
BANK = 512


class Stage:

    def __init__(self, nc, name):
        self.nc, self.name, self.ctx, self.sems = nc, name, ExitStack(), []

    def __enter__(self):
        return self

    def __exit__(self, *error):
        if not error[0] and self.name != "all":
            with self.nc.Block() as block:
                @block.sync
                def _(sp):
                    for sem in self.sems:
                        sp.sem_clear(sem)
        self.ctx.close()

    def buf(self, name, shape, dtype=F32):
        return self.ctx.enter_context(self.nc.sbuf_tensor(f"{self.name}_{name}", shape, dtype))

    def sem(self, name):
        self.sems.append(self.ctx.enter_context(self.nc.semaphore(f"{self.name}_{name}")))
        return self.sems[-1]


def layer_norm(nc, name, ps, x, xn, mean_of):
    with Stage(nc, name) as s:
        square = s.buf("square", [P, KC, N])
        std = s.buf("std", [P, B, T])
        eps = s.buf("eps", [P, 1])
        mean_ready, centred, squared = s.sem("mean_ready"), s.sem("centred"), s.sem("squared")
        var_ready, std_ready, rstd_ready, normed = (
            s.sem("var_ready"), s.sem("std_ready"), s.sem("rstd_ready"), s.sem("normed"))
        eps_ready = s.sem("eps_ready")
        with nc.Block() as block:

            @block.tensor
            def _(pe):
                for b in range(B):
                    for k in range(KC):
                        mm = pe.matmul(ps[:, b, :], mean_of[:, :], x[:, k, b * T:(b + 1) * T],
                                       start=k == 0, stop=k == KC - 1)
                    mm.then_inc(mean_ready, 1)
                for b in range(B):
                    pe.wait_ge(squared, KC * (b + 1))
                    for k in range(KC):
                        mm = pe.matmul(ps[:, B + b, :], mean_of[:, :], square[:, k, b * T:(b + 1) * T],
                                       start=k == 0, stop=k == KC - 1)
                    mm.then_inc(var_ready, 1)

            @block.vector
            def _(dve):
                dve.memset(eps[:, :], 1e-5).then_inc(eps_ready, 1)
                for b in range(B):
                    dve.wait_ge(mean_ready, b + 1)
                    for k in range(KC):
                        part = slice(b * T, (b + 1) * T)
                        dve.tensor_tensor(xn[:, k, part], x[:, k, part], ps[:, b, :],
                                          ALU.subtract).then_inc(centred, 1)
                for b in range(B):
                    dve.wait_ge(std_ready, b + 1)
                    dve.reciprocal(std[:, b, :], std[:, b, :]).then_inc(rstd_ready, 1)
                    dve.wait_ge(rstd_ready, b + 1)
                    dve.wait_ge(squared, KC * (b + 1))
                    for k in range(KC):
                        part = slice(b * T, (b + 1) * T)
                        dve.tensor_tensor(xn[:, k, part], xn[:, k, part], std[:, b, :],
                                          ALU.mult).then_inc(normed, 1)

            @block.scalar
            def _(act):
                for b in range(B):
                    for k in range(KC):
                        act.wait_ge(centred, KC * b + k + 1)
                        part = slice(b * T, (b + 1) * T)
                        act.activation(square[:, k, part], xn[:, k, part],
                                       ACT.Square).then_inc(squared, 1)
                act.wait_ge(eps_ready, 1)
                for b in range(B):
                    act.wait_ge(var_ready, b + 1)
                    act.activation(std[:, b, :], ps[:, B + b, :], ACT.Sqrt,
                                   bias=eps[:, 0:1]).then_inc(std_ready, 1)


def rope_attention(nc, ps, d, x, xn):
    with Stage(nc, "a0") as s:
        wq, wk = s.buf("wq", [P, KC, NG * P]), s.buf("wk", [P, KC, NG * P])
        wv, wo = s.buf("wv", [P, KC, NG * HD]), s.buf("wo", [P, NG, C])
        rope = s.buf("rope", [P, 2, T])
        turn, sums_of, ones = s.buf("turn", [P, P]), s.buf("sums_of", [P, P]), s.buf("ones", [P, P])
        qk = s.buf("qk", [P, 2, B * NG, T])
        square = s.buf("square", [P, 4, T])
        rms = s.buf("rms", [P, 2 * B, T])
        turned = s.buf("turned", [P, 2, 2 * B, T])
        by_sin, by_cos = s.buf("by_sin", [P, 2, T]), s.buf("by_cos", [P, 2, T])
        values = s.buf("values", [P, TT * NG, HP])
        q_cur, k_cur = s.buf("q_cur", [P, 2, T]), s.buf("k_cur", [P, 2, T])
        v_cur = s.buf("v_cur", [P, 2, T // P, HP])
        probs = s.buf("probs", [P, 8, T])
        mixed = s.buf("mixed", [P, 2, T])
        recip = s.buf("recip", [P, 2, T])
        heads = s.buf("heads", [P, B * NG, T])
        eps = s.buf("eps", [P, 1])
        loaded, filled, v_ready, values_ready = (
            s.sem("loaded"), s.sem("filled"), s.sem("v_ready"), s.sem("values_ready"))
        proj_ready, raw_ready, sq_ready, sq_used = (
            s.sem("proj_ready"), s.sem("raw_ready"), s.sem("sq_ready"), s.sem("sq_used"))
        rms_ready, rrms_ready, turned_ready = (
            s.sem("rms_ready"), s.sem("rrms_ready"), s.sem("turned_ready"))
        swapped, sin_done, cos_done, roped = (
            s.sem("swapped"), s.sem("sin_done"), s.sem("cos_done"), s.sem("roped"))
        cur_ready, score_ready, probs_ready, probs_used = (
            s.sem("cur_ready"), s.sem("score_ready"), s.sem("probs_ready"), s.sem("probs_used"))
        mixed_ready, sums_ready, recip_ready, heads_ready = (
            s.sem("mixed_ready"), s.sem("sums_ready"), s.sem("recip_ready"), s.sem("heads_ready"))
        out_ready, added = s.sem("out_ready"), s.sem("added")
        NT = 2 * B * NG
        ST = T // P
        PER = 2 * ST * HG
        SCORES, PROBS = 4, 8

        def tile(t):
            return t // (B * NG), t // NG % B, t % NG

        with nc.Block() as block:

            @block.sync
            def _(sp):
                for to, of in ((wv, "a0_wv"), (wq, "a0_wq"), (wk, "a0_wk")):
                    sp.dma_start(to[:, :, :], d[of].rearrange("(k p) n -> p k n", p=P)).then_inc(loaded, 16)
                sp.dma_start(ones[:, :], d["ones"]).then_inc(loaded, 16)
                sp.dma_start(turn[:, :], d["turn"]).then_inc(loaded, 16)
                sp.dma_start(sums_of[:, :], d["sums_of"]).then_inc(loaded, 16)
                sp.dma_start(rope[:, :, :], d["rope"]).then_inc(loaded, 16)
                sp.dma_start(wo[:, :, :], d["a0_wo"].rearrange("(g p) n -> p g n", p=P)).then_inc(loaded, 16)

            @block.tensor
            def _(pe):
                pe.wait_ge(loaded, 8 * 16)
                for tt in range(TT):
                    for k in range(KC):
                        mm = pe.matmul(ps[:, 3, tt * 64:(tt + 1) * 64], xn[:, k, tt * P:(tt + 1) * P],
                                       wv[:, k, :], start=k == 0, stop=k == KC - 1)
                mm.then_inc(v_ready, 1)

                def add_squares(t):
                    kind, b, g = tile(t)
                    pe.wait_ge(sq_ready, t + 1)
                    pe.matmul(ps[:, 4 + kind * B + b, :], ones[:, :], square[:, t % 4, :],
                              start=g == 0, stop=g == NG - 1).then_inc(sq_used, 1)

                for t in range(NT):
                    kind, b, g = tile(t)
                    w = wk if kind else wq
                    if t >= 3:
                        pe.wait_ge(raw_ready, t - 2)
                    for k in range(KC):
                        mm = pe.matmul(ps[:, t % 3, :], w[:, k, g * P:(g + 1) * P],
                                       xn[:, k, b * T:(b + 1) * T], start=k == 0, stop=k == KC - 1)
                    mm.then_inc(proj_ready, 1)
                    if t >= 2:
                        add_squares(t - 2)
                add_squares(NT - 2)
                add_squares(NT - 1)
                for t in range(NT):
                    if t < 3:
                        pe.wait_ge(raw_ready, NT)
                    else:
                        pe.wait_ge(sin_done, t - 2)
                    kind, b, g = tile(t)
                    pe.matmul(ps[:, t % 3, :], turn[:, :], qk[:, kind, b * NG + g, :],
                              start=True, stop=True).then_inc(swapped, 1)
                pe.wait_ge(sin_done, NT)

                def mix(u, n):
                    v, st, j = n // (ST * HG), n // HG % ST, n % HG
                    pe.wait_ge(probs_ready, u * PER + n + 1 + SCORES)
                    pe.matmul(ps[j * HP:(j + 1) * HP, 4 + v, :], v_cur[:, v, st, :], probs[:, n % PROBS, :],
                              start=st == 0, stop=st == ST - 1).then_inc(probs_used, 1)

                def sum_weights(u, v):
                    pe.wait_ge(mixed_ready, 2 * u + v + 3)
                    pe.wait_ge(recip_ready, 2 * u + v + 1)
                    pe.matmul(ps[:, 6, :], sums_of[:, :], mixed[:, v, :],
                              start=True, stop=True).then_inc(sums_ready, 1)

                with pe.Fori(0, B * NG // 2) as u:
                    for v in range(2):
                        pe.wait_ge(cur_ready, u * 6 + 3 * v + 3)
                        for st in range(ST):
                            for j in range(HG):
                                n = (v * ST + st) * HG + j
                                pe.wait_ge(probs_ready, u * PER + n + 1)
                                rows = slice(j * HP, (j + 1) * HP)
                                pe.matmul(ps[:, n % SCORES, :], k_cur[rows, v, st * P:(st + 1) * P],
                                          q_cur[rows, v, :], start=True, stop=True).then_inc(score_ready, 1)
                            if st == 1 and v:
                                sum_weights(u, 0)
                            if v or st:
                                for j in range(HG):
                                    mix(u, n - 2 * HG + 1 + j)
                    for j in range(HG):
                        mix(u, PER - HG + j)
                    sum_weights(u, 1)
                for b in range(B):
                    pe.wait_ge(heads_ready, B * NG)
                    for m in range(KC):
                        for g in range(NG):
                            mm = pe.matmul(ps[:, b * KC + m, :], wo[:, g, m * P:(m + 1) * P],
                                           heads[:, b * NG + g, :], start=g == 0, stop=g == NG - 1)
                        mm.then_inc(out_ready, 1)

            @block.scalar
            def _(act):
                for t in range(NT):
                    kind, b, g = tile(t)
                    act.wait_ge(proj_ready, t + 1)
                    act.activation(qk[:, kind, b * NG + g, :], ps[:, t % 3, :],
                                   ACT.Copy).then_inc(raw_ready, 1)
                act.wait_ge(filled, 2)
                for r in range(2 * B):
                    act.wait_ge(sq_used, NG * (r + 1))
                    act.activation(rms[:, r, :], ps[:, 4 + r, :], ACT.Sqrt, bias=eps[:, 0:1],
                                   scale=1.0 / C).then_inc(rms_ready, 1)
                act.sem_inc(probs_ready, SCORES)
                with act.Fori(0, B * NG // 2) as u:
                    for n in range(PER):
                        act.wait_ge(score_ready, u * PER + n + 1)
                        act.wait_ge(probs_used, u * PER + n + 1)
                        act.activation(probs[:, n % PROBS, :], ps[:, n % SCORES, :], ACT.Exp,
                                       scale=HD ** -0.5).then_inc(probs_ready, 1)

            @block.gpsimd
            def _(pool):
                pool.sem_inc(probs_used, PROBS)
                pool.sem_inc(recip_ready, 1)
                pool.sem_inc(mixed_ready, 2)
                for t in range(NT):
                    kind, b, g = tile(t)
                    raw = qk[:, kind, b * NG + g, :]
                    pool.wait_ge(raw_ready, t + 1)
                    if t >= 4:
                        pool.wait_ge(sq_used, t - 3)
                    pool.tensor_tensor(square[:, t % 4, :], raw, raw, ALU.mult).then_inc(sq_ready, 1)
                for t in range(NT):
                    kind, b, g = tile(t)
                    pool.wait_ge(turned_ready, 2 * (kind * B + b) + 1)
                    if t >= 2:
                        pool.wait_ge(roped, t - 1)
                    pool.tensor_tensor(by_cos[:, t % 2, :], qk[:, kind, b * NG + g, :],
                                       turned[:, 0, kind * B + b, :], ALU.mult).then_inc(cos_done, 1)
                pool.wait_ge(roped, NT)
                pool.wait_ge(values_ready, 1)
                with pool.Fori(0, B * NG // 2) as u:
                    for v in range(2):
                        pool.wait_ge(mixed_ready, 2 * u + v + 1)
                        i = u * 2 + v
                        pool.tensor_copy(q_cur[:, v, :], qk[:, 0, i, :]).then_inc(cur_ready, 1)
                        pool.tensor_copy(k_cur[:, v, :], qk[:, 1, i, :]).then_inc(cur_ready, 1)
                        pool.tensor_copy(v_cur[:, v, :, :], values[:, bass.ds(i * ST, ST), :]).then_inc(cur_ready, 1)

            @block.vector
            def _(dve):
                dve.memset(eps[:, :], 1e-6).then_inc(filled, 1)
                dve.memset(values[:, :, :], 1.0).then_inc(filled, 1)
                dve.wait_ge(filled, 2)
                dve.wait_ge(v_ready, 1)
                for b in range(B):
                    for g in range(NG):
                        at = (b * NG + g) * ST
                        of = ps[:, 3, b * 256:(b + 1) * 256].rearrange("p (s g e) -> p s g e", s=ST, g=NG)
                        cp = dve.tensor_copy(values[:, at:at + ST, 0:HD], of[:, :, g, :])
                cp.then_inc(values_ready, 1)
                dve.wait_ge(loaded, 8 * 16)
                for r in range(2 * B):
                    dve.wait_ge(rms_ready, r + 1)
                    dve.reciprocal(rms[:, r, :], rms[:, r, :]).then_inc(rrms_ready, 1)
                    dve.wait_ge(rrms_ready, r + 1)
                    for c in range(2):
                        dve.tensor_tensor(turned[:, c, r, :], rope[:, c, :], rms[:, r, :],
                                          ALU.mult).then_inc(turned_ready, 1)
                for t in range(NT):
                    kind, b, g = tile(t)
                    dve.wait_ge(turned_ready, 2 * (kind * B + b) + 2)
                    dve.wait_ge(swapped, t + 1)
                    dve.tensor_tensor(by_sin[:, t % 2, :], ps[:, t % 3, :],
                                      turned[:, 1, kind * B + b, :], ALU.mult).then_inc(sin_done, 1)
                    dve.wait_ge(sin_done, t + 1)
                    dve.wait_ge(cos_done, t + 1)
                    dve.tensor_tensor(qk[:, kind, b * NG + g, :], by_sin[:, t % 2, :], by_cos[:, t % 2, :],
                                      ALU.add).then_inc(roped, 1)
                with dve.Fori(0, B * NG // 2) as u:
                    for v in range(2):
                        dve.wait_ge(probs_used, u * PER + (v + 1) * (PER // 2) + PROBS)
                        dve.tensor_copy(mixed[:, v, :], ps[:, 4 + v, :]).then_inc(mixed_ready, 1)
                        dve.wait_ge(sums_ready, 2 * u + v + 1)
                        dve.reciprocal(recip[:, v, :], ps[:, 6, :]).then_inc(recip_ready, 1)
                        dve.wait_ge(recip_ready, 2 * u + v + 2)
                        dve.tensor_tensor(heads[:, u * 2 + v, :], mixed[:, v, :], recip[:, v, :],
                                          ALU.mult).then_inc(heads_ready, 1)
                for b in range(B):
                    for m in range(KC):
                        dve.wait_ge(out_ready, b * KC + m + 1)
                        part = x[:, m, b * T:(b + 1) * T]
                        dve.tensor_tensor(part, part, ps[:, b * KC + m, :], ALU.add).then_inc(added, 1)


def alibi_attention(nc, ps, d, x, xn):
    with Stage(nc, "a1") as s:
        wq, wk = s.buf("wq", [P, KC, NG * P]), s.buf("wk", [P, KC, NG * P])
        wv, wo = s.buf("wv", [P, KC, C]), s.buf("wo", [P, NG, C])
        bq, bk, bo = s.buf("bq", [P, NG]), s.buf("bk", [P, NG]), s.buf("bo", [P, KC])
        bq_s = s.buf("bq_s", [P, NG])
        bv = s.buf("bv", [P, C])
        sums_of, ident = s.buf("sums_of", [P, P]), s.buf("ident", [P, P])
        away = s.buf("away", [P, T])
        slopes = s.buf("slopes", [P, NH])
        qk = s.buf("qk", [P, 2, NG * B, T])
        values = s.buf("values", [P, NG * B * (T // P), HG, HP])
        q_cur, k_cur = s.buf("q_cur", [P, 2, T]), s.buf("k_cur", [P, 2, T])
        v_cur = s.buf("v_cur", [P, 2, T // P, HG, HP])
        slope_cur = s.buf("slope_cur", [P, HG])
        score = s.buf("score", [P, 4, T])
        least = s.buf("least", [P, 4, 1])
        probs, probs_t = s.buf("probs", [P, 4, T]), s.buf("probs_t", [P, 4, T])
        mixed = s.buf("mixed", [P, 2, T])
        recip = s.buf("recip", [P, 2, T])
        heads = s.buf("heads", [P, NG * B, T])
        loaded, filled, bias_ready = s.sem("loaded"), s.sem("filled"), s.sem("bias_ready")
        proj_ready, qk_ready, v_ready, values_ready = (
            s.sem("proj_ready"), s.sem("qk_ready"), s.sem("v_ready"), s.sem("values_ready"))
        cur_ready, slope_ready, score_ready, biased, least_ready = (
            s.sem("cur_ready"), s.sem("slope_ready"), s.sem("score_ready"), s.sem("biased"),
            s.sem("least_ready"))
        probs_ready, turned, turned_ready, turned_used = (
            s.sem("probs_ready"), s.sem("turned"), s.sem("turned_ready"), s.sem("turned_used"))
        mixed_ready, sums_ready, recip_ready, heads_ready = (
            s.sem("mixed_ready"), s.sem("sums_ready"), s.sem("recip_ready"), s.sem("heads_ready"))
        out_ready, added = s.sem("out_ready"), s.sem("added")
        NT = 2 * NG * B
        ST = T // P
        HALF = ST * HG
        PER = 2 * HALF
        LOADS = 14

        def tile(t):
            return t // (NG * B), t // B % NG, t % B

        def unit(n):
            return n // HALF, n % HALF // HG, n % HG

        with nc.Block() as block:

            @block.sync
            def _(sp):
                for to, of in ((wq, "a1_wq"), (wk, "a1_wk"), (wv, "a1_wv"), (wo, "a1_wo")):
                    sp.dma_start(to[:, :, :], d[of].rearrange("(k p) n -> p k n", p=P)).then_inc(loaded, 16)
                for to, of in ((bq, "a1_bq"), (bk, "a1_bk"), (bo, "a1_bo")):
                    sp.dma_start(to[:, :], d[of]).then_inc(loaded, 16)
                sp.dma_start(bv[:, :], d["a1_bv"].partition_broadcast(P)).then_inc(loaded, 16)
                for to, of in ((sums_of, "sums_of"), (ident, "ident"), (away, "away"), (slopes, "slopes")):
                    sp.dma_start(to[:, :], d[of]).then_inc(loaded, 16)

            @block.tensor
            def _(pe):
                pe.wait_ge(loaded, 12 * 16)
                for t in range(NT):
                    kind, g, b = tile(t)
                    w = wk if kind else wq
                    if t >= 3:
                        pe.wait_ge(qk_ready, t - 2)
                    for k in range(KC):
                        mm = pe.matmul(ps[:, t % 3, :], w[:, k, g * P:(g + 1) * P],
                                       xn[:, k, b * T:(b + 1) * T], start=k == 0, stop=k == KC - 1)
                    mm.then_inc(proj_ready, 1)
                for tt in range(TT):
                    if tt >= 4:
                        pe.wait_ge(values_ready, tt - 3)
                    for k in range(KC):
                        mm = pe.matmul(ps[:, 3 + tt % 4, 0:C], xn[:, k, tt * P:(tt + 1) * P],
                                       wv[:, k, :], start=k == 0, stop=k == KC - 1)
                    mm.then_inc(v_ready, 1)
                pe.wait_ge(qk_ready, NT)
                pe.wait_ge(values_ready, TT)

                def scores(u, n):
                    v, qt, j = unit(n)
                    rows = slice(j * HP, (j + 1) * HP)
                    pe.wait_ge(biased, u * PER + n + 1)
                    pe.matmul(ps[:, n % 3, 0:(qt + 1) * P], q_cur[rows, v, qt * P:(qt + 1) * P],
                              k_cur[rows, v, 0:(qt + 1) * P], start=True, stop=True).then_inc(score_ready, 1)

                def turn(u, n):
                    v, qt, j = unit(n)
                    pe.wait_ge(probs_ready, u * PER + n + 1 + 4)
                    pe.wait_ge(turned_ready, u * PER + n + 1)
                    for kt in range(qt + 1):
                        mm = pe.transpose(ps[:, 3 + n % 2, kt * P:(kt + 1) * P],
                                          probs[:, n % 4, kt * P:(kt + 1) * P], ident[:, :])
                    mm.then_inc(turned, 1)

                def mix(u, n):
                    v, qt, j = unit(n)
                    pe.wait_ge(turned_ready, u * PER + n + 1 + 2)
                    for kt in range(qt + 1):
                        mm = pe.matmul(ps[j * HP:(j + 1) * HP, 5 + v, qt * P:(qt + 1) * P],
                                       v_cur[:, v, kt, j, :], probs_t[:, n % 4, kt * P:(kt + 1) * P],
                                       start=kt == 0, stop=kt == qt)
                    mm.then_inc(turned_used, 1)

                def sum_weights(u, v):
                    pe.wait_ge(mixed_ready, 2 * u + v + 1 + 2)
                    pe.wait_ge(recip_ready, 2 * u + v + 1)
                    pe.matmul(ps[:, 7, :], sums_of[:, :], mixed[:, v, :],
                              start=True, stop=True).then_inc(sums_ready, 1)

                with pe.Fori(0, NG) as u:
                    for n in range(PER + 4):
                        if n < PER:
                            if n % HALF == 0:
                                pe.wait_ge(cur_ready, 6 * u + 3 * (n // HALF) + 3)
                            scores(u, n)
                        if 2 <= n < PER + 2:
                            turn(u, n - 2)
                        if n >= 4:
                            mix(u, n - 4)
                        if n == HALF + 8:
                            sum_weights(u, 0)
                    sum_weights(u, 1)
                pe.wait_ge(heads_ready, NG * B)
                for b in range(B):
                    for m in range(KC):
                        for g in range(NG):
                            mm = pe.matmul(ps[:, b * KC + m, :], wo[:, g, m * P:(m + 1) * P],
                                           heads[:, g * B + b, :], start=g == 0, stop=g == NG - 1)
                        mm.then_inc(out_ready, 1)

            @block.scalar
            def _(act):
                act.wait_ge(loaded, 12 * 16)
                act.wait_ge(bias_ready, 1)
                for t in range(NT):
                    kind, g, b = tile(t)
                    act.wait_ge(proj_ready, t + 1)
                    if kind:
                        act.activation(qk[:, 1, g * B + b, :], ps[:, t % 3, :], ACT.Identity,
                                       bias=bk[:, g:g + 1]).then_inc(qk_ready, 1)
                    else:
                        act.activation(qk[:, 0, g * B + b, :], ps[:, t % 3, :], ACT.Identity,
                                       bias=bq_s[:, g:g + 1], scale=-HD ** -0.5).then_inc(qk_ready, 1)
                act.sem_inc(probs_ready, 4)
                act.sem_inc(turned_ready, 2)

                def copy_turned(u, n):
                    v, qt, j = unit(n)
                    act.wait_ge(turned, u * PER + n + 1 + 4)
                    act.wait_ge(turned_used, u * PER + n + 1)
                    act.activation(probs_t[:, n % 4, 0:(qt + 1) * P], ps[:, 3 + n % 2, 0:(qt + 1) * P],
                                   ACT.Copy).then_inc(turned_ready, 1)

                with act.Fori(0, NG) as u:
                    for n in range(PER + 2):
                        if n < PER:
                            v, qt, j = unit(n)
                            act.wait_ge(least_ready, u * PER + n + 1)
                            act.wait_ge(turned, u * PER + n + 1)
                            act.activation(probs[:, n % 4, 0:(qt + 1) * P], score[:, n % 4, 0:(qt + 1) * P],
                                           ACT.Exp, bias=least[:, n % 4, :], scale=-1.0).then_inc(probs_ready, 1)
                        if n >= 2:
                            copy_turned(u, n - 2)

            @block.gpsimd
            def _(pool):
                pool.sem_inc(biased, 3)
                pool.sem_inc(turned, 4)
                pool.sem_inc(turned_used, 4)
                pool.sem_inc(recip_ready, 1)
                pool.sem_inc(mixed_ready, 2)
                pool.wait_ge(qk_ready, NT)
                pool.wait_ge(values_ready, TT)
                with pool.Fori(0, NG) as u:
                    for v in range(2):
                        pool.wait_ge(mixed_ready, 2 * u + v + 1)
                        i = u * 2 + v
                        pool.tensor_copy(q_cur[:, v, :], qk[:, 0, i, :]).then_inc(cur_ready, 1)
                        pool.tensor_copy(k_cur[:, v, :], qk[:, 1, i, :]).then_inc(cur_ready, 1)
                        pool.tensor_copy(v_cur[:, v, :, :, :],
                                         values[:, bass.ds(i * ST, ST), :, :]).then_inc(cur_ready, 1)

            @block.vector
            def _(dve):
                dve.memset(values[:, :, :, :], 1.0).then_inc(filled, 1)
                dve.wait_ge(loaded, 12 * 16)
                dve.tensor_scalar(bq_s[:, :], bq[:, :], -HD ** -0.5, None, ALU.mult).then_inc(bias_ready, 1)
                dve.wait_ge(filled, 1)
                for tt in range(TT):
                    b, st = tt // ST, tt % ST
                    dve.wait_ge(v_ready, tt + 1)
                    of = ps[:, 3 + tt % 4, 0:C].rearrange("p (g j e) -> p g j e", g=NG, j=HG)
                    to = values[:, :, :, :].rearrange("p (g b s) j e -> p g b s j e", g=NG, b=B)
                    for g in range(NG):
                        cp = dve.tensor_tensor(to[:, g, b, st, :, 0:HD], of[:, g, :, :],
                                               bv[:, g * 64:(g + 1) * 64].rearrange("p (j e) -> p j e", j=HG),
                                               ALU.add)
                    cp.then_inc(values_ready, 1)

                def norm(u, v):
                    dve.wait_ge(turned_used, u * PER + (v + 1) * HALF + 4)
                    dve.tensor_copy(mixed[:, v, :], ps[:, 5 + v, :]).then_inc(mixed_ready, 1)

                def weigh(u, v):
                    dve.wait_ge(sums_ready, 2 * u + v + 1)
                    dve.reciprocal(recip[:, v, :], ps[:, 7, :]).then_inc(recip_ready, 1)
                    dve.wait_ge(recip_ready, 2 * u + v + 2)
                    dve.tensor_tensor(heads[:, u * 2 + v, :], mixed[:, v, :], recip[:, v, :],
                                      ALU.mult).then_inc(heads_ready, 1)

                with dve.Fori(0, NG) as u:
                    dve.tensor_copy(slope_cur[:, :], slopes[:, bass.ds(u * HG, HG)]).then_inc(slope_ready, 1)
                    dve.wait_ge(slope_ready, u + 1)
                    for n in range(PER):
                        v, qt, j = unit(n)
                        w = (qt + 1) * P
                        dve.wait_ge(score_ready, u * PER + n + 1)
                        dve.wait_ge(probs_ready, u * PER + n + 1)
                        dve.scalar_tensor_tensor(score[:, n % 4, 0:w], away[:, T - w:T], slope_cur[:, j:j + 1],
                                                 ps[:, n % 3, 0:w], ALU.mult, ALU.add).then_inc(biased, 1)
                        dve.wait_ge(biased, u * PER + n + 1 + 3)
                        dve.tensor_reduce(least[:, n % 4, :], score[:, n % 4, 0:w], AX.X,
                                          ALU.min).then_inc(least_ready, 1)
                        if n == HALF + 5:
                            norm(u, 0)
                        if n == HALF + 9:
                            weigh(u, 0)
                    norm(u, 1)
                    weigh(u, 1)
                for b in range(B):
                    for m in range(KC):
                        dve.wait_ge(out_ready, b * KC + m + 1)
                        part = x[:, m, b * T:(b + 1) * T]
                        dve.scalar_tensor_tensor(part, ps[:, b * KC + m, :], bo[:, m:m + 1], part,
                                                 ALU.add, ALU.add).then_inc(added, 1)


def linear_attention(nc, ps, d, x, xn):
    with Stage(nc, "a2") as s:
        w = s.buf("w", [P, 3, KC, C])
        wo, bias, bo = s.buf("wo", [P, KC, C]), s.buf("bias", [P, 3, KC]), s.buf("bo", [P, KC])
        ones = s.buf("ones", [P, T])
        expo, relu = s.buf("expo", [P, 2 * KC * B, T]), s.buf("relu", [P, 2 * KC * B, T])
        val = s.buf("val", [P, KC * B, T])
        total = s.buf("total", [P, KC * B, T])
        loaded, filled, proj_ready, exp_ready, relu_ready = (
            s.sem("loaded"), s.sem("filled"), s.sem("proj_ready"), s.sem("exp_ready"), s.sem("relu_ready"))
        phi_ready, val_ready, kv_ready, total_ready, ctx_ready, out_ready, added = (
            s.sem("phi_ready"), s.sem("val_ready"), s.sem("kv_ready"), s.sem("total_ready"),
            s.sem("ctx_ready"), s.sem("out_ready"), s.sem("added"))
        KINDS = (1, 2, 0)
        NT = 3 * KC * B

        def tile(t):
            return KINDS[t // (KC * B)], t // B % KC, t % B

        with nc.Block() as block:

            @block.sync
            def _(sp):
                sp.dma_start(w[:, :, :, :], d["a2_w"].rearrange("q (k p) n -> p q k n", p=P)).then_inc(loaded, 16)
                sp.dma_start(wo[:, :, :], d["a2_wo"].rearrange("(k p) n -> p k n", p=P)).then_inc(loaded, 16)
                sp.dma_start(bias[:, :, :], d["a2_bias"]).then_inc(loaded, 16)
                sp.dma_start(bo[:, :], d["a2_bo"]).then_inc(loaded, 16)

            @block.tensor
            def _(pe):
                pe.wait_ge(loaded, 4 * 16)
                for t in range(NT):
                    kind, m, b = tile(t)
                    if t >= 8:
                        pe.wait_ge(relu_ready, t - 7)
                    for k in range(KC):
                        mm = pe.matmul(ps[:, t % 8, :], w[:, kind, k, m * P:(m + 1) * P],
                                       xn[:, k, b * T:(b + 1) * T], start=k == 0, stop=k == KC - 1)
                    mm.then_inc(proj_ready, 1)
                for b in range(B):
                    for m in range(KC):
                        pe.wait_ge(val_ready, KC * B)
                        pe.wait_ge(ctx_ready, KC * (b + 1))
                        for k in range(KC):
                            mm = pe.matmul(ps[:, 4 + b * KC + m, :], wo[:, k, m * P:(m + 1) * P],
                                           total[:, k * B + b, :], start=k == 0, stop=k == KC - 1)
                        mm.then_inc(out_ready, 1)

            @block.scalar
            def _(act):
                act.wait_ge(loaded, 4 * 16)
                n = 0
                for t in range(NT):
                    kind, m, b = tile(t)
                    act.wait_ge(proj_ready, t + 1)
                    at = ps[:, t % 8, :]
                    if kind == 2:
                        act.activation(val[:, m * B + b, :], at, ACT.Identity,
                                       bias=bias[:, kind, m:m + 1]).then_inc(val_ready, 1)
                        continue
                    act.activation(expo[:, n, :], at, ACT.Exp, bias=bias[:, kind, m:m + 1]).then_inc(exp_ready, 1)
                    act.activation(relu[:, n, :], at, ACT.Relu, bias=bias[:, kind, m:m + 1]).then_inc(relu_ready, 1)
                    n += 1

            @block.vector
            def _(dve):
                dve.memset(ones[:, :], 1.0).then_inc(filled, 1)

                def phi(n):
                    dve.wait_ge(exp_ready, n + 1)
                    dve.wait_ge(relu_ready, n + 1)
                    dve.scalar_tensor_tensor(expo[:, n, :], expo[:, n, :], 1.0, relu[:, n, :],
                                             ALU.min, ALU.add).then_inc(phi_ready, 1)

                for n in range(KC * B):
                    phi(n)
                dve.wait_ge(filled, 1)
                for n in range(KC * B):
                    dve.wait_ge(phi_ready, n + 1)
                    dve.wait_ge(val_ready, n + 1)
                    dve.tensor_tensor(val[:, n, :], expo[:, n, :], val[:, n, :], ALU.mult).then_inc(kv_ready, 1)
                for n in range(KC * B):
                    dve.wait_ge(kv_ready, n + 1)
                    dve.tensor_tensor_scan(total[:, n, :], ones[:, :], val[:, n, :], 0.0,
                                           ALU.mult, ALU.add).then_inc(total_ready, 1)
                for n in range(KC * B):
                    phi(KC * B + n)
                for b in range(B):
                    for m in range(KC):
                        n = m * B + b
                        dve.wait_ge(phi_ready, KC * B + n + 1)
                        dve.wait_ge(total_ready, n + 1)
                        dve.scalar_tensor_tensor(total[:, n, :], expo[:, KC * B + n, :], HD ** -0.5,
                                                 total[:, n, :], ALU.mult, ALU.mult).then_inc(ctx_ready, 1)
                for b in range(B):
                    for m in range(KC):
                        dve.wait_ge(out_ready, b * KC + m + 1)
                        part = x[:, m, b * T:(b + 1) * T]
                        dve.scalar_tensor_tensor(part, ps[:, 4 + b * KC + m, :], bo[:, m:m + 1], part,
                                                 ALU.add, ALU.add).then_inc(added, 1)


E_ALL = 8
TOP = 2


def expert_layer(nc, name, ps, d, x, xn, width, by_sigmoid, looked_up=None):
    FT = width // P
    with Stage(nc, name) as s:
        wr = s.buf("wr", [P, KC, E_ALL])
        ident, order = s.buf("ident", [P, P]), s.buf("order", [P, TT, E_ALL])
        bias = s.buf("bias", [P, E_ALL])
        choice, prob = s.buf("choice", [P, TT, E_ALL]), s.buf("prob", [P, TT, E_ALL])
        best, where = s.buf("best", [P, TT, 8]), s.buf("where", [P, TT, 8], U32)
        index = s.buf("index", [P, TT, 8])
        taken, also = s.buf("taken", [P, TT, E_ALL]), s.buf("also", [P, TT, E_ALL])
        norm = s.buf("norm", [P, TT])
        share = s.buf("share", [P, E_ALL, N])
        w1, w3 = s.buf("w1", [P, 2, KC, width]), s.buf("w3", [P, 2, KC, width])
        w2 = s.buf("w2", [P, 2, FT, C])
        act_h, gated = s.buf("act_h", [P, 2, T]), s.buf("gated", [P, 4, T])
        part_out = s.buf("part_out", [P, 4, T])
        routed = s.sem("routed")
        if looked_up is not None:
            index_in = s.buf("index_in", [P, LOOKED], I32)
            table, entry = s.buf("table", [P, LUT]), s.buf("entry", [P, LUT])
            term = s.buf("term", [P, 2, LOOKED // 4])
            t_loaded, summed, term_ready = s.sem("t_loaded"), s.sem("summed"), s.sem("term_ready")
        r_loaded, logits_ready, r_step, prob_ready = (
            s.sem("r_loaded"), s.sem("logits_ready"), s.sem("r_step"), s.sem("prob_ready"))
        share_ready, share_copied = s.sem("share_ready"), s.sem("share_copied")
        w_loaded = [s.sem("w_loaded0"), s.sem("w_loaded1")]
        up_ready, silu_ready, gated_ready, down_done = (
            s.sem("up_ready"), s.sem("silu_ready"), s.sem("gated_ready"), s.sem("down_done"))
        part_ready, added = s.sem("part_ready"), s.sem("added")
        TILES = FT * B
        PER = 2 * TILES

        with nc.Block() as block:

            def load(eng, e, v):
                eng.dma_start(w1[:, v, :, :], d[name + "_w1"][e, :, :].rearrange("(k p) n -> p k n", p=P)
                              ).then_inc(w_loaded[v], 16)
                eng.dma_start(w3[:, v, :, :], d[name + "_w3"][e, :, :].rearrange("(k p) n -> p k n", p=P)
                              ).then_inc(w_loaded[v], 16)
                eng.dma_start(w2[:, v, :, :], d[name + "_w2"][e, :, :].rearrange("(f p) n -> p f n", p=P)
                              ).then_inc(w_loaded[v], 16)

            @block.sync
            def _(sp):
                sp.dma_start(wr[:, :, :], d[name + "_wr"].rearrange("(k p) n -> p k n", p=P)).then_inc(r_loaded, 16)
                sp.dma_start(ident[:, :], d["ident"]).then_inc(r_loaded, 16)
                sp.dma_start(order[:, :, :], d["order"]).then_inc(r_loaded, 16)
                if by_sigmoid:
                    sp.dma_start(bias[:, :], d[name + "_bias"].partition_broadcast(P)).then_inc(r_loaded, 16)
                for v in range(2):
                    load(sp, v, v)
                if looked_up is not None:
                    sp.dma_start(index_in[:, :], d["f3_index"]).then_inc(t_loaded, 16)
                    sp.dma_start(table[:, :], d["f3_lut"].partition_broadcast(P)).then_inc(t_loaded, 16)
                    sp.dma_start(entry[:, :], d["entry"]).then_inc(t_loaded, 16)
                with sp.Fori(0, E_ALL // 2 - 1) as u:
                    for v in range(2):
                        sp.wait_ge(down_done, u * PER + (v + 1) * TILES + 4)
                        load(sp, u * 2 + 2 + v, v)

            @block.tensor
            def _(pe):
                pe.wait_ge(r_loaded, (3 + by_sigmoid) * 16)
                for tt in range(TT):
                    for k in range(KC):
                        mm = pe.matmul(ps[:, 0, tt * E_ALL:(tt + 1) * E_ALL], xn[:, k, tt * P:(tt + 1) * P],
                                       wr[:, k, :], start=k == 0, stop=k == KC - 1)
                mm.then_inc(logits_ready, 1)
                pe.wait_ge(routed, 1)
                for e in range(E_ALL):
                    for b in range(B):
                        n = e * B + b
                        if n >= 4:
                            pe.wait_ge(share_copied, n - 3)
                        for q in range(T // P):
                            mm = pe.matmul(ps[:, n % 4, q * P:(q + 1) * P],
                                           taken[:, b * (T // P) + q, e:e + 1].to_broadcast([P, P]),
                                           ident[:, :], start=True, stop=True)
                        mm.then_inc(share_ready, 1)
                pe.wait_ge(share_copied, E_ALL * B)

                def down(u, v, i):
                    f, b = i // B, i % B
                    pe.wait_ge(gated_ready, u * PER + v * TILES + i + 1 + 2)
                    if f == 0:
                        pe.wait_ge(part_ready, 8 * u + 4 * v + 2 * b + 2)
                    for m in range(KC):
                        mm = pe.matmul(ps[:, 4 + b * KC + m, :], w2[:, v, f, m * P:(m + 1) * P],
                                       gated[:, (v * TILES + i) % 4, :], start=f == 0, stop=f == FT - 1)
                    mm.then_inc(down_done, 1)

                with pe.Fori(0, E_ALL // 2) as u:
                    for n in range(PER + 1):
                        v, i = n // TILES, n % TILES
                        f, b = i // B, i % B
                        if n < PER:
                            if i == 0:
                                pe.wait_ge(w_loaded[v], 48 * u + 48)
                            pe.wait_ge(gated_ready, u * PER + n + 1)
                            for w, bank in ((w1, 0), (w3, 2)):
                                for k in range(KC):
                                    mm = pe.matmul(ps[:, bank + n % 2, :], w[:, v, k, f * P:(f + 1) * P],
                                                   xn[:, k, b * T:(b + 1) * T],
                                                   start=k == 0, stop=k == KC - 1)
                            mm.then_inc(up_ready, 1)
                        if n >= 1:
                            down(u, (n - 1) // TILES, (n - 1) % TILES)

            @block.scalar
            def _(act):
                if by_sigmoid:
                    act.wait_ge(logits_ready, 1)
                    act.activation(prob[:, :, :], ps[:, 0, 0:TT * E_ALL].rearrange("p (t e) -> p t e", e=E_ALL),
                                   ACT.Sigmoid).then_inc(prob_ready, 1)
                else:
                    act.wait_ge(r_step, 4)
                    act.activation(prob[:, :, :], also[:, :, :], ACT.Exp).then_inc(prob_ready, 1)
                for n in range(E_ALL * B):
                    act.wait_ge(share_ready, n + 1)
                    act.activation(share[:, n // B, n % B * T:(n % B + 1) * T], ps[:, n % 4, :],
                                   ACT.Copy).then_inc(share_copied, 1)
                with act.Fori(0, E_ALL // 2) as u:
                    for n in range(PER):
                        act.wait_ge(up_ready, u * PER + n + 1)
                        act.activation(act_h[:, n % 2, :], ps[:, n % 2, :], ACT.Silu).then_inc(silu_ready, 1)

            @block.vector
            def _(dve):
                def choose():
                    dve.wait_ge(r_loaded, (3 + by_sigmoid) * 16)
                    dve.wait_ge(logits_ready, 1)
                    logits = ps[:, 0, 0:TT * E_ALL].rearrange("p (t e) -> p t e", e=E_ALL)
                    if by_sigmoid:
                        dve.wait_ge(prob_ready, 1)
                        dve.tensor_tensor(choice[:, :, :], prob[:, :, :],
                                          bias[:, :].unsqueeze(1).broadcast_to([P, TT, E_ALL]),
                                          ALU.add).then_inc(r_step, 1)
                    else:
                        dve.tensor_copy(choice[:, :, :], logits).then_inc(r_step, 1)
                    dve.wait_ge(r_step, 1)
                    for tt in range(TT):
                        last = dve.max(best[:, tt, :], choice[:, tt, :])
                    last.then_inc(r_step, 1)
                    dve.wait_ge(r_step, 2)
                    for tt in range(TT):
                        last = dve.max_index(where[:, tt, :], best[:, tt, :], choice[:, tt, :])
                    last.then_inc(r_step, 1)
                    dve.wait_ge(r_step, 3)
                    dve.tensor_tensor(also[:, :, :], choice[:, :, :],
                                      best[:, :, 0:1].broadcast_to([P, TT, E_ALL]),
                                      ALU.subtract).then_inc(r_step, 1)
                    dve.tensor_copy(index[:, :, :], where[:, :, :]).then_inc(r_step, 1)
                    dve.wait_ge(r_step, 5)
                    dve.tensor_tensor(taken[:, :, :], order[:, :, :],
                                      index[:, :, 0:1].broadcast_to([P, TT, E_ALL]),
                                      ALU.is_equal).then_inc(r_step, 1)
                    dve.wait_ge(prob_ready, 1)
                    dve.tensor_tensor(also[:, :, :], order[:, :, :],
                                      index[:, :, 1:2].broadcast_to([P, TT, E_ALL]),
                                      ALU.is_equal).then_inc(r_step, 1)
                    dve.wait_ge(r_step, 7)
                    dve.tensor_tensor(taken[:, :, :], taken[:, :, :], also[:, :, :], ALU.add).then_inc(r_step, 1)
                    dve.wait_ge(r_step, 8)
                    dve.tensor_tensor(taken[:, :, :], taken[:, :, :], prob[:, :, :], ALU.mult).then_inc(r_step, 1)
                    dve.wait_ge(r_step, 9)
                    dve.tensor_reduce(norm[:, :], taken[:, :, :], AX.X, ALU.add).then_inc(r_step, 1)
                    dve.wait_ge(r_step, 10)
                    dve.reciprocal(norm[:, :], norm[:, :]).then_inc(r_step, 1)
                    dve.wait_ge(r_step, 11)
                    dve.tensor_tensor(taken[:, :, :], taken[:, :, :],
                                      norm[:, :].unsqueeze(2).broadcast_to([P, TT, E_ALL]),
                                      ALU.mult).then_inc(routed, 1)

                choose()
                dve.sem_inc(gated_ready, 2)
                dve.sem_inc(part_ready, 4)
                dve.wait_ge(share_copied, E_ALL * B)
                if looked_up is not None:
                    dve.memset(looked_up[:, :], 0.0).then_inc(summed, 1)
                    dve.wait_ge(t_loaded, 3 * 16)

                def look_up(u, n):
                    e, q = u * (LUT * 2 // E_ALL) + n // 4, n % 4
                    part = slice(q * LOOKED // 4, (q + 1) * LOOKED // 4)
                    dve.tensor_scalar(term[:, n % 2, :], index_in[:, part], entry[:, bass.ds(e, 1)],
                                      table[:, bass.ds(e, 1)], ALU.is_equal, ALU.mult).then_inc(term_ready, 1)
                    dve.wait_ge(term_ready, u * PER + n + 1)
                    dve.wait_ge(summed, u * PER + n + 1)
                    dve.tensor_tensor(looked_up[:, part], looked_up[:, part], term[:, n % 2, :],
                                      ALU.add).then_inc(summed, 1)

                def weigh(u, v):
                    for b in range(B):
                        dve.wait_ge(down_done, u * PER + (v + 1) * TILES - B + b + 1 + 4)
                        for m in range(KC):
                            n = b * KC + m
                            dve.wait_ge(added, 8 * u + 4 * v + n + 1)
                            dve.tensor_tensor(part_out[:, n, :], ps[:, 4 + n, :],
                                              share[:, u * 2 + v, b * T:(b + 1) * T],
                                              ALU.mult).then_inc(part_ready, 1)

                with dve.Fori(0, E_ALL // 2) as u:
                    for n in range(PER):
                        dve.wait_ge(silu_ready, u * PER + n + 1)
                        dve.wait_ge(down_done, u * PER + n + 1)
                        dve.tensor_tensor(gated[:, n % 4, :], act_h[:, n % 2, :], ps[:, 2 + n % 2, :],
                                          ALU.mult).then_inc(gated_ready, 1)
                        if n == TILES + 1:
                            weigh(u, 0)
                        if looked_up is not None:
                            look_up(u, n)
                    weigh(u, 1)

            @block.gpsimd
            def _(pool):
                pool.sem_inc(down_done, 4)
                pool.sem_inc(added, 4)
                with pool.Fori(0, E_ALL // 2) as u:
                    for v in range(2):
                        for b in range(B):
                            for m in range(KC):
                                n = b * KC + m
                                part = x[:, m, b * T:(b + 1) * T]
                                pool.wait_ge(part_ready, 8 * u + 4 * v + n + 1 + 4)
                                pool.wait_ge(added, 8 * u + 4 * v + n + 1)
                                pool.tensor_tensor(part, part, part_out[:, n, :], ALU.add).then_inc(added, 1)


LUT = 16
WIDE = 688
WF = -(-WIDE // P)
LOOKED = 2 * KC * WIDE + WF * C


def looked_up_layer(nc, ps, weights, x, xn):
    with Stage(nc, "f3") as s:
        act_h, gated = s.buf("act_h", [P, 2, T]), s.buf("gated", [P, 4, T])
        up_ready, silu_ready, gated_ready, down_done, added = (
            s.sem("up_ready"), s.sem("silu_ready"), s.sem("gated_ready"), s.sem("down_done"), s.sem("added"))
        w_gate = weights[:, 0:KC * WIDE].rearrange("p (k n) -> p k n", k=KC)
        w_up = weights[:, KC * WIDE:2 * KC * WIDE].rearrange("p (k n) -> p k n", k=KC)
        w_down = weights[:, 2 * KC * WIDE:].rearrange("p (f n) -> p f n", f=WF)
        TILES = WF * B

        def tile(t):
            return t // B, t % B, min(P, WIDE - t // B * P)

        with nc.Block() as block:

            @block.tensor
            def _(pe):
                def down(t):
                    f, b, rows = tile(t)
                    pe.wait_ge(gated_ready, t + 1)
                    for m in range(KC):
                        mm = pe.matmul(ps[:, 4 + b * KC + m, :], w_down[0:rows, f, m * P:(m + 1) * P],
                                       gated[0:rows, t % 4, :], start=f == 0, stop=f == WF - 1)
                    mm.then_inc(down_done, 1)

                for t in range(TILES):
                    f, b, rows = tile(t)
                    if t >= 2:
                        pe.wait_ge(gated_ready, t - 1)
                    for w, bank in ((w_gate, 0), (w_up, 2)):
                        for k in range(KC):
                            mm = pe.matmul(ps[0:rows, bank + t % 2, :], w[:, k, f * P:f * P + rows],
                                           xn[:, k, b * T:(b + 1) * T], start=k == 0, stop=k == KC - 1)
                    mm.then_inc(up_ready, 1)
                    if t >= 1:
                        down(t - 1)
                down(TILES - 1)

            @block.scalar
            def _(act):
                for t in range(TILES):
                    f, b, rows = tile(t)
                    act.wait_ge(up_ready, t + 1)
                    act.activation(act_h[0:rows, t % 2, :], ps[0:rows, t % 2, :], ACT.Silu).then_inc(silu_ready, 1)

            @block.vector
            def _(dve):
                for t in range(TILES):
                    f, b, rows = tile(t)
                    dve.wait_ge(silu_ready, t + 1)
                    if t >= 4:
                        dve.wait_ge(down_done, t - 3)
                    dve.tensor_tensor(gated[0:rows, t % 4, :], act_h[0:rows, t % 2, :],
                                      ps[0:rows, 2 + t % 2, :], ALU.mult).then_inc(gated_ready, 1)
                for b in range(B):
                    dve.wait_ge(down_done, TILES - B + b + 1)
                    for m in range(KC):
                        part = x[:, m, b * T:(b + 1) * T]
                        dve.tensor_tensor(part, part, ps[:, 4 + b * KC + m, :], ALU.add).then_inc(added, 1)


def hadamard_layer(nc, ps, d, x, xn):
    INTER = 1024
    FT = INTER // P
    with Stage(nc, "f1") as s:
        w_gate, w_up = s.buf("w_gate", [P, KC, INTER]), s.buf("w_up", [P, KC, INTER])
        w_raw, w_mid = s.buf("w_raw", [P, FT, C]), s.buf("w_mid", [P, FT, C])
        w_down = s.buf("w_down", [P, FT, C])
        had = s.buf("had", [P, P])
        su_ug, su_dp = s.buf("su_ug", [P, KC]), s.buf("su_dp", [P, FT])
        sc_up, sc_gate, sc_dp = s.buf("sc_up", [P, FT]), s.buf("sc_gate", [P, FT]), s.buf("sc_dp", [P, KC])
        sc_both = s.buf("sc_both", [P, FT])
        signed, mixed = s.buf("signed", [P, KC, N]), s.buf("mixed", [P, KC, N])
        xh = s.buf("xh", [P, KC, N])
        act_h, gated = s.buf("act_h", [P, 2, T]), s.buf("gated", [P, 4, T])
        small, w_loaded, down_loaded = s.sem("small"), s.sem("w_loaded"), s.sem("down_loaded")
        signed_ready, mixed_ready, xh_psum, xh_ready = (
            s.sem("signed_ready"), s.sem("mixed_ready"), s.sem("xh_psum"), s.sem("xh_ready"))
        w_step, w_psum, w_ready, both_ready = (
            s.sem("w_step"), s.sem("w_psum"), s.sem("w_ready"), s.sem("both_ready"))
        up_ready, silu_ready, gated_ready, down_done, added = (
            s.sem("up_ready"), s.sem("silu_ready"), s.sem("gated_ready"), s.sem("down_done"), s.sem("added"))
        TILES = FT * B

        with nc.Block() as block:

            @block.sync
            def _(sp):
                for to, of in ((su_ug, "f1_su_ug"), (had, "hadamard"), (su_dp, "f1_su_dp"), (sc_up, "f1_sc_up"),
                               (sc_gate, "f1_sc_gate"), (sc_dp, "f1_sc_dp")):
                    sp.dma_start(to[:, :], d[of]).then_inc(small, 16)
                sp.dma_start(w_raw[:, :, :], d["f1_w_down"].rearrange("(f p) n -> p f n", p=P)
                             ).then_inc(down_loaded, 16)
                for to, of in ((w_gate, "f1_w_gate"), (w_up, "f1_w_up")):
                    sp.dma_start(to[:, :, :], d[of].rearrange("(k p) n -> p k n", p=P)).then_inc(w_loaded, 16)

            @block.tensor
            def _(pe):
                pe.wait_ge(small, 6 * 16)
                for k in range(KC):
                    pe.wait_ge(mixed_ready, k + 1)
                    for b in range(B):
                        pe.matmul(ps[:, k * B + b, :], had[:, :], mixed[:, k, b * T:(b + 1) * T],
                                  start=True, stop=True).then_inc(xh_psum, 1)
                pe.wait_ge(w_step, 3)
                for q in range(4):
                    pe.matmul(ps[:, 4 + q, :], had[:, :],
                              w_mid[:, 2 * q:2 * q + 2, :].rearrange("p f n -> p (f n)"),
                              start=True, stop=True).then_inc(w_psum, 1)
                pe.wait_ge(w_loaded, 2 * 16)
                pe.wait_ge(xh_ready, KC * B)

                def down(t):
                    f, b = t // B, t % B
                    pe.wait_ge(gated_ready, t + 1)
                    if t < B:
                        pe.wait_ge(w_ready, 4)
                    for m in range(KC):
                        mm = pe.matmul(ps[:, 4 + b * KC + m, :], w_down[:, f, m * P:(m + 1) * P],
                                       gated[:, t % 4, :], start=f == 0, stop=f == FT - 1)
                    mm.then_inc(down_done, 1)

                for t in range(TILES):
                    f, b = t // B, t % B
                    if t >= 2:
                        pe.wait_ge(gated_ready, t - 1)
                    for w, bank in ((w_gate, 0), (w_up, 2)):
                        for k in range(KC):
                            mm = pe.matmul(ps[:, bank + t % 2, :], w[:, k, f * P:(f + 1) * P],
                                           xh[:, k, b * T:(b + 1) * T], start=k == 0, stop=k == KC - 1)
                    mm.then_inc(up_ready, 1)
                    if t >= 1:
                        down(t - 1)
                down(TILES - 1)

            @block.scalar
            def _(act):
                for n in range(KC * B):
                    act.wait_ge(xh_psum, n + 1)
                    act.activation(xh[:, n // B, n % B * T:(n % B + 1) * T], ps[:, n, :], ACT.Copy,
                                   scale=1.0 / 16).then_inc(xh_ready, 1)
                for q in range(4):
                    act.wait_ge(w_psum, q + 1)
                    act.activation(w_down[:, 2 * q:2 * q + 2, :].rearrange("p f n -> p (f n)"), ps[:, 4 + q, :],
                                   ACT.Copy, scale=1.0 / 32).then_inc(w_ready, 1)
                act.wait_ge(small, 6 * 16)
                for t in range(TILES):
                    act.wait_ge(up_ready, t + 1)
                    act.activation(act_h[:, t % 2, :], ps[:, t % 2, :], ACT.Silu,
                                   scale=sc_gate[:, t // B:t // B + 1]).then_inc(silu_ready, 1)

            @block.gpsimd
            def _(pool):
                pool.wait_ge(down_loaded, 16)
                for n, (of, to) in enumerate(((w_raw, w_mid), (w_mid, w_raw), (w_raw, w_mid))):
                    if n:
                        pool.wait_ge(w_step, n)
                    r = 1 << n
                    a = of[:, :, :].rearrange("p (q two r) n -> p q two (r n)", two=2, r=r)
                    o = to[:, :, :].rearrange("p (q two r) n -> p q two (r n)", two=2, r=r)
                    pool.tensor_tensor(o[:, :, 0, :], a[:, :, 0, :], a[:, :, 1, :], ALU.add)
                    pool.tensor_tensor(o[:, :, 1, :], a[:, :, 0, :], a[:, :, 1, :],
                                       ALU.subtract).then_inc(w_step, 1)

            @block.vector
            def _(dve):
                dve.wait_ge(small, 6 * 16)
                dve.tensor_tensor(sc_both[:, :], sc_up[:, :], su_dp[:, :], ALU.mult).then_inc(both_ready, 1)
                for k in range(KC):
                    dve.tensor_scalar(signed[:, k, :], xn[:, k, :], su_ug[:, k:k + 1], None,
                                      ALU.mult).then_inc(signed_ready, 1)
                dve.wait_ge(signed_ready, KC)
                for k, op in enumerate((ALU.add, ALU.subtract)):
                    dve.tensor_tensor(mixed[:, k, :], signed[:, 0, :], signed[:, 1, :], op).then_inc(mixed_ready, 1)
                dve.wait_ge(both_ready, 1)
                for t in range(TILES):
                    f = t // B
                    dve.wait_ge(silu_ready, t + 1)
                    if t >= 4:
                        dve.wait_ge(down_done, t - 3)
                    dve.scalar_tensor_tensor(gated[:, t % 4, :], ps[:, 2 + t % 2, :], sc_both[:, f:f + 1],
                                             act_h[:, t % 2, :], ALU.mult, ALU.mult).then_inc(gated_ready, 1)
                for b in range(B):
                    dve.wait_ge(down_done, TILES - B + b + 1)
                    for m in range(KC):
                        part = x[:, m, b * T:(b + 1) * T]
                        dve.scalar_tensor_tensor(part, ps[:, 4 + b * KC + m, :], sc_dp[:, m:m + 1], part,
                                                 ALU.mult, ALU.add).then_inc(added, 1)


KH, VPK = 16, 2
VH = KH * VPK
TAPS = 4
CH = T // P
PR = B * VPK


def delta_attention(nc, ps, d, x, xn):
    K_G, K_NBETA, K_BETA, K_NEG, K_LEFT, K_END, K_GC = range(7)
    KINDS = 7
    LEVELS = 6
    with Stage(nc, "a3") as s:
        w_ba, dt_bias, a_log = s.buf("w_ba", [P, KC, 2 * VH]), s.buf("dt_bias", [P, VH]), s.buf("a_log", [P, VH])
        taps = s.buf("taps", [P, KH, 4 * TAPS])
        nw = s.buf("nw", [P, 1])
        ident, upto, strict, floor = (s.buf(n, [P, P]) for n in ("ident", "upto", "strict", "floor"))
        ones = s.buf("ones", [P, P])
        half = s.buf("half", [P, PR])
        gates = s.buf("gates", [P, KINDS * TT, VH])
        z_a, z_b = s.buf("z_a", [P, TT, VH]), s.buf("z_b", [P, TT, VH])
        w_qkv, w_z = s.buf("w_qkv", [P, KC, 4 * P]), s.buf("w_z", [P, KC, VPK * P])
        w_out = s.buf("w_out", [P, VPK, C])
        raw = s.buf("raw", [P, 4, B, TAPS - 1 + T])
        conv = s.buf("conv", [P, 4, B, T])
        qkv = s.buf("qkv", [P, 4, B, T])
        zs = s.buf("zs", [P, TT, VPK * P])
        cur = s.buf("cur", [P, KINDS * TT, VPK])
        cur_taps = s.buf("cur_taps", [P, 4 * TAPS])
        low, decay, grown, rough = (s.buf(n, [P, PR, P]) for n in ("low", "decay", "grown", "rough"))
        v0, vt0 = s.buf("v0", [P, PR, P]), s.buf("vt0", [P, PR, P])
        vp, vtp = s.buf("vp", [P, 2, PR, P]), s.buf("vtp", [P, 2, PR, P])
        inv, at, qg = (s.buf(n, [P, 2, PR, P]) for n in ("inv", "at", "qg"))
        v_row, k_row = s.buf("v_row", [P, 2, PR, P]), s.buf("k_row", [P, 2, PR, P])
        state, rest, v_new = (s.buf(n, [P, PR, P]) for n in ("state", "rest", "v_new"))
        xf, sq, xnorm, out_t = (s.buf(n, [P, PR, P]) for n in ("xf", "sq", "xnorm", "out_t"))
        var, rstd = s.buf("var", [P, PR]), s.buf("rstd", [P, PR])

        def sems(*names):
            return [s.sem(n) for n in names]

        (small, filled, w1_loaded, wz_loaded, wo_loaded) = sems(
            "small", "filled", "w1_loaded", "wz_loaded", "wo_loaded")
        (filled_raw,) = sems("filled_raw")
        (ba_ready, g_act, g_step, sums_ready, gates_ready) = sems(
            "ba_ready", "g_act", "g_step", "sums_ready", "gates_ready")
        (proj_ready, raw_ready, conv_step, conv_ready, taps_ready, q_ready, qkv_ready, z_ready, zs_ready) = sems(
            "proj_ready", "raw_ready", "conv_step", "conv_ready", "taps_ready", "q_ready", "qkv_ready",
            "z_ready", "zs_ready")
        (cur_ready, gc_ready, kq_ready, vrow_psum, krow_psum, low_ready, decay_ready, grown_ready) = sems(
            "cur_ready", "gc_ready", "kq_ready", "vrow_psum", "krow_psum", "low_ready", "decay_ready",
            "grown_ready")
        (at_ready, rough_ready, v0_ready, inv_ready, qg_ready, vrow_ready, krow_ready, vt0_psum, vt0_ready) = sems(
            "at_ready", "rough_ready", "v0_ready", "inv_ready", "qg_ready", "vrow_ready", "krow_ready",
            "vt0_psum", "vt0_ready")
        (sq_psum, sqt_psum, v_ready, vt_ready, upd_psum) = sems(
            "sq_psum", "sqt_psum", "v_ready", "vt_ready", "upd_psum")
        (zeroed, ks_psum, rest_ready, x_psum, vnew_ready, o_psum, ds_psum, state_ready) = sems(
            "zeroed", "ks_psum", "rest_ready", "x_psum", "vnew_ready", "o_psum", "ds_psum", "state_ready")
        (xf_ready, sq_ready, var_ready, var_step, rstd_ready, xnorm_ready, ot_psum, ot_ready, y_psum, added) = sems(
            "xf_ready", "sq_ready", "var_ready", "var_step", "rstd_ready", "xnorm_ready", "ot_psum",
            "ot_ready", "y_psum", "added")
        SMALL = 10
        BG, BK, BT, BO, BSQ, BSQT, BUP, BR = range(8)
        PROJ = (BSQ, BSQT, BUP)

        def bank(n):
            return ps[:, n, :].rearrange("p (r t) -> p r t", r=PR)

        def gate(kind, c, r):
            tt = r // VPK * CH + c
            return cur[:, kind * TT + tt, r % VPK:r % VPK + 1]

        def chunk(mt, b, c):
            return qkv[:, mt, b, c * P:(c + 1) * P]

        with nc.Block() as block:

            def load_qkv(eng, h):
                eng.dma_start(w_qkv[:, :, :], d["a3_w"][h, :, 0:4 * P].rearrange("(k p) n -> p k n", p=P)
                              ).then_inc(w1_loaded, 16)

            def load_z(eng, h):
                eng.dma_start(w_z[:, :, :], d["a3_w"][h, :, 4 * P:].rearrange("(k p) n -> p k n", p=P)
                              ).then_inc(wz_loaded, 16)

            def load_out(eng, h):
                eng.dma_start(w_out[:, :, :], d["a3_wo"][h, :, :].rearrange("(v p) n -> p v n", p=P)
                              ).then_inc(wo_loaded, 16)

            @block.sync
            def _(sp):
                sp.dma_start(w_ba[:, :, :], d["a3_w_ba"].rearrange("(k p) n -> p k n", p=P)).then_inc(small, 16)
                sp.dma_start(dt_bias[:, :], d["a3_dt"].partition_broadcast(P)).then_inc(small, 16)
                sp.dma_start(a_log[:, :], d["a3_a_log"].partition_broadcast(P)).then_inc(small, 16)
                sp.dma_start(taps[:, :, :], d["a3_taps"]).then_inc(small, 16)
                sp.dma_start(nw[:, :], d["a3_nw"]).then_inc(small, 16)
                for to, of in ((ident, "ident"), (upto, "upto"), (strict, "strict"), (floor, "floor"),
                               (ones, "ones")):
                    sp.dma_start(to[:, :], d[of]).then_inc(small, 16)
                load_qkv(sp, 0)
                load_z(sp, 0)
                load_out(sp, 0)
                with sp.Fori(0, KH - 1) as h:
                    sp.wait_ge(proj_ready, 8 * h + 8)
                    load_qkv(sp, h + 1)
                    sp.wait_ge(z_ready, 4 * h + 4)
                    load_z(sp, h + 1)
                    sp.wait_ge(y_psum, CH * h + CH)
                    load_out(sp, h + 1)

            @block.tensor
            def _(pe):
                def project(h, t):
                    mt, b = t // B, t % B
                    pe.wait_ge(raw_ready, 8 * h + t + 1)
                    for k in range(KC):
                        mm = pe.matmul(ps[:, PROJ[t % 3], :], w_qkv[:, k, mt * P:(mt + 1) * P],
                                       xn[:, k, b * T:(b + 1) * T], start=k == 0, stop=k == KC - 1)
                    mm.then_inc(proj_ready, 1)

                def project_z(h, n):
                    if n < 3:
                        pe.wait_ge(raw_ready, 8 * h + 8 + 3)
                    else:
                        pe.wait_ge(zs_ready, 4 * h + n - 2)
                    for i in range(2):
                        tt = 2 * n + i
                        for k in range(KC):
                            mm = pe.matmul(ps[:, PROJ[n % 3], i * 256:(i + 1) * 256],
                                           xn[:, k, tt * P:(tt + 1) * P], w_z[:, k, :],
                                           start=k == 0, stop=k == KC - 1)
                    mm.then_inc(z_ready, 1)

                def make(h, c):
                    w = CH * h + c
                    pe.wait_ge(low_ready, PR * w + PR)
                    pe.wait_ge(grown_ready, w + 1)
                    for r in range(PR):
                        mm = pe.matmul(bank(BG)[:, r, :], gate(K_G, c, r).to_broadcast([P, P]), upto[:, :],
                                       start=True, stop=True)
                    mm.then_inc(gc_ready, 1)
                    pe.wait_ge(rough_ready, w + 1)
                    if c == 0:
                        pe.wait_ge(qkv_ready, 4 * h + 4 + 4)
                    for b in range(B):
                        pe.matmul(bank(BK)[:, b, :], chunk(1, b, c), chunk(1, b, c), start=True, stop=True)
                    for b in range(B):
                        mm = pe.matmul(bank(BK)[:, B + b, :], chunk(1, b, c), chunk(0, b, c),
                                       start=True, stop=True)
                    mm.then_inc(kq_ready, 1)
                    pe.wait_ge(vt0_ready, w + 1)
                    for r in range(PR):
                        mm = pe.transpose(bank(BT)[:, r, :], chunk(2 + r % VPK, r // VPK, c), ident[:, :])
                    mm.then_inc(vrow_psum, 1)
                    pe.wait_ge(vrow_ready, w + 1)
                    for b in range(B):
                        mm = pe.transpose(bank(BT)[:, b, :], chunk(1, b, c), ident[:, :])
                    mm.then_inc(krow_psum, 1)

                def turn(w):
                    pe.wait_ge(krow_ready, PR * w + PR)
                    pe.wait_ge(v0_ready, PR * w + PR)
                    for r in range(PR):
                        mm = pe.transpose(bank(BT)[:, r, :], v0[:, r, :], ident[:, :])
                    mm.then_inc(vt0_psum, 1)

                def level(w, n):
                    if n == 1:
                        pe.wait_ge(vt0_ready, w + 1 + 1)
                        a, a_t = v0[:, :, :], vt0[:, :, :]
                        pe.wait_ge(inv_ready, 7 * w + 1)
                    else:
                        pe.wait_ge(v_ready, (LEVELS - 1) * w + n - 1)
                        pe.wait_ge(vt_ready, LEVELS * w + n - 1)
                        a, a_t = vp[:, (n - 1) % 2, :, :], vtp[:, (n - 1) % 2, :, :]
                    if n < LEVELS:
                        for r in range(PR):
                            mm = pe.matmul(bank(BSQ)[:, r, :], a_t[:, r, :], a[:, r, :], start=True, stop=True)
                        mm.then_inc(sq_psum, 1)
                    for r in range(PR):
                        mm = pe.matmul(bank(BSQT)[:, r, :], a[:, r, :], a_t[:, r, :], start=True, stop=True)
                    mm.then_inc(sqt_psum, 1)

                def update(w, c, n):
                    pe.wait_ge(vt_ready, LEVELS * w + n)
                    pe.wait_ge(inv_ready, (LEVELS + 1) * w + n)
                    for r in range(PR):
                        mm = pe.matmul(bank(BUP)[:, r, :], vtp[:, n % 2, r, :], inv[:, c % 2, r, :],
                                       start=True, stop=True)
                    mm.then_inc(upd_psum, 1)

                def recall(h, w, c):
                    pe.wait_ge(ot_ready, w + 1)
                    if c == 0:
                        pe.wait_ge(zeroed, h + 1)
                    else:
                        pe.wait_ge(state_ready, PR * w)
                    for b in range(B):
                        mm = pe.matmul(bank(BR)[:, VPK * b:VPK * (b + 1), :], chunk(1, b, c),
                                       state[:, VPK * b:VPK * (b + 1), :], start=True, stop=True)
                    mm.then_inc(ks_psum, 1)

                def solve(w, c):
                    pe.wait_ge(rest_ready, PR * w + PR)
                    pe.wait_ge(inv_ready, (LEVELS + 1) * (w + 1))
                    for r in range(PR):
                        mm = pe.matmul(bank(BR)[:, r, :], inv[:, c % 2, r, :], rest[:, r, :],
                                       start=True, stop=True)
                    mm.then_inc(x_psum, 1)

                def answer(w, c):
                    pe.wait_ge(vnew_ready, PR * w + PR)
                    pe.wait_ge(at_ready, w + 1)
                    pe.wait_ge(qg_ready, w + 1)
                    pe.wait_ge(added, w + 1)
                    for r in range(PR):
                        pe.matmul(bank(BO)[:, r, :], qg[:, c % 2, r, :], state[:, r, :], start=True, stop=False)
                        mm = pe.matmul(bank(BO)[:, r, :], at[:, c % 2, r, :], v_new[:, r, :],
                                       start=False, stop=True)
                    mm.then_inc(o_psum, 1)
                    for r in range(PR):
                        mm = pe.matmul(bank(BR)[:, r, :], k_row[:, c % 2, r, :], v_new[:, r, :],
                                       start=True, stop=True)
                    mm.then_inc(ds_psum, 1)

                def turn_out(w):
                    pe.wait_ge(state_ready, PR * w + PR)
                    pe.wait_ge(xnorm_ready, w + 1)
                    for r in range(PR):
                        mm = pe.transpose(bank(BR)[:, r, :], xnorm[:, r, :], ident[:, :])
                    mm.then_inc(ot_psum, 1)

                def project_out(h, w, c):
                    if c == 0:
                        pe.wait_ge(wo_loaded, 16 * h + 16)
                    pe.wait_ge(ot_ready, w + 1 + 1)
                    for m in range(KC):
                        for v in range(VPK):
                            mm = pe.matmul(bank(BO)[:, B * m:B * (m + 1), :], w_out[:, v, m * P:(m + 1) * P],
                                           out_t[:, v::VPK, :], start=v == 0, stop=v == VPK - 1)
                    mm.then_inc(y_psum, 1)

                def head(h, last=False):
                    pe.wait_ge(cur_ready, h + 1)
                    pe.wait_ge(wz_loaded, 16 * h + 16)
                    for n in range(4):
                        project_z(h, n)
                    make(h, 0)
                    turn(CH * h)
                    pe.wait_ge(zs_ready, 4 * h + 4)
                    for c in range(CH):
                        w = CH * h + c
                        level(w, 1)
                        if c:
                            recall(h, w - 1, c - 1)
                        level(w, 2)
                        update(w, c, 1)
                        if c:
                            solve(w - 1, c - 1)
                        level(w, 3)
                        update(w, c, 2)
                        if c:
                            answer(w - 1, c - 1)
                        level(w, 4)
                        update(w, c, 3)
                        if c + 1 < CH:
                            make(h, c + 1)
                        level(w, 5)
                        update(w, c, 4)
                        if c:
                            turn_out(w - 1)
                        level(w, 6)
                        update(w, c, 5)
                        if c + 1 < CH:
                            turn(w + 1)
                        if c:
                            project_out(h, w - 1, c - 1)
                        update(w, c, 6)
                    w = CH * h + CH - 1
                    pe.wait_ge(inv_ready, (LEVELS + 1) * (w + 1))
                    if not last:
                        pe.wait_ge(w1_loaded, 16 * h + 32)
                    pieces = [lambda: recall(h, w, CH - 1), lambda: solve(w, CH - 1), lambda: answer(w, CH - 1),
                              lambda: turn_out(w), lambda: project_out(h, w, CH - 1)]
                    for n, piece in enumerate(pieces):
                        piece()
                        if not last:
                            for t in ((0, 1), (2, 3), (4, 5), (6, 7), ())[n]:
                                project(h + 1, t)

                pe.wait_ge(small, SMALL * 16)
                for tt in range(TT):
                    for k in range(KC):
                        mm = pe.matmul(ps[:, 0, tt * 2 * VH:(tt + 1) * 2 * VH], xn[:, k, tt * P:(tt + 1) * P],
                                       w_ba[:, k, :], start=k == 0, stop=k == KC - 1)
                mm.then_inc(ba_ready, 1)
                pe.wait_ge(w1_loaded, 16)
                for t in range(8):
                    project(0, t)
                pe.wait_ge(g_step, 4)
                g_all = gates[:, K_G * TT:(K_G + 1) * TT, :].rearrange("p t v -> p (t v)")
                pe.matmul(ps[:, 1, 0:TT * VH], upto[:, :], g_all, start=True, stop=True)
                pe.matmul(ps[:, 2, 0:TT * VH], ones[:, :], g_all, start=True, stop=True).then_inc(sums_ready, 1)
                with pe.Fori(0, KH - 1) as h:
                    head(h)
                head(KH - 1, last=True)

            @block.scalar
            def _(act):
                def copy_raw(h, t):
                    mt, b = t // B, t % B
                    act.wait_ge(proj_ready, 8 * h + t + 1)
                    act.wait_ge(conv_ready, 4 * h + mt + 1)
                    act.activation(raw[:, mt, b, TAPS - 1:], ps[:, PROJ[t % 3], :], ACT.Copy).then_inc(raw_ready, 1)

                def gates_z(h):
                    for n in range(4):
                        act.wait_ge(z_ready, 4 * h + n + 1)
                        if n == 0:
                            act.wait_ge(xf_ready, CH * h + 1)
                        act.activation(zs[:, 2 * n:2 * n + 2, :].rearrange("p t n -> p (t n)"),
                                       ps[:, PROJ[n % 3], :], ACT.Silu).then_inc(zs_ready, 1)

                def silus(h):
                    for mt in range(4):
                        act.wait_ge(conv_ready, 4 * h + mt + 1 + 4)
                        if mt == 0:
                            act.wait_ge(ks_psum, CH * h + 1)
                            act.activation(qkv[:, 0, :, :], conv[:, 0, :, :], ACT.Silu).then_inc(q_ready, 1)
                            act.wait_ge(q_ready, h + 1)
                            act.activation(qkv[:, 0, :, :], qkv[:, 0, :, :], ACT.Copy,
                                           scale=float(P) ** -0.5).then_inc(qkv_ready, 1)
                        else:
                            act.activation(qkv[:, mt, :, :], conv[:, mt, :, :], ACT.Silu).then_inc(qkv_ready, 1)

                def make_rows(w, c):
                    act.wait_ge(vrow_psum, w + 1)
                    act.activation(v_row[:, c % 2, :, :], bank(BT), ACT.Copy).then_inc(vrow_ready, 1)

                def make(w, c):
                    act.wait_ge(low_ready, PR * w + PR + PR)
                    act.activation(decay[:, :, :], low[:, :, :], ACT.Exp).then_inc(decay_ready, 1)
                    act.wait_ge(gc_ready, w + 1)
                    act.activation(grown[:, :, :], bank(BG), ACT.Exp).then_inc(grown_ready, 1)
                    act.wait_ge(krow_psum, w + 1)
                    for r in range(PR):
                        act.activation(k_row[:, c % 2, r, :], bank(BT)[:, r // VPK, :], ACT.Copy,
                                       scale=gate(K_LEFT, c, r)).then_inc(krow_ready, 1)

                def turn(w):
                    act.wait_ge(vt0_psum, w + 1)
                    act.activation(vt0[:, :, :], bank(BT), ACT.Copy).then_inc(vt0_ready, 1)

                def level(w, n):
                    if n < LEVELS:
                        act.wait_ge(sq_psum, (LEVELS - 1) * w + n)
                        act.activation(vp[:, n % 2, :, :], bank(BSQ), ACT.Copy).then_inc(v_ready, 1)
                    act.wait_ge(sqt_psum, LEVELS * w + n)
                    act.activation(vtp[:, n % 2, :, :], bank(BSQT), ACT.Copy).then_inc(vt_ready, 1)

                def new_values(w, c):
                    act.wait_ge(x_psum, w + 1)
                    for r in range(PR):
                        act.activation(v_new[:, r, :], bank(BR)[:, r, :], ACT.Copy,
                                       scale=gate(K_BETA, c, r)).then_inc(vnew_ready, 1)

                def square(w):
                    act.wait_ge(xf_ready, w + 1 + 1)
                    act.activation(sq[:, :, :], xf[:, :, :], ACT.Square).then_inc(sq_ready, 1)

                def copy_out(w):
                    act.wait_ge(ot_psum, w + 1)
                    act.activation(out_t[:, :, :], bank(BR), ACT.Copy, scale=nw[:, 0:1]).then_inc(ot_ready, 1)

                def head(h, last=False):
                    act.wait_ge(cur_ready, h + 1)
                    gates_z(h)
                    silus(h)
                    make_rows(CH * h, 0)
                    make(CH * h, 0)
                    turn(CH * h)
                    for c in range(CH):
                        w = CH * h + c
                        level(w, 1)
                        level(w, 2)
                        if c:
                            new_values(w - 1, c - 1)
                        level(w, 3)
                        level(w, 4)
                        if c:
                            square(w - 1)
                        if c + 1 < CH:
                            make_rows(w + 1, c + 1)
                        level(w, 5)
                        if c + 1 < CH:
                            make(w + 1, c + 1)
                        if c:
                            copy_out(w - 1)
                        level(w, 6)
                        if c + 1 < CH:
                            turn(w + 1)
                    w = CH * h + CH - 1
                    pieces = [lambda: None, lambda: new_values(w, CH - 1), lambda: square(w),
                              lambda: copy_out(w), lambda: None]
                    for n, piece in enumerate(pieces):
                        piece()
                        if not last:
                            for t in ((0, 1), (2, 3), (4, 5), (), (6, 7))[n]:
                                copy_raw(h + 1, t)

                act.wait_ge(small, SMALL * 16)
                act.wait_ge(ba_ready, 1)
                act.sem_inc(raw_ready, 3)
                ba = ps[:, 0, :].rearrange("p (t n) -> p t n", t=TT)
                act.activation(gates[:, K_BETA * TT:(K_BETA + 1) * TT, :], ba[:, :, 0:VH],
                               ACT.Sigmoid).then_inc(g_act, 1)
                for t in range(8):
                    copy_raw(0, t)
                act.wait_ge(g_step, 1)
                act.activation(z_b[:, :, :], z_a[:, :, :], ACT.Abs).then_inc(g_act, 1)
                act.wait_ge(g_act, 2)
                act.activation(z_b[:, :, :], z_b[:, :, :], ACT.Exp, scale=-1.0).then_inc(g_act, 1)
                act.wait_ge(g_act, 3)
                act.activation(z_b[:, :, :], z_b[:, :, :], ACT.Ln, bias=1.0).then_inc(g_act, 1)
                act.activation(a_log[:, :], a_log[:, :], ACT.Exp).then_inc(g_act, 1)
                act.wait_ge(g_step, 6)
                for kind, n in ((K_LEFT, 6), (K_NEG, 7), (K_END, 8)):
                    act.activation(gates[:, kind * TT:(kind + 1) * TT, :],
                                   gates[:, kind * TT:(kind + 1) * TT, :], ACT.Exp).then_inc(g_act, 1)
                act.sem_inc(grown_ready, 1)
                act.sem_inc(vt0_ready, 1)
                act.sem_inc(ot_ready, 1)
                with act.Fori(0, KH - 1) as h:
                    head(h)
                head(KH - 1, last=True)

            @block.gpsimd
            def _(pool):
                pool.memset(half[:, :], -0.5).then_inc(filled, 1)
                pool.wait_ge(filled, 1)

                def root(w):
                    pool.wait_ge(var_ready, w + 1)
                    pool.tensor_tensor(rstd[:, :], var[:, :], half[:, :], ALU.pow).then_inc(rstd_ready, 1)

                with pool.Fori(0, VH * 2) as w:
                    root(w)

            @block.vector
            def _(dve):
                def convolve(h, mt):
                    if mt == 0:
                        dve.tensor_copy(cur_taps[:, :], taps[:, bass.ds(h, 1), :].rearrange("p h n -> p (h n)")
                                        if not isinstance(h, int) else taps[:, h, :]).then_inc(taps_ready, 1)
                        dve.wait_ge(taps_ready, h + 1)
                    dve.wait_ge(raw_ready, 8 * h + 2 * mt + 2 + 3)
                    dve.wait_ge(qkv_ready, 4 * h + mt + 1)
                    for j in range(TAPS):
                        tap = cur_taps[:, mt * TAPS + j:mt * TAPS + j + 1]
                        rows = raw[:, mt, :, j:j + T]
                        if j == 0:
                            dve.tensor_scalar(conv[:, mt, :, :], rows, tap, None, ALU.mult).then_inc(conv_step, 1)
                            continue
                        dve.wait_ge(conv_step, 12 * h + 3 * mt + j)
                        dve.scalar_tensor_tensor(conv[:, mt, :, :], rows, tap, conv[:, mt, :, :], ALU.mult,
                                                 ALU.add).then_inc(conv_ready if j == TAPS - 1 else conv_step, 1)

                def make_low(w, c):
                    dve.wait_ge(gc_ready, w + 1)
                    for r in range(PR):
                        dve.scalar_tensor_tensor(low[:, r, :], bank(BG)[:, r, :], gate(K_GC, c, r), floor[:, :],
                                                 ALU.subtract, ALU.min).then_inc(low_ready, 1)

                def make(w, c):
                    dve.wait_ge(kq_ready, w + 1)
                    dve.wait_ge(decay_ready, w + 1)
                    kq = bank(BK)
                    for k, to in ((B, at[:, c % 2, :, :]), (0, rough[:, :, :])):
                        mm = dve.tensor_tensor(
                            to.rearrange("p (b v) t -> p b v t", b=B),
                            kq[:, k:k + B, :].unsqueeze(2).broadcast_to([P, B, VPK, P]),
                            decay[:, :, :].rearrange("p (b v) t -> p b v t", b=B), ALU.mult)
                        mm.then_inc(rough_ready if k == 0 else at_ready, 1)
                    dve.wait_ge(rough_ready, w + 1 + 1)
                    for r in range(PR):
                        dve.scalar_tensor_tensor(v0[:, r, :], rough[:, r, :], gate(K_NBETA, c, r), strict[:, :],
                                                 ALU.mult, ALU.mult).then_inc(v0_ready, 1)

                def make_rest(w, c):
                    dve.wait_ge(v0_ready, PR * w + PR)
                    dve.tensor_tensor(inv[:, c % 2, :, :], v0[:, :, :],
                                      ident[:, :].unsqueeze(1).broadcast_to([P, PR, P]), ALU.add
                                      ).then_inc(inv_ready, 1)
                    dve.wait_ge(grown_ready, w + 1 + 1)
                    dve.tensor_tensor(qg[:, c % 2, :, :].rearrange("p (b v) t -> p b v t", b=B),
                                      qkv[:, 0, :, c * P:(c + 1) * P].unsqueeze(2).broadcast_to([P, B, VPK, P]),
                                      grown[:, :, :].rearrange("p (b v) t -> p b v t", b=B), ALU.mult
                                      ).then_inc(qg_ready, 1)

                def update(w, c, n):
                    dve.wait_ge(upd_psum, LEVELS * w + n)
                    dve.wait_ge(inv_ready, (LEVELS + 1) * w + n)
                    dve.tensor_tensor(inv[:, c % 2, :, :], inv[:, c % 2, :, :], bank(BUP), ALU.add
                                      ).then_inc(inv_ready, 1)

                def make_right(w, c):
                    dve.wait_ge(ks_psum, w + 1 + 1)
                    dve.wait_ge(vrow_ready, w + 1)
                    for r in range(PR):
                        dve.scalar_tensor_tensor(rest[:, r, :], bank(BR)[:, r, :], gate(K_NEG, c, r),
                                                 v_row[:, c % 2, r, :], ALU.mult, ALU.add).then_inc(rest_ready, 1)

                def gated(h, w, c):
                    dve.wait_ge(o_psum, w + 1)
                    if c == 0:
                        dve.wait_ge(zs_ready, 4 * h + 4)
                    dve.tensor_tensor(xf[:, :, :].rearrange("p (b v) t -> p b v t", b=B),
                                      bank(BO).rearrange("p (b v) t -> p b v t", b=B),
                                      zs[:, c::CH, :].rearrange("p b (v t) -> p b v t", v=VPK), ALU.mult
                                      ).then_inc(xf_ready, 1)
                    dve.wait_ge(ds_psum, w + 1)
                    for r in range(PR):
                        dve.scalar_tensor_tensor(state[:, r, :], state[:, r, :], gate(K_END, c, r),
                                                 bank(BR)[:, r, :], ALU.mult, ALU.add).then_inc(state_ready, 1)

                def reduce(w):
                    dve.wait_ge(sq_ready, w + 1)
                    dve.tensor_reduce(var[:, :], sq[:, :, :], AX.X, ALU.add).then_inc(var_step, 1)
                    dve.wait_ge(var_step, w + 1)
                    dve.tensor_scalar(var[:, :], var[:, :], 1.0 / P, 1e-6, ALU.mult, ALU.add).then_inc(var_ready, 1)

                def normed(w):
                    dve.wait_ge(rstd_ready, w + 1)
                    dve.tensor_tensor(xnorm[:, :, :], xf[:, :, :],
                                      rstd[:, :].unsqueeze(2).broadcast_to([P, PR, P]), ALU.mult
                                      ).then_inc(xnorm_ready, 1)

                def add_out(w, c):
                    dve.wait_ge(y_psum, w + 1)
                    part = x[:, :, :].rearrange("p m (b t) -> p m b t", b=B)[:, :, :, c * P:(c + 1) * P]
                    dve.tensor_tensor(part, part, ps[:, BO, :].rearrange("p (m b t) -> p m b t", m=KC, b=B),
                                      ALU.add).then_inc(added, 1)

                def head(h, last=False):
                    of = gates[:, :, bass.ds(h * VPK, VPK)]
                    dve.tensor_copy(cur[:, :, :], of).then_inc(cur_ready, 1)
                    dve.memset(state[:, :, :], 0.0).then_inc(zeroed, 1)
                    dve.wait_ge(cur_ready, h + 1)
                    make_low(CH * h, 0)
                    make(CH * h, 0)
                    make_rest(CH * h, 0)
                    for c in range(CH):
                        w = CH * h + c
                        if c:
                            make_right(w - 1, c - 1)
                        update(w, c, 1)
                        update(w, c, 2)
                        if c:
                            gated(h, w - 1, c - 1)
                        update(w, c, 3)
                        if c:
                            reduce(w - 1)
                        if c + 1 < CH:
                            make_low(w + 1, c + 1)
                        update(w, c, 4)
                        if c:
                            normed(w - 1)
                        if c + 1 < CH:
                            make(w + 1, c + 1)
                        update(w, c, 5)
                        if c + 1 < CH:
                            make_rest(w + 1, c + 1)
                        if c:
                            add_out(w - 1, c - 1)
                        update(w, c, 6)
                    w = CH * h + CH - 1
                    pieces = [lambda: make_right(w, CH - 1), lambda: None, lambda: gated(h, w, CH - 1),
                              lambda: (reduce(w), normed(w)), lambda: add_out(w, CH - 1)]
                    for n, piece in enumerate(pieces):
                        piece()
                        if not last:
                            for mt in ((), (0,), (1,), (2,), (3,))[n]:
                                convolve(h + 1, mt)

                dve.sem_inc(conv_ready, 4)
                dve.memset(raw[:, :, :, 0:TAPS - 1], 0.0).then_inc(filled_raw, 1)
                dve.wait_ge(filled_raw, 1)
                dve.wait_ge(small, SMALL * 16)
                dve.wait_ge(ba_ready, 1)
                ba = ps[:, 0, :].rearrange("p (t n) -> p t n", t=TT)
                dve.wait_ge(g_act, 1)
                dve.tensor_tensor(z_a[:, :, :], ba[:, :, VH:], dt_bias[:, :].unsqueeze(1).broadcast_to([P, TT, VH]),
                                  ALU.add).then_inc(g_step, 1)
                dve.wait_ge(g_act, 5)

                def kind(k):
                    return gates[:, k * TT:(k + 1) * TT, :]

                dve.scalar_tensor_tensor(z_b[:, :, :], z_a[:, :, :], 0.0, z_b[:, :, :], ALU.max,
                                         ALU.add).then_inc(g_step, 1)
                dve.tensor_scalar(a_log[:, :], a_log[:, :], -1.0, None, ALU.mult).then_inc(g_step, 1)
                dve.wait_ge(g_step, 3)
                dve.tensor_tensor(kind(K_G), z_b[:, :, :], a_log[:, :].unsqueeze(1).broadcast_to([P, TT, VH]),
                                  ALU.mult).then_inc(g_step, 1)
                dve.wait_ge(sums_ready, 1)
                gc = ps[:, 1, 0:TT * VH].rearrange("p (t v) -> p t v", t=TT)
                total = ps[:, 2, 0:TT * VH].rearrange("p (t v) -> p t v", t=TT)
                dve.tensor_copy(kind(K_GC), gc).then_inc(g_step, 1)
                dve.wait_ge(g_step, 5)
                dve.tensor_copy(kind(K_NEG), kind(K_GC))
                dve.tensor_copy(kind(K_END), total)
                dve.tensor_tensor(kind(K_LEFT), total, kind(K_GC), ALU.subtract).then_inc(g_step, 1)
                dve.tensor_scalar(kind(K_NBETA), kind(K_BETA), -1.0, None, ALU.mult).then_inc(g_step, 1)
                dve.wait_ge(g_act, 8)
                dve.wait_ge(g_step, 7)
                dve.tensor_scalar(kind(K_NEG), kind(K_NEG), -1.0, None, ALU.mult).then_inc(gates_ready, 1)
                dve.wait_ge(gates_ready, 1)
                dve.sem_inc(low_ready, PR)
                dve.sem_inc(rough_ready, 1)
                dve.sem_inc(xf_ready, 1)
                dve.sem_inc(added, 1)
                dve.sem_inc(ks_psum, 1)
                dve.sem_inc(qkv_ready, 4)
                for mt in range(4):
                    convolve(0, mt)
                with dve.Fori(0, KH - 1) as h:
                    head(h)
                head(KH - 1, last=True)



def _heads_padded(w, copies=1):
    k = w.shape[0]
    out = np.zeros((k, w.shape[1] // HD * copies, HP), np.float32)
    out[:, :, :HD] = np.repeat(w.reshape(k, -1, HD), copies, axis=1)
    return np.ascontiguousarray(out.reshape(k, -1))


def _blocks(m):
    return m.reshape(-1, P, m.shape[1]).transpose(1, 0, 2).reshape(P, -1)


def _constants():
    f = np.float32
    half = HD // 2
    frac = np.arange(0, HD, 2, dtype=f) / f(HD)
    inv = (f(1.0) / (f(10000.0) ** frac)).astype(f)
    ang = np.arange(T, dtype=f)[:, None] * inv[None, :]
    rope = np.zeros((P, 2, T), f)
    turn = np.zeros((P, P), f)
    sums_of = np.zeros((P, P), f)
    for p in range(P):
        r = p % HP
        if r < HD:
            rope[p, 0] = np.cos(ang[:, r % half])
            rope[p, 1] = np.sin(ang[:, r % half])
            if r < half:
                turn[p + half, p] = -1.0
            else:
                turn[p - half, p] = 1.0
        sums_of[p - r + HD, p] = 1.0
    rel = (np.arange(P)[:, None] + (T - P)) - np.arange(T)[None, :]
    away = np.where(rel < 0, f(1e30), rel).astype(f)
    had = np.ones((1, 1), f)
    while len(had) < P:
        had = np.block([[had, had], [had, -had]])
    start = 2.0 ** (-8.0 / NH)
    slopes = np.asarray([start * start ** i for i in range(NH)], f)
    return {
        "rope": rope, "turn": turn, "sums_of": sums_of, "ones": np.ones((P, P), f),
        "mean_of": np.full((P, P), 1.0 / C, f),
        "upto": np.triu(np.ones((P, P), f)), "strict": np.triu(np.ones((P, P), f), 1),
        "floor": np.where(np.triu(np.ones((P, P), bool)), f(0), f(-1e30)).astype(f),
        "ident": np.eye(P, dtype=f), "hadamard": had,
        "entry": np.tile(np.arange(LUT, dtype=f), (P, 1)),
        "away": away, "slopes": np.tile(slopes, (P, 1)),
        "order": np.tile(np.arange(E_ALL, dtype=f), (P, TT, 1)),
    }


def _arrays(i):
    a = _constants()
    a["x_t"] = i["L0_attn_x"].reshape(N, C).T
    a["a0_wq"] = _heads_padded(i["L0_attn_q_kernel"])
    a["a0_wk"] = _heads_padded(i["L0_attn_k_kernel"], HG)
    a["a0_wv"] = i["L0_attn_v_kernel"]
    a["a0_wo"] = _heads_padded(i["L0_attn_out_kernel"].T).T
    def columns(v):
        return v.reshape(-1, P).T

    a["a1_wq"] = _heads_padded(i["L1_attn_wq"])
    a["a1_wk"] = _heads_padded(i["L1_attn_wk"])
    a["a1_bq"] = columns(_heads_padded(i["L1_attn_bq"][None])[0])
    a["a1_bk"] = columns(_heads_padded(i["L1_attn_bk"][None])[0])
    a["a1_wv"], a["a1_bv"] = i["L1_attn_wv"], i["L1_attn_bv"]
    a["a1_wo"] = _heads_padded(i["L1_attn_wo"].T).T
    a["a1_bo"] = columns(i["L1_attn_bo"])
    a["a2_w"] = np.stack([i["L2_attn_W" + c].T for c in "qkv"])
    a["a2_bias"] = np.stack([columns(i["L2_attn_b" + c]) for c in "qkv"], axis=1)
    a["a2_wo"], a["a2_bo"] = i["L2_attn_Wo"].T, columns(i["L2_attn_bo"])
    a["f0_wr"] = i["L0_ffn_router_w"]
    a["f0_w1"], a["f0_w3"], a["f0_w2"] = i["L0_ffn_w1"], i["L0_ffn_v1"], i["L0_ffn_w2"]
    a["f2_wr"], a["f2_bias"] = i["L2_ffn_Wg"].T, i["L2_ffn_bias"]
    for w in ("W1", "W3", "W2"):
        a["f2_" + w.lower()] = i["L2_ffn_" + w].transpose(0, 2, 1)
    a["f1_su_ug"], a["f1_su_dp"] = columns(i["L1_ffn_SU_ug"]), columns(i["L1_ffn_SU_dp"])
    a["f1_sc_up"], a["f1_sc_gate"] = (columns(v) for v in np.split(i["L1_ffn_Wscale_ug"], 2))
    a["f1_sc_dp"] = columns(i["L1_ffn_Wscale_dp"])
    for w in ("up", "gate", "down"):
        a["f1_w_" + w] = i["L1_ffn_W_" + w].T
    down = np.zeros((WF * P, C), np.int32)
    down[:WIDE] = i["L3_ffn_down_idx"].T
    a["f3_index"] = np.concatenate(
        [_blocks(i["L3_ffn_gate_idx"].T), _blocks(i["L3_ffn_up_idx"].T), _blocks(down)], axis=1)
    a["f3_lut"] = i["L3_ffn_lut"]
    a["a3_w"] = i["L3_attn_W_qkvz"].reshape(C, KH, 6 * P).transpose(1, 0, 2)
    a["a3_wo"] = i["L3_attn_W_out"].reshape(KH, VPK * P, C)
    a["a3_w_ba"] = i["L3_attn_W_ba"].reshape(C, KH, 2, VPK).transpose(0, 2, 1, 3).reshape(C, 2 * VH)
    taps = i["L3_attn_conv_kernel"].reshape(TAPS, -1)
    q_taps, k_taps = (t.reshape(TAPS, KH, 1, P) for t in (taps[:, :KH * P], taps[:, KH * P:2 * KH * P]))
    by_head = np.concatenate([q_taps, k_taps, taps[:, 2 * KH * P:].reshape(TAPS, KH, VPK, P)], axis=2)
    a["a3_taps"] = by_head.transpose(3, 1, 2, 0).reshape(P, KH, 4 * TAPS)
    a["a3_dt"], a["a3_a_log"] = i["L3_attn_dt_bias"], i["L3_attn_A_log"]
    a["a3_nw"] = i["L3_attn_norm_weight"][:, None]
    return {k: np.ascontiguousarray(v) for k, v in a.items()}


ALL = ("n0", "a0", "f0", "n1", "a1", "f1", "n2", "a2", "f2", "n3", "a3", "f3")


def build(nc, d, stages=ALL):
    with Stage(nc, "all") as s:
        x, xn, mean_of = s.buf("x", [P, KC, N]), s.buf("xn", [P, KC, N]), s.buf("mean_of", [P, P])
        looked_up = s.buf("looked_up", [P, LOOKED])
        ps = s.ctx.enter_context(nc.psum_tensor("ps", [P, 8, BANK], F32))
        arrived, stored = s.sem("arrived"), s.sem("stored")
        with nc.Block() as block:
            @block.sync
            def _(sp):
                sp.dma_start(x[:, :, :], d["x_t"].rearrange("(k p) t -> p k t", p=P)).then_inc(arrived, 16)
                sp.dma_start(mean_of[:, :], d["mean_of"]).then_inc(arrived, 16)
                sp.wait_ge(arrived, 32)
        if "n0" in stages:
            layer_norm(nc, "n0", ps, x, xn, mean_of)
        if "a0" in stages:
            rope_attention(nc, ps, d, x, xn)
        if "f0" in stages:
            expert_layer(nc, "f0", ps, d, x, xn, 512, False, looked_up)
        if "n1" in stages:
            layer_norm(nc, "n1", ps, x, xn, mean_of)
        if "a1" in stages:
            alibi_attention(nc, ps, d, x, xn)
        if "f1" in stages:
            hadamard_layer(nc, ps, d, x, xn)
        if "n2" in stages:
            layer_norm(nc, "n2", ps, x, xn, mean_of)
        if "a2" in stages:
            linear_attention(nc, ps, d, x, xn)
        if "f2" in stages:
            expert_layer(nc, "f2", ps, d, x, xn, 128, True)
        if "n3" in stages:
            layer_norm(nc, "n3", ps, x, xn, mean_of)
        if "a3" in stages:
            delta_attention(nc, ps, d, x, xn)
        if "f3" in stages:
            looked_up_layer(nc, ps, looked_up, x, xn)
        with nc.Block() as block:
            @block.sync
            def _(sp):
                sp.dma_start(d["out_t"].rearrange("(k p) t -> p k t", p=P), x[:, :, :]).then_inc(stored, 16)
                sp.wait_ge(stored, 16)


def kernel(**inputs):
    import concourse.bacc as bacc
    from concourse.bass_utils import run_bass_kernel_spmd

    nc = bacc.Bacc("TRN2", target_bir_lowering=False, num_devices=1)
    arrays = _arrays({k: np.asarray(v) for k, v in inputs.items()})
    d = {k: nc.dram_tensor(f"in_{k}", v.shape, mybir.dt.from_np(v.dtype), kind="ExternalInput").ap()
         for k, v in arrays.items()}
    d["out_t"] = nc.dram_tensor("out_t", (C, N), F32, kind="ExternalOutput").ap()
    build(nc, d)
    r = run_bass_kernel_spmd(nc, [{f"in_{k}": v for k, v in arrays.items()}], core_ids=[0])
    return np.ascontiguousarray(r.results[0]["out_t"].T).reshape(B, T, C)
```

```python
from contextlib import ExitStack

import numpy as np

import concourse.bass as bass
from concourse import mybir

F32 = mybir.dt.float32
I32 = mybir.dt.int32
U32 = mybir.dt.uint32
ALU = mybir.AluOpType
ACT = mybir.ActivationFunctionType
AX = mybir.AxisListType

P = 128
B, T, C = 2, 512, 256
N = B * T
KC = C // P
TT = N // P
NH, HD = 16, 16
HP = 32
HG = P // HP
NG = NH // HG
BANK = 512


class Stage:

    def __init__(self, nc, name):
        self.nc, self.name, self.ctx, self.sems = nc, name, ExitStack(), []

    def __enter__(self):
        return self

    def __exit__(self, *error):
        if not error[0] and self.name != "all":
            with self.nc.Block() as block:
                @block.sync
                def _(sp):
                    for sem in self.sems:
                        sp.sem_clear(sem)
        self.ctx.close()

    def buf(self, name, shape, dtype=F32):
        return self.ctx.enter_context(self.nc.sbuf_tensor(f"{self.name}_{name}", shape, dtype))

    def sem(self, name):
        self.sems.append(self.ctx.enter_context(self.nc.semaphore(f"{self.name}_{name}")))
        return self.sems[-1]


def layer_norm(nc, name, ps, x, xn, mean_of):
    with Stage(nc, name) as s:
        square = s.buf("square", [P, KC, N])
        std = s.buf("std", [P, B, T])
        eps = s.buf("eps", [P, 1])
        mean_ready, centred, squared = s.sem("mean_ready"), s.sem("centred"), s.sem("squared")
        var_ready, std_ready, rstd_ready, normed = (
            s.sem("var_ready"), s.sem("std_ready"), s.sem("rstd_ready"), s.sem("normed"))
        eps_ready = s.sem("eps_ready")
        with nc.Block() as block:

            @block.tensor
            def _(pe):
                for b in range(B):
                    for k in range(KC):
                        mm = pe.matmul(ps[:, b, :], mean_of[:, :], x[:, k, b * T:(b + 1) * T],
                                       start=k == 0, stop=k == KC - 1)
                    mm.then_inc(mean_ready, 1)
                for b in range(B):
                    pe.wait_ge(squared, KC * (b + 1))
                    for k in range(KC):
                        mm = pe.matmul(ps[:, B + b, :], mean_of[:, :], square[:, k, b * T:(b + 1) * T],
                                       start=k == 0, stop=k == KC - 1)
                    mm.then_inc(var_ready, 1)

            @block.vector
            def _(dve):
                dve.memset(eps[:, :], 1e-5).then_inc(eps_ready, 1)
                for b in range(B):
                    dve.wait_ge(mean_ready, b + 1)
                    for k in range(KC):
                        part = slice(b * T, (b + 1) * T)
                        dve.tensor_tensor(xn[:, k, part], x[:, k, part], ps[:, b, :],
                                          ALU.subtract).then_inc(centred, 1)
                for b in range(B):
                    dve.wait_ge(std_ready, b + 1)
                    dve.reciprocal(std[:, b, :], std[:, b, :]).then_inc(rstd_ready, 1)
                    dve.wait_ge(rstd_ready, b + 1)
                    dve.wait_ge(squared, KC * (b + 1))
                    for k in range(KC):
                        part = slice(b * T, (b + 1) * T)
                        dve.tensor_tensor(xn[:, k, part], xn[:, k, part], std[:, b, :],
                                          ALU.mult).then_inc(normed, 1)

            @block.scalar
            def _(act):
                for b in range(B):
                    for k in range(KC):
                        act.wait_ge(centred, KC * b + k + 1)
                        part = slice(b * T, (b + 1) * T)
                        act.activation(square[:, k, part], xn[:, k, part],
                                       ACT.Square).then_inc(squared, 1)
                act.wait_ge(eps_ready, 1)
                for b in range(B):
                    act.wait_ge(var_ready, b + 1)
                    act.activation(std[:, b, :], ps[:, B + b, :], ACT.Sqrt,
                                   bias=eps[:, 0:1]).then_inc(std_ready, 1)


def rope_attention(nc, ps, d, x, xn):
    with Stage(nc, "a0") as s:
        wq, wk = s.buf("wq", [P, KC, NG * P]), s.buf("wk", [P, KC, NG * P])
        wv, wo = s.buf("wv", [P, KC, NG * HD]), s.buf("wo", [P, NG, C])
        rope = s.buf("rope", [P, 2, T])
        turn, sums_of, ones = s.buf("turn", [P, P]), s.buf("sums_of", [P, P]), s.buf("ones", [P, P])
        qk = s.buf("qk", [P, 2, B * NG, T])
        square = s.buf("square", [P, 4, T])
        rms = s.buf("rms", [P, 2 * B, T])
        turned = s.buf("turned", [P, 2, 2 * B, T])
        by_sin, by_cos = s.buf("by_sin", [P, 2, T]), s.buf("by_cos", [P, 2, T])
        values = s.buf("values", [P, TT * NG, HP])
        q_cur, k_cur = s.buf("q_cur", [P, 2, T]), s.buf("k_cur", [P, 2, T])
        v_cur = s.buf("v_cur", [P, 2, T // P, HP])
        probs = s.buf("probs", [P, 8, T])
        mixed = s.buf("mixed", [P, 2, T])
        recip = s.buf("recip", [P, 2, T])
        heads = s.buf("heads", [P, B * NG, T])
        eps = s.buf("eps", [P, 1])
        loaded, filled, v_ready, values_ready = (
            s.sem("loaded"), s.sem("filled"), s.sem("v_ready"), s.sem("values_ready"))
        proj_ready, raw_ready, sq_ready, sq_used = (
            s.sem("proj_ready"), s.sem("raw_ready"), s.sem("sq_ready"), s.sem("sq_used"))
        rms_ready, rrms_ready, turned_ready = (
            s.sem("rms_ready"), s.sem("rrms_ready"), s.sem("turned_ready"))
        swapped, sin_done, cos_done, roped = (
            s.sem("swapped"), s.sem("sin_done"), s.sem("cos_done"), s.sem("roped"))
        cur_ready, score_ready, probs_ready, probs_used = (
            s.sem("cur_ready"), s.sem("score_ready"), s.sem("probs_ready"), s.sem("probs_used"))
        mixed_ready, sums_ready, recip_ready, heads_ready = (
            s.sem("mixed_ready"), s.sem("sums_ready"), s.sem("recip_ready"), s.sem("heads_ready"))
        out_ready, added = s.sem("out_ready"), s.sem("added")
        NT = 2 * B * NG
        ST = T // P
        PER = 2 * ST * HG
        SCORES, PROBS = 4, 8

        def tile(t):
            return t // (B * NG), t // NG % B, t % NG

        with nc.Block() as block:

            @block.sync
            def _(sp):
                for to, of in ((wv, "a0_wv"), (wq, "a0_wq"), (wk, "a0_wk")):
                    sp.dma_start(to[:, :, :], d[of].rearrange("(k p) n -> p k n", p=P)).then_inc(loaded, 16)
                sp.dma_start(ones[:, :], d["ones"]).then_inc(loaded, 16)
                sp.dma_start(turn[:, :], d["turn"]).then_inc(loaded, 16)
                sp.dma_start(sums_of[:, :], d["sums_of"]).then_inc(loaded, 16)
                sp.dma_start(rope[:, :, :], d["rope"]).then_inc(loaded, 16)
                sp.dma_start(wo[:, :, :], d["a0_wo"].rearrange("(g p) n -> p g n", p=P)).then_inc(loaded, 16)

            @block.tensor
            def _(pe):
                pe.wait_ge(loaded, 8 * 16)
                for tt in range(TT):
                    for k in range(KC):
                        mm = pe.matmul(ps[:, 3, tt * 64:(tt + 1) * 64], xn[:, k, tt * P:(tt + 1) * P],
                                       wv[:, k, :], start=k == 0, stop=k == KC - 1)
                mm.then_inc(v_ready, 1)

                def add_squares(t):
                    kind, b, g = tile(t)
                    pe.wait_ge(sq_ready, t + 1)
                    pe.matmul(ps[:, 4 + kind * B + b, :], ones[:, :], square[:, t % 4, :],
                              start=g == 0, stop=g == NG - 1).then_inc(sq_used, 1)

                for t in range(NT):
                    kind, b, g = tile(t)
                    w = wk if kind else wq
                    if t >= 3:
                        pe.wait_ge(raw_ready, t - 2)
                    for k in range(KC):
                        mm = pe.matmul(ps[:, t % 3, :], w[:, k, g * P:(g + 1) * P],
                                       xn[:, k, b * T:(b + 1) * T], start=k == 0, stop=k == KC - 1)
                    mm.then_inc(proj_ready, 1)
                    if t >= 2:
                        add_squares(t - 2)
                add_squares(NT - 2)
                add_squares(NT - 1)
                for t in range(NT):
                    if t < 3:
                        pe.wait_ge(raw_ready, NT)
                    else:
                        pe.wait_ge(sin_done, t - 2)
                    kind, b, g = tile(t)
                    pe.matmul(ps[:, t % 3, :], turn[:, :], qk[:, kind, b * NG + g, :],
                              start=True, stop=True).then_inc(swapped, 1)
                pe.wait_ge(sin_done, NT)

                def mix(u, n):
                    v, st, j = n // (ST * HG), n // HG % ST, n % HG
                    pe.wait_ge(probs_ready, u * PER + n + 1 + SCORES)
                    pe.matmul(ps[j * HP:(j + 1) * HP, 4 + v, :], v_cur[:, v, st, :], probs[:, n % PROBS, :],
                              start=st == 0, stop=st == ST - 1).then_inc(probs_used, 1)

                def sum_weights(u, v):
                    pe.wait_ge(mixed_ready, 2 * u + v + 3)
                    pe.wait_ge(recip_ready, 2 * u + v + 1)
                    pe.matmul(ps[:, 6, :], sums_of[:, :], mixed[:, v, :],
                              start=True, stop=True).then_inc(sums_ready, 1)

                with pe.Fori(0, B * NG // 2) as u:
                    for v in range(2):
                        pe.wait_ge(cur_ready, u * 6 + 3 * v + 3)
                        for st in range(ST):
                            for j in range(HG):
                                n = (v * ST + st) * HG + j
                                pe.wait_ge(probs_ready, u * PER + n + 1)
                                rows = slice(j * HP, (j + 1) * HP)
                                pe.matmul(ps[:, n % SCORES, :], k_cur[rows, v, st * P:(st + 1) * P],
                                          q_cur[rows, v, :], start=True, stop=True).then_inc(score_ready, 1)
                            if st == 1 and v:
                                sum_weights(u, 0)
                            if v or st:
                                for j in range(HG):
                                    mix(u, n - 2 * HG + 1 + j)
                    for j in range(HG):
                        mix(u, PER - HG + j)
                    sum_weights(u, 1)
                for b in range(B):
                    pe.wait_ge(heads_ready, B * NG)
                    for m in range(KC):
                        for g in range(NG):
                            mm = pe.matmul(ps[:, b * KC + m, :], wo[:, g, m * P:(m + 1) * P],
                                           heads[:, b * NG + g, :], start=g == 0, stop=g == NG - 1)
                        mm.then_inc(out_ready, 1)

            @block.scalar
            def _(act):
                for t in range(NT):
                    kind, b, g = tile(t)
                    act.wait_ge(proj_ready, t + 1)
                    act.activation(qk[:, kind, b * NG + g, :], ps[:, t % 3, :],
                                   ACT.Copy).then_inc(raw_ready, 1)
                act.wait_ge(filled, 2)
                for r in range(2 * B):
                    act.wait_ge(sq_used, NG * (r + 1))
                    act.activation(rms[:, r, :], ps[:, 4 + r, :], ACT.Sqrt, bias=eps[:, 0:1],
                                   scale=1.0 / C).then_inc(rms_ready, 1)
                act.sem_inc(probs_ready, SCORES)
                with act.Fori(0, B * NG // 2) as u:
                    for n in range(PER):
                        act.wait_ge(score_ready, u * PER + n + 1)
                        act.wait_ge(probs_used, u * PER + n + 1)
                        act.activation(probs[:, n % PROBS, :], ps[:, n % SCORES, :], ACT.Exp,
                                       scale=HD ** -0.5).then_inc(probs_ready, 1)

            @block.gpsimd
            def _(pool):
                pool.sem_inc(probs_used, PROBS)
                pool.sem_inc(recip_ready, 1)
                pool.sem_inc(mixed_ready, 2)
                for t in range(NT):
                    kind, b, g = tile(t)
                    raw = qk[:, kind, b * NG + g, :]
                    pool.wait_ge(raw_ready, t + 1)
                    if t >= 4:
                        pool.wait_ge(sq_used, t - 3)
                    pool.tensor_tensor(square[:, t % 4, :], raw, raw, ALU.mult).then_inc(sq_ready, 1)
                for t in range(NT):
                    kind, b, g = tile(t)
                    pool.wait_ge(turned_ready, 2 * (kind * B + b) + 1)
                    if t >= 2:
                        pool.wait_ge(roped, t - 1)
                    pool.tensor_tensor(by_cos[:, t % 2, :], qk[:, kind, b * NG + g, :],
                                       turned[:, 0, kind * B + b, :], ALU.mult).then_inc(cos_done, 1)
                pool.wait_ge(roped, NT)
                pool.wait_ge(values_ready, 1)
                with pool.Fori(0, B * NG // 2) as u:
                    for v in range(2):
                        pool.wait_ge(mixed_ready, 2 * u + v + 1)
                        i = u * 2 + v
                        pool.tensor_copy(q_cur[:, v, :], qk[:, 0, i, :]).then_inc(cur_ready, 1)
                        pool.tensor_copy(k_cur[:, v, :], qk[:, 1, i, :]).then_inc(cur_ready, 1)
                        pool.tensor_copy(v_cur[:, v, :, :], values[:, bass.ds(i * ST, ST), :]).then_inc(cur_ready, 1)

            @block.vector
            def _(dve):
                dve.memset(eps[:, :], 1e-6).then_inc(filled, 1)
                dve.memset(values[:, :, :], 1.0).then_inc(filled, 1)
                dve.wait_ge(filled, 2)
                dve.wait_ge(v_ready, 1)
                for b in range(B):
                    for g in range(NG):
                        at = (b * NG + g) * ST
                        of = ps[:, 3, b * 256:(b + 1) * 256].rearrange("p (s g e) -> p s g e", s=ST, g=NG)
                        cp = dve.tensor_copy(values[:, at:at + ST, 0:HD], of[:, :, g, :])
                cp.then_inc(values_ready, 1)
                dve.wait_ge(loaded, 8 * 16)
                for r in range(2 * B):
                    dve.wait_ge(rms_ready, r + 1)
                    dve.reciprocal(rms[:, r, :], rms[:, r, :]).then_inc(rrms_ready, 1)
                    dve.wait_ge(rrms_ready, r + 1)
                    for c in range(2):
                        dve.tensor_tensor(turned[:, c, r, :], rope[:, c, :], rms[:, r, :],
                                          ALU.mult).then_inc(turned_ready, 1)
                for t in range(NT):
                    kind, b, g = tile(t)
                    dve.wait_ge(turned_ready, 2 * (kind * B + b) + 2)
                    dve.wait_ge(swapped, t + 1)
                    dve.tensor_tensor(by_sin[:, t % 2, :], ps[:, t % 3, :],
                                      turned[:, 1, kind * B + b, :], ALU.mult).then_inc(sin_done, 1)
                    dve.wait_ge(sin_done, t + 1)
                    dve.wait_ge(cos_done, t + 1)
                    dve.tensor_tensor(qk[:, kind, b * NG + g, :], by_sin[:, t % 2, :], by_cos[:, t % 2, :],
                                      ALU.add).then_inc(roped, 1)
                with dve.Fori(0, B * NG // 2) as u:
                    for v in range(2):
                        dve.wait_ge(probs_used, u * PER + (v + 1) * (PER // 2) + PROBS)
                        dve.tensor_copy(mixed[:, v, :], ps[:, 4 + v, :]).then_inc(mixed_ready, 1)
                        dve.wait_ge(sums_ready, 2 * u + v + 1)
                        dve.reciprocal(recip[:, v, :], ps[:, 6, :]).then_inc(recip_ready, 1)
                        dve.wait_ge(recip_ready, 2 * u + v + 2)
                        dve.tensor_tensor(heads[:, u * 2 + v, :], mixed[:, v, :], recip[:, v, :],
                                          ALU.mult).then_inc(heads_ready, 1)
                for b in range(B):
                    for m in range(KC):
                        dve.wait_ge(out_ready, b * KC + m + 1)
                        part = x[:, m, b * T:(b + 1) * T]
                        dve.tensor_tensor(part, part, ps[:, b * KC + m, :], ALU.add).then_inc(added, 1)


def alibi_attention(nc, ps, d, x, xn):
    with Stage(nc, "a1") as s:
        wq, wk = s.buf("wq", [P, KC, NG * P]), s.buf("wk", [P, KC, NG * P])
        wv, wo = s.buf("wv", [P, KC, C]), s.buf("wo", [P, NG, C])
        bq, bk, bo = s.buf("bq", [P, NG]), s.buf("bk", [P, NG]), s.buf("bo", [P, KC])
        bq_s = s.buf("bq_s", [P, NG])
        bv = s.buf("bv", [P, C])
        sums_of, ident = s.buf("sums_of", [P, P]), s.buf("ident", [P, P])
        away = s.buf("away", [P, T])
        slopes = s.buf("slopes", [P, NH])
        qk = s.buf("qk", [P, 2, NG * B, T])
        values = s.buf("values", [P, NG * B * (T // P), HG, HP])
        q_cur, k_cur = s.buf("q_cur", [P, 2, T]), s.buf("k_cur", [P, 2, T])
        v_cur = s.buf("v_cur", [P, 2, T // P, HG, HP])
        slope_cur = s.buf("slope_cur", [P, HG])
        score = s.buf("score", [P, 4, T])
        least = s.buf("least", [P, 4, 1])
        probs, probs_t = s.buf("probs", [P, 4, T]), s.buf("probs_t", [P, 4, T])
        mixed = s.buf("mixed", [P, 2, T])
        recip = s.buf("recip", [P, 2, T])
        heads = s.buf("heads", [P, NG * B, T])
        loaded, filled, bias_ready = s.sem("loaded"), s.sem("filled"), s.sem("bias_ready")
        proj_ready, qk_ready, v_ready, values_ready = (
            s.sem("proj_ready"), s.sem("qk_ready"), s.sem("v_ready"), s.sem("values_ready"))
        cur_ready, slope_ready, score_ready, biased, least_ready = (
            s.sem("cur_ready"), s.sem("slope_ready"), s.sem("score_ready"), s.sem("biased"),
            s.sem("least_ready"))
        probs_ready, turned, turned_ready, turned_used = (
            s.sem("probs_ready"), s.sem("turned"), s.sem("turned_ready"), s.sem("turned_used"))
        mixed_ready, sums_ready, recip_ready, heads_ready = (
            s.sem("mixed_ready"), s.sem("sums_ready"), s.sem("recip_ready"), s.sem("heads_ready"))
        out_ready, added = s.sem("out_ready"), s.sem("added")
        NT = 2 * NG * B
        ST = T // P
        HALF = ST * HG
        PER = 2 * HALF
        LOADS = 14

        def tile(t):
            return t // (NG * B), t // B % NG, t % B

        def unit(n):
            return n // HALF, n % HALF // HG, n % HG

        with nc.Block() as block:

            @block.sync
            def _(sp):
                for to, of in ((wq, "a1_wq"), (wk, "a1_wk"), (wv, "a1_wv"), (wo, "a1_wo")):
                    sp.dma_start(to[:, :, :], d[of].rearrange("(k p) n -> p k n", p=P)).then_inc(loaded, 16)
                for to, of in ((bq, "a1_bq"), (bk, "a1_bk"), (bo, "a1_bo")):
                    sp.dma_start(to[:, :], d[of]).then_inc(loaded, 16)
                sp.dma_start(bv[:, :], d["a1_bv"].partition_broadcast(P)).then_inc(loaded, 16)
                for to, of in ((sums_of, "sums_of"), (ident, "ident"), (away, "away"), (slopes, "slopes")):
                    sp.dma_start(to[:, :], d[of]).then_inc(loaded, 16)

            @block.tensor
            def _(pe):
                pe.wait_ge(loaded, 12 * 16)
                for t in range(NT):
                    kind, g, b = tile(t)
                    w = wk if kind else wq
                    if t >= 3:
                        pe.wait_ge(qk_ready, t - 2)
                    for k in range(KC):
                        mm = pe.matmul(ps[:, t % 3, :], w[:, k, g * P:(g + 1) * P],
                                       xn[:, k, b * T:(b + 1) * T], start=k == 0, stop=k == KC - 1)
                    mm.then_inc(proj_ready, 1)
                for tt in range(TT):
                    if tt >= 4:
                        pe.wait_ge(values_ready, tt - 3)
                    for k in range(KC):
                        mm = pe.matmul(ps[:, 3 + tt % 4, 0:C], xn[:, k, tt * P:(tt + 1) * P],
                                       wv[:, k, :], start=k == 0, stop=k == KC - 1)
                    mm.then_inc(v_ready, 1)
                pe.wait_ge(qk_ready, NT)
                pe.wait_ge(values_ready, TT)

                def scores(u, n):
                    v, qt, j = unit(n)
                    rows = slice(j * HP, (j + 1) * HP)
                    pe.wait_ge(biased, u * PER + n + 1)
                    pe.matmul(ps[:, n % 3, 0:(qt + 1) * P], q_cur[rows, v, qt * P:(qt + 1) * P],
                              k_cur[rows, v, 0:(qt + 1) * P], start=True, stop=True).then_inc(score_ready, 1)

                def turn(u, n):
                    v, qt, j = unit(n)
                    pe.wait_ge(probs_ready, u * PER + n + 1 + 4)
                    pe.wait_ge(turned_ready, u * PER + n + 1)
                    for kt in range(qt + 1):
                        mm = pe.transpose(ps[:, 3 + n % 2, kt * P:(kt + 1) * P],
                                          probs[:, n % 4, kt * P:(kt + 1) * P], ident[:, :])
                    mm.then_inc(turned, 1)

                def mix(u, n):
                    v, qt, j = unit(n)
                    pe.wait_ge(turned_ready, u * PER + n + 1 + 2)
                    for kt in range(qt + 1):
                        mm = pe.matmul(ps[j * HP:(j + 1) * HP, 5 + v, qt * P:(qt + 1) * P],
                                       v_cur[:, v, kt, j, :], probs_t[:, n % 4, kt * P:(kt + 1) * P],
                                       start=kt == 0, stop=kt == qt)
                    mm.then_inc(turned_used, 1)

                def sum_weights(u, v):
                    pe.wait_ge(mixed_ready, 2 * u + v + 1 + 2)
                    pe.wait_ge(recip_ready, 2 * u + v + 1)
                    pe.matmul(ps[:, 7, :], sums_of[:, :], mixed[:, v, :],
                              start=True, stop=True).then_inc(sums_ready, 1)

                with pe.Fori(0, NG) as u:
                    for n in range(PER + 4):
                        if n < PER:
                            if n % HALF == 0:
                                pe.wait_ge(cur_ready, 6 * u + 3 * (n // HALF) + 3)
                            scores(u, n)
                        if 2 <= n < PER + 2:
                            turn(u, n - 2)
                        if n >= 4:
                            mix(u, n - 4)
                        if n == HALF + 8:
                            sum_weights(u, 0)
                    sum_weights(u, 1)
                pe.wait_ge(heads_ready, NG * B)
                for b in range(B):
                    for m in range(KC):
                        for g in range(NG):
                            mm = pe.matmul(ps[:, b * KC + m, :], wo[:, g, m * P:(m + 1) * P],
                                           heads[:, g * B + b, :], start=g == 0, stop=g == NG - 1)
                        mm.then_inc(out_ready, 1)

            @block.scalar
            def _(act):
                act.wait_ge(loaded, 12 * 16)
                act.wait_ge(bias_ready, 1)
                for t in range(NT):
                    kind, g, b = tile(t)
                    act.wait_ge(proj_ready, t + 1)
                    if kind:
                        act.activation(qk[:, 1, g * B + b, :], ps[:, t % 3, :], ACT.Identity,
                                       bias=bk[:, g:g + 1]).then_inc(qk_ready, 1)
                    else:
                        act.activation(qk[:, 0, g * B + b, :], ps[:, t % 3, :], ACT.Identity,
                                       bias=bq_s[:, g:g + 1], scale=-HD ** -0.5).then_inc(qk_ready, 1)
                act.sem_inc(probs_ready, 4)
                act.sem_inc(turned_ready, 2)

                def copy_turned(u, n):
                    v, qt, j = unit(n)
                    act.wait_ge(turned, u * PER + n + 1 + 4)
                    act.wait_ge(turned_used, u * PER + n + 1)
                    act.activation(probs_t[:, n % 4, 0:(qt + 1) * P], ps[:, 3 + n % 2, 0:(qt + 1) * P],
                                   ACT.Copy).then_inc(turned_ready, 1)

                with act.Fori(0, NG) as u:
                    for n in range(PER + 2):
                        if n < PER:
                            v, qt, j = unit(n)
                            act.wait_ge(least_ready, u * PER + n + 1)
                            act.wait_ge(turned, u * PER + n + 1)
                            act.activation(probs[:, n % 4, 0:(qt + 1) * P], score[:, n % 4, 0:(qt + 1) * P],
                                           ACT.Exp, bias=least[:, n % 4, :], scale=-1.0).then_inc(probs_ready, 1)
                        if n >= 2:
                            copy_turned(u, n - 2)

            @block.gpsimd
            def _(pool):
                pool.sem_inc(biased, 3)
                pool.sem_inc(turned, 4)
                pool.sem_inc(turned_used, 4)
                pool.sem_inc(recip_ready, 1)
                pool.sem_inc(mixed_ready, 2)
                pool.wait_ge(qk_ready, NT)
                pool.wait_ge(values_ready, TT)
                with pool.Fori(0, NG) as u:
                    for v in range(2):
                        pool.wait_ge(mixed_ready, 2 * u + v + 1)
                        i = u * 2 + v
                        pool.tensor_copy(q_cur[:, v, :], qk[:, 0, i, :]).then_inc(cur_ready, 1)
                        pool.tensor_copy(k_cur[:, v, :], qk[:, 1, i, :]).then_inc(cur_ready, 1)
                        pool.tensor_copy(v_cur[:, v, :, :, :],
                                         values[:, bass.ds(i * ST, ST), :, :]).then_inc(cur_ready, 1)

            @block.vector
            def _(dve):
                dve.memset(values[:, :, :, :], 1.0).then_inc(filled, 1)
                dve.wait_ge(loaded, 12 * 16)
                dve.tensor_scalar(bq_s[:, :], bq[:, :], -HD ** -0.5, None, ALU.mult).then_inc(bias_ready, 1)
                dve.wait_ge(filled, 1)
                for tt in range(TT):
                    b, st = tt // ST, tt % ST
                    dve.wait_ge(v_ready, tt + 1)
                    of = ps[:, 3 + tt % 4, 0:C].rearrange("p (g j e) -> p g j e", g=NG, j=HG)
                    to = values[:, :, :, :].rearrange("p (g b s) j e -> p g b s j e", g=NG, b=B)
                    for g in range(NG):
                        cp = dve.tensor_tensor(to[:, g, b, st, :, 0:HD], of[:, g, :, :],
                                               bv[:, g * 64:(g + 1) * 64].rearrange("p (j e) -> p j e", j=HG),
                                               ALU.add)
                    cp.then_inc(values_ready, 1)

                def norm(u, v):
                    dve.wait_ge(turned_used, u * PER + (v + 1) * HALF + 4)
                    dve.tensor_copy(mixed[:, v, :], ps[:, 5 + v, :]).then_inc(mixed_ready, 1)

                def weigh(u, v):
                    dve.wait_ge(sums_ready, 2 * u + v + 1)
                    dve.reciprocal(recip[:, v, :], ps[:, 7, :]).then_inc(recip_ready, 1)
                    dve.wait_ge(recip_ready, 2 * u + v + 2)
                    dve.tensor_tensor(heads[:, u * 2 + v, :], mixed[:, v, :], recip[:, v, :],
                                      ALU.mult).then_inc(heads_ready, 1)

                with dve.Fori(0, NG) as u:
                    dve.tensor_copy(slope_cur[:, :], slopes[:, bass.ds(u * HG, HG)]).then_inc(slope_ready, 1)
                    dve.wait_ge(slope_ready, u + 1)
                    for n in range(PER):
                        v, qt, j = unit(n)
                        w = (qt + 1) * P
                        dve.wait_ge(score_ready, u * PER + n + 1)
                        dve.wait_ge(probs_ready, u * PER + n + 1)
                        dve.scalar_tensor_tensor(score[:, n % 4, 0:w], away[:, T - w:T], slope_cur[:, j:j + 1],
                                                 ps[:, n % 3, 0:w], ALU.mult, ALU.add).then_inc(biased, 1)
                        dve.wait_ge(biased, u * PER + n + 1 + 3)
                        dve.tensor_reduce(least[:, n % 4, :], score[:, n % 4, 0:w], AX.X,
                                          ALU.min).then_inc(least_ready, 1)
                        if n == HALF + 5:
                            norm(u, 0)
                        if n == HALF + 9:
                            weigh(u, 0)
                    norm(u, 1)
                    weigh(u, 1)
                for b in range(B):
                    for m in range(KC):
                        dve.wait_ge(out_ready, b * KC + m + 1)
                        part = x[:, m, b * T:(b + 1) * T]
                        dve.scalar_tensor_tensor(part, ps[:, b * KC + m, :], bo[:, m:m + 1], part,
                                                 ALU.add, ALU.add).then_inc(added, 1)


def linear_attention(nc, ps, d, x, xn):
    with Stage(nc, "a2") as s:
        w = s.buf("w", [P, 3, KC, C])
        wo, bias, bo = s.buf("wo", [P, KC, C]), s.buf("bias", [P, 3, KC]), s.buf("bo", [P, KC])
        ones = s.buf("ones", [P, T])
        expo, relu = s.buf("expo", [P, 2 * KC * B, T]), s.buf("relu", [P, 2 * KC * B, T])
        val = s.buf("val", [P, KC * B, T])
        total = s.buf("total", [P, KC * B, T])
        loaded, filled, proj_ready, exp_ready, relu_ready = (
            s.sem("loaded"), s.sem("filled"), s.sem("proj_ready"), s.sem("exp_ready"), s.sem("relu_ready"))
        phi_ready, val_ready, kv_ready, total_ready, ctx_ready, out_ready, added = (
            s.sem("phi_ready"), s.sem("val_ready"), s.sem("kv_ready"), s.sem("total_ready"),
            s.sem("ctx_ready"), s.sem("out_ready"), s.sem("added"))
        KINDS = (1, 2, 0)
        NT = 3 * KC * B

        def tile(t):
            return KINDS[t // (KC * B)], t // B % KC, t % B

        with nc.Block() as block:

            @block.sync
            def _(sp):
                sp.dma_start(w[:, :, :, :], d["a2_w"].rearrange("q (k p) n -> p q k n", p=P)).then_inc(loaded, 16)
                sp.dma_start(wo[:, :, :], d["a2_wo"].rearrange("(k p) n -> p k n", p=P)).then_inc(loaded, 16)
                sp.dma_start(bias[:, :, :], d["a2_bias"]).then_inc(loaded, 16)
                sp.dma_start(bo[:, :], d["a2_bo"]).then_inc(loaded, 16)

            @block.tensor
            def _(pe):
                pe.wait_ge(loaded, 4 * 16)
                for t in range(NT):
                    kind, m, b = tile(t)
                    if t >= 8:
                        pe.wait_ge(relu_ready, t - 7)
                    for k in range(KC):
                        mm = pe.matmul(ps[:, t % 8, :], w[:, kind, k, m * P:(m + 1) * P],
                                       xn[:, k, b * T:(b + 1) * T], start=k == 0, stop=k == KC - 1)
                    mm.then_inc(proj_ready, 1)
                for b in range(B):
                    for m in range(KC):
                        pe.wait_ge(val_ready, KC * B)
                        pe.wait_ge(ctx_ready, KC * (b + 1))
                        for k in range(KC):
                            mm = pe.matmul(ps[:, 4 + b * KC + m, :], wo[:, k, m * P:(m + 1) * P],
                                           total[:, k * B + b, :], start=k == 0, stop=k == KC - 1)
                        mm.then_inc(out_ready, 1)

            @block.scalar
            def _(act):
                act.wait_ge(loaded, 4 * 16)
                n = 0
                for t in range(NT):
                    kind, m, b = tile(t)
                    act.wait_ge(proj_ready, t + 1)
                    at = ps[:, t % 8, :]
                    if kind == 2:
                        act.activation(val[:, m * B + b, :], at, ACT.Identity,
                                       bias=bias[:, kind, m:m + 1]).then_inc(val_ready, 1)
                        continue
                    act.activation(expo[:, n, :], at, ACT.Exp, bias=bias[:, kind, m:m + 1]).then_inc(exp_ready, 1)
                    act.activation(relu[:, n, :], at, ACT.Relu, bias=bias[:, kind, m:m + 1]).then_inc(relu_ready, 1)
                    n += 1

            @block.vector
            def _(dve):
                dve.memset(ones[:, :], 1.0).then_inc(filled, 1)

                def phi(n):
                    dve.wait_ge(exp_ready, n + 1)
                    dve.wait_ge(relu_ready, n + 1)
                    dve.scalar_tensor_tensor(expo[:, n, :], expo[:, n, :], 1.0, relu[:, n, :],
                                             ALU.min, ALU.add).then_inc(phi_ready, 1)

                for n in range(KC * B):
                    phi(n)
                dve.wait_ge(filled, 1)
                for n in range(KC * B):
                    dve.wait_ge(phi_ready, n + 1)
                    dve.wait_ge(val_ready, n + 1)
                    dve.tensor_tensor(val[:, n, :], expo[:, n, :], val[:, n, :], ALU.mult).then_inc(kv_ready, 1)
                for n in range(KC * B):
                    dve.wait_ge(kv_ready, n + 1)
                    dve.tensor_tensor_scan(total[:, n, :], ones[:, :], val[:, n, :], 0.0,
                                           ALU.mult, ALU.add).then_inc(total_ready, 1)
                for n in range(KC * B):
                    phi(KC * B + n)
                for b in range(B):
                    for m in range(KC):
                        n = m * B + b
                        dve.wait_ge(phi_ready, KC * B + n + 1)
                        dve.wait_ge(total_ready, n + 1)
                        dve.scalar_tensor_tensor(total[:, n, :], expo[:, KC * B + n, :], HD ** -0.5,
                                                 total[:, n, :], ALU.mult, ALU.mult).then_inc(ctx_ready, 1)
                for b in range(B):
                    for m in range(KC):
                        dve.wait_ge(out_ready, b * KC + m + 1)
                        part = x[:, m, b * T:(b + 1) * T]
                        dve.scalar_tensor_tensor(part, ps[:, 4 + b * KC + m, :], bo[:, m:m + 1], part,
                                                 ALU.add, ALU.add).then_inc(added, 1)


E_ALL = 8
TOP = 2


def expert_layer(nc, name, ps, d, x, xn, width, by_sigmoid, looked_up=None):
    FT = width // P
    with Stage(nc, name) as s:
        wr = s.buf("wr", [P, KC, E_ALL])
        ident, order = s.buf("ident", [P, P]), s.buf("order", [P, TT, E_ALL])
        bias = s.buf("bias", [P, E_ALL])
        choice, prob = s.buf("choice", [P, TT, E_ALL]), s.buf("prob", [P, TT, E_ALL])
        best, where = s.buf("best", [P, TT, 8]), s.buf("where", [P, TT, 8], U32)
        index = s.buf("index", [P, TT, 8])
        taken, also = s.buf("taken", [P, TT, E_ALL]), s.buf("also", [P, TT, E_ALL])
        norm = s.buf("norm", [P, TT])
        share = s.buf("share", [P, E_ALL, N])
        w1, w3 = s.buf("w1", [P, 2, KC, width]), s.buf("w3", [P, 2, KC, width])
        w2 = s.buf("w2", [P, 2, FT, C])
        act_h, gated = s.buf("act_h", [P, 2, T]), s.buf("gated", [P, 4, T])
        part_out = s.buf("part_out", [P, 4, T])
        routed = s.sem("routed")
        if looked_up is not None:
            index_in = s.buf("index_in", [P, LOOKED], I32)
            table, entry = s.buf("table", [P, LUT]), s.buf("entry", [P, LUT])
            term = s.buf("term", [P, 2, LOOKED // 4])
            t_loaded, summed, term_ready = s.sem("t_loaded"), s.sem("summed"), s.sem("term_ready")
        r_loaded, logits_ready, r_step, prob_ready = (
            s.sem("r_loaded"), s.sem("logits_ready"), s.sem("r_step"), s.sem("prob_ready"))
        share_ready, share_copied = s.sem("share_ready"), s.sem("share_copied")
        w_loaded = [s.sem("w_loaded0"), s.sem("w_loaded1")]
        up_ready, silu_ready, gated_ready, down_done = (
            s.sem("up_ready"), s.sem("silu_ready"), s.sem("gated_ready"), s.sem("down_done"))
        part_ready, added = s.sem("part_ready"), s.sem("added")
        TILES = FT * B
        PER = 2 * TILES

        with nc.Block() as block:

            def load(eng, e, v):
                eng.dma_start(w1[:, v, :, :], d[name + "_w1"][e, :, :].rearrange("(k p) n -> p k n", p=P)
                              ).then_inc(w_loaded[v], 16)
                eng.dma_start(w3[:, v, :, :], d[name + "_w3"][e, :, :].rearrange("(k p) n -> p k n", p=P)
                              ).then_inc(w_loaded[v], 16)
                eng.dma_start(w2[:, v, :, :], d[name + "_w2"][e, :, :].rearrange("(f p) n -> p f n", p=P)
                              ).then_inc(w_loaded[v], 16)

            @block.sync
            def _(sp):
                sp.dma_start(wr[:, :, :], d[name + "_wr"].rearrange("(k p) n -> p k n", p=P)).then_inc(r_loaded, 16)
                sp.dma_start(ident[:, :], d["ident"]).then_inc(r_loaded, 16)
                sp.dma_start(order[:, :, :], d["order"]).then_inc(r_loaded, 16)
                if by_sigmoid:
                    sp.dma_start(bias[:, :], d[name + "_bias"].partition_broadcast(P)).then_inc(r_loaded, 16)
                for v in range(2):
                    load(sp, v, v)
                if looked_up is not None:
                    sp.dma_start(index_in[:, :], d["f3_index"]).then_inc(t_loaded, 16)
                    sp.dma_start(table[:, :], d["f3_lut"].partition_broadcast(P)).then_inc(t_loaded, 16)
                    sp.dma_start(entry[:, :], d["entry"]).then_inc(t_loaded, 16)
                with sp.Fori(0, E_ALL // 2 - 1) as u:
                    for v in range(2):
                        sp.wait_ge(down_done, u * PER + (v + 1) * TILES + 4)
                        load(sp, u * 2 + 2 + v, v)

            @block.tensor
            def _(pe):
                pe.wait_ge(r_loaded, (3 + by_sigmoid) * 16)
                for tt in range(TT):
                    for k in range(KC):
                        mm = pe.matmul(ps[:, 0, tt * E_ALL:(tt + 1) * E_ALL], xn[:, k, tt * P:(tt + 1) * P],
                                       wr[:, k, :], start=k == 0, stop=k == KC - 1)
                mm.then_inc(logits_ready, 1)
                pe.wait_ge(routed, 1)
                for e in range(E_ALL):
                    for b in range(B):
                        n = e * B + b
                        if n >= 4:
                            pe.wait_ge(share_copied, n - 3)
                        for q in range(T // P):
                            mm = pe.matmul(ps[:, n % 4, q * P:(q + 1) * P],
                                           taken[:, b * (T // P) + q, e:e + 1].to_broadcast([P, P]),
                                           ident[:, :], start=True, stop=True)
                        mm.then_inc(share_ready, 1)
                pe.wait_ge(share_copied, E_ALL * B)

                def down(u, v, i):
                    f, b = i // B, i % B
                    pe.wait_ge(gated_ready, u * PER + v * TILES + i + 1 + 2)
                    if f == 0:
                        pe.wait_ge(part_ready, 8 * u + 4 * v + 2 * b + 2)
                    for m in range(KC):
                        mm = pe.matmul(ps[:, 4 + b * KC + m, :], w2[:, v, f, m * P:(m + 1) * P],
                                       gated[:, (v * TILES + i) % 4, :], start=f == 0, stop=f == FT - 1)
                    mm.then_inc(down_done, 1)

                with pe.Fori(0, E_ALL // 2) as u:
                    for n in range(PER + 1):
                        v, i = n // TILES, n % TILES
                        f, b = i // B, i % B
                        if n < PER:
                            if i == 0:
                                pe.wait_ge(w_loaded[v], 48 * u + 48)
                            pe.wait_ge(gated_ready, u * PER + n + 1)
                            for w, bank in ((w1, 0), (w3, 2)):
                                for k in range(KC):
                                    mm = pe.matmul(ps[:, bank + n % 2, :], w[:, v, k, f * P:(f + 1) * P],
                                                   xn[:, k, b * T:(b + 1) * T],
                                                   start=k == 0, stop=k == KC - 1)
                            mm.then_inc(up_ready, 1)
                        if n >= 1:
                            down(u, (n - 1) // TILES, (n - 1) % TILES)

            @block.scalar
            def _(act):
                if by_sigmoid:
                    act.wait_ge(logits_ready, 1)
                    act.activation(prob[:, :, :], ps[:, 0, 0:TT * E_ALL].rearrange("p (t e) -> p t e", e=E_ALL),
                                   ACT.Sigmoid).then_inc(prob_ready, 1)
                else:
                    act.wait_ge(r_step, 4)
                    act.activation(prob[:, :, :], also[:, :, :], ACT.Exp).then_inc(prob_ready, 1)
                for n in range(E_ALL * B):
                    act.wait_ge(share_ready, n + 1)
                    act.activation(share[:, n // B, n % B * T:(n % B + 1) * T], ps[:, n % 4, :],
                                   ACT.Copy).then_inc(share_copied, 1)
                with act.Fori(0, E_ALL // 2) as u:
                    for n in range(PER):
                        act.wait_ge(up_ready, u * PER + n + 1)
                        act.activation(act_h[:, n % 2, :], ps[:, n % 2, :], ACT.Silu).then_inc(silu_ready, 1)

            @block.vector
            def _(dve):
                def choose():
                    dve.wait_ge(r_loaded, (3 + by_sigmoid) * 16)
                    dve.wait_ge(logits_ready, 1)
                    logits = ps[:, 0, 0:TT * E_ALL].rearrange("p (t e) -> p t e", e=E_ALL)
                    if by_sigmoid:
                        dve.wait_ge(prob_ready, 1)
                        dve.tensor_tensor(choice[:, :, :], prob[:, :, :],
                                          bias[:, :].unsqueeze(1).broadcast_to([P, TT, E_ALL]),
                                          ALU.add).then_inc(r_step, 1)
                    else:
                        dve.tensor_copy(choice[:, :, :], logits).then_inc(r_step, 1)
                    dve.wait_ge(r_step, 1)
                    for tt in range(TT):
                        last = dve.max(best[:, tt, :], choice[:, tt, :])
                    last.then_inc(r_step, 1)
                    dve.wait_ge(r_step, 2)
                    for tt in range(TT):
                        last = dve.max_index(where[:, tt, :], best[:, tt, :], choice[:, tt, :])
                    last.then_inc(r_step, 1)
                    dve.wait_ge(r_step, 3)
                    dve.tensor_tensor(also[:, :, :], choice[:, :, :],
                                      best[:, :, 0:1].broadcast_to([P, TT, E_ALL]),
                                      ALU.subtract).then_inc(r_step, 1)
                    dve.tensor_copy(index[:, :, :], where[:, :, :]).then_inc(r_step, 1)
                    dve.wait_ge(r_step, 5)
                    dve.tensor_tensor(taken[:, :, :], order[:, :, :],
                                      index[:, :, 0:1].broadcast_to([P, TT, E_ALL]),
                                      ALU.is_equal).then_inc(r_step, 1)
                    dve.wait_ge(prob_ready, 1)
                    dve.tensor_tensor(also[:, :, :], order[:, :, :],
                                      index[:, :, 1:2].broadcast_to([P, TT, E_ALL]),
                                      ALU.is_equal).then_inc(r_step, 1)
                    dve.wait_ge(r_step, 7)
                    dve.tensor_tensor(taken[:, :, :], taken[:, :, :], also[:, :, :], ALU.add).then_inc(r_step, 1)
                    dve.wait_ge(r_step, 8)
                    dve.tensor_tensor(taken[:, :, :], taken[:, :, :], prob[:, :, :], ALU.mult).then_inc(r_step, 1)
                    dve.wait_ge(r_step, 9)
                    dve.tensor_reduce(norm[:, :], taken[:, :, :], AX.X, ALU.add).then_inc(r_step, 1)
                    dve.wait_ge(r_step, 10)
                    dve.reciprocal(norm[:, :], norm[:, :]).then_inc(r_step, 1)
                    dve.wait_ge(r_step, 11)
                    dve.tensor_tensor(taken[:, :, :], taken[:, :, :],
                                      norm[:, :].unsqueeze(2).broadcast_to([P, TT, E_ALL]),
                                      ALU.mult).then_inc(routed, 1)

                choose()
                dve.sem_inc(gated_ready, 2)
                dve.sem_inc(part_ready, 4)
                dve.wait_ge(share_copied, E_ALL * B)
                if looked_up is not None:
                    dve.memset(looked_up[:, :], 0.0).then_inc(summed, 1)
                    dve.wait_ge(t_loaded, 3 * 16)

                def look_up(u, n):
                    e, q = u * (LUT * 2 // E_ALL) + n // 4, n % 4
                    part = slice(q * LOOKED // 4, (q + 1) * LOOKED // 4)
                    dve.tensor_scalar(term[:, n % 2, :], index_in[:, part], entry[:, bass.ds(e, 1)],
                                      table[:, bass.ds(e, 1)], ALU.is_equal, ALU.mult).then_inc(term_ready, 1)
                    dve.wait_ge(term_ready, u * PER + n + 1)
                    dve.wait_ge(summed, u * PER + n + 1)
                    dve.tensor_tensor(looked_up[:, part], looked_up[:, part], term[:, n % 2, :],
                                      ALU.add).then_inc(summed, 1)

                def weigh(u, v):
                    for b in range(B):
                        dve.wait_ge(down_done, u * PER + (v + 1) * TILES - B + b + 1 + 4)
                        for m in range(KC):
                            n = b * KC + m
                            dve.wait_ge(added, 8 * u + 4 * v + n + 1)
                            dve.tensor_tensor(part_out[:, n, :], ps[:, 4 + n, :],
                                              share[:, u * 2 + v, b * T:(b + 1) * T],
                                              ALU.mult).then_inc(part_ready, 1)

                with dve.Fori(0, E_ALL // 2) as u:
                    for n in range(PER):
                        dve.wait_ge(silu_ready, u * PER + n + 1)
                        dve.wait_ge(down_done, u * PER + n + 1)
                        dve.tensor_tensor(gated[:, n % 4, :], act_h[:, n % 2, :], ps[:, 2 + n % 2, :],
                                          ALU.mult).then_inc(gated_ready, 1)
                        if n == TILES + 1:
                            weigh(u, 0)
                        if looked_up is not None:
                            look_up(u, n)
                    weigh(u, 1)

            @block.gpsimd
            def _(pool):
                pool.sem_inc(down_done, 4)
                pool.sem_inc(added, 4)
                with pool.Fori(0, E_ALL // 2) as u:
                    for v in range(2):
                        for b in range(B):
                            for m in range(KC):
                                n = b * KC + m
                                part = x[:, m, b * T:(b + 1) * T]
                                pool.wait_ge(part_ready, 8 * u + 4 * v + n + 1 + 4)
                                pool.wait_ge(added, 8 * u + 4 * v + n + 1)
                                pool.tensor_tensor(part, part, part_out[:, n, :], ALU.add).then_inc(added, 1)


LUT = 16
WIDE = 688
WF = -(-WIDE // P)
LOOKED = 2 * KC * WIDE + WF * C


def looked_up_layer(nc, ps, weights, x, xn):
    with Stage(nc, "f3") as s:
        act_h, gated = s.buf("act_h", [P, 2, T]), s.buf("gated", [P, 4, T])
        up_ready, silu_ready, gated_ready, down_done, added = (
            s.sem("up_ready"), s.sem("silu_ready"), s.sem("gated_ready"), s.sem("down_done"), s.sem("added"))
        w_gate = weights[:, 0:KC * WIDE].rearrange("p (k n) -> p k n", k=KC)
        w_up = weights[:, KC * WIDE:2 * KC * WIDE].rearrange("p (k n) -> p k n", k=KC)
        w_down = weights[:, 2 * KC * WIDE:].rearrange("p (f n) -> p f n", f=WF)
        TILES = WF * B

        def tile(t):
            return t // B, t % B, min(P, WIDE - t // B * P)

        with nc.Block() as block:

            @block.tensor
            def _(pe):
                def down(t):
                    f, b, rows = tile(t)
                    pe.wait_ge(gated_ready, t + 1)
                    for m in range(KC):
                        mm = pe.matmul(ps[:, 4 + b * KC + m, :], w_down[0:rows, f, m * P:(m + 1) * P],
                                       gated[0:rows, t % 4, :], start=f == 0, stop=f == WF - 1)
                    mm.then_inc(down_done, 1)

                for t in range(TILES):
                    f, b, rows = tile(t)
                    if t >= 2:
                        pe.wait_ge(gated_ready, t - 1)
                    for w, bank in ((w_gate, 0), (w_up, 2)):
                        for k in range(KC):
                            mm = pe.matmul(ps[0:rows, bank + t % 2, :], w[:, k, f * P:f * P + rows],
                                           xn[:, k, b * T:(b + 1) * T], start=k == 0, stop=k == KC - 1)
                    mm.then_inc(up_ready, 1)
                    if t >= 1:
                        down(t - 1)
                down(TILES - 1)

            @block.scalar
            def _(act):
                for t in range(TILES):
                    f, b, rows = tile(t)
                    act.wait_ge(up_ready, t + 1)
                    act.activation(act_h[0:rows, t % 2, :], ps[0:rows, t % 2, :], ACT.Silu).then_inc(silu_ready, 1)

            @block.vector
            def _(dve):
                for t in range(TILES):
                    f, b, rows = tile(t)
                    dve.wait_ge(silu_ready, t + 1)
                    if t >= 4:
                        dve.wait_ge(down_done, t - 3)
                    dve.tensor_tensor(gated[0:rows, t % 4, :], act_h[0:rows, t % 2, :],
                                      ps[0:rows, 2 + t % 2, :], ALU.mult).then_inc(gated_ready, 1)
                for b in range(B):
                    dve.wait_ge(down_done, TILES - B + b + 1)
                    for m in range(KC):
                        part = x[:, m, b * T:(b + 1) * T]
                        dve.tensor_tensor(part, part, ps[:, 4 + b * KC + m, :], ALU.add).then_inc(added, 1)


def hadamard_layer(nc, ps, d, x, xn):
    INTER = 1024
    FT = INTER // P
    with Stage(nc, "f1") as s:
        w_gate, w_up = s.buf("w_gate", [P, KC, INTER]), s.buf("w_up", [P, KC, INTER])
        w_raw, w_mid = s.buf("w_raw", [P, FT, C]), s.buf("w_mid", [P, FT, C])
        w_down = s.buf("w_down", [P, FT, C])
        had = s.buf("had", [P, P])
        su_ug, su_dp = s.buf("su_ug", [P, KC]), s.buf("su_dp", [P, FT])
        sc_up, sc_gate, sc_dp = s.buf("sc_up", [P, FT]), s.buf("sc_gate", [P, FT]), s.buf("sc_dp", [P, KC])
        sc_both = s.buf("sc_both", [P, FT])
        signed, mixed = s.buf("signed", [P, KC, N]), s.buf("mixed", [P, KC, N])
        xh = s.buf("xh", [P, KC, N])
        act_h, gated = s.buf("act_h", [P, 2, T]), s.buf("gated", [P, 4, T])
        small, w_loaded, down_loaded = s.sem("small"), s.sem("w_loaded"), s.sem("down_loaded")
        signed_ready, mixed_ready, xh_psum, xh_ready = (
            s.sem("signed_ready"), s.sem("mixed_ready"), s.sem("xh_psum"), s.sem("xh_ready"))
        w_step, w_psum, w_ready, both_ready = (
            s.sem("w_step"), s.sem("w_psum"), s.sem("w_ready"), s.sem("both_ready"))
        up_ready, silu_ready, gated_ready, down_done, added = (
            s.sem("up_ready"), s.sem("silu_ready"), s.sem("gated_ready"), s.sem("down_done"), s.sem("added"))
        TILES = FT * B

        with nc.Block() as block:

            @block.sync
            def _(sp):
                for to, of in ((su_ug, "f1_su_ug"), (had, "hadamard"), (su_dp, "f1_su_dp"), (sc_up, "f1_sc_up"),
                               (sc_gate, "f1_sc_gate"), (sc_dp, "f1_sc_dp")):
                    sp.dma_start(to[:, :], d[of]).then_inc(small, 16)
                sp.dma_start(w_raw[:, :, :], d["f1_w_down"].rearrange("(f p) n -> p f n", p=P)
                             ).then_inc(down_loaded, 16)
                for to, of in ((w_gate, "f1_w_gate"), (w_up, "f1_w_up")):
                    sp.dma_start(to[:, :, :], d[of].rearrange("(k p) n -> p k n", p=P)).then_inc(w_loaded, 16)

            @block.tensor
            def _(pe):
                pe.wait_ge(small, 6 * 16)
                for k in range(KC):
                    pe.wait_ge(mixed_ready, k + 1)
                    for b in range(B):
                        pe.matmul(ps[:, k * B + b, :], had[:, :], mixed[:, k, b * T:(b + 1) * T],
                                  start=True, stop=True).then_inc(xh_psum, 1)
                pe.wait_ge(w_step, 3)
                for q in range(4):
                    pe.matmul(ps[:, 4 + q, :], had[:, :],
                              w_mid[:, 2 * q:2 * q + 2, :].rearrange("p f n -> p (f n)"),
                              start=True, stop=True).then_inc(w_psum, 1)
                pe.wait_ge(w_loaded, 2 * 16)
                pe.wait_ge(xh_ready, KC * B)

                def down(t):
                    f, b = t // B, t % B
                    pe.wait_ge(gated_ready, t + 1)
                    if t < B:
                        pe.wait_ge(w_ready, 4)
                    for m in range(KC):
                        mm = pe.matmul(ps[:, 4 + b * KC + m, :], w_down[:, f, m * P:(m + 1) * P],
                                       gated[:, t % 4, :], start=f == 0, stop=f == FT - 1)
                    mm.then_inc(down_done, 1)

                for t in range(TILES):
                    f, b = t // B, t % B
                    if t >= 2:
                        pe.wait_ge(gated_ready, t - 1)
                    for w, bank in ((w_gate, 0), (w_up, 2)):
                        for k in range(KC):
                            mm = pe.matmul(ps[:, bank + t % 2, :], w[:, k, f * P:(f + 1) * P],
                                           xh[:, k, b * T:(b + 1) * T], start=k == 0, stop=k == KC - 1)
                    mm.then_inc(up_ready, 1)
                    if t >= 1:
                        down(t - 1)
                down(TILES - 1)

            @block.scalar
            def _(act):
                for n in range(KC * B):
                    act.wait_ge(xh_psum, n + 1)
                    act.activation(xh[:, n // B, n % B * T:(n % B + 1) * T], ps[:, n, :], ACT.Copy,
                                   scale=1.0 / 16).then_inc(xh_ready, 1)
                for q in range(4):
                    act.wait_ge(w_psum, q + 1)
                    act.activation(w_down[:, 2 * q:2 * q + 2, :].rearrange("p f n -> p (f n)"), ps[:, 4 + q, :],
                                   ACT.Copy, scale=1.0 / 32).then_inc(w_ready, 1)
                act.wait_ge(small, 6 * 16)
                for t in range(TILES):
                    act.wait_ge(up_ready, t + 1)
                    act.activation(act_h[:, t % 2, :], ps[:, t % 2, :], ACT.Silu,
                                   scale=sc_gate[:, t // B:t // B + 1]).then_inc(silu_ready, 1)

            @block.gpsimd
            def _(pool):
                pool.wait_ge(down_loaded, 16)
                for n, (of, to) in enumerate(((w_raw, w_mid), (w_mid, w_raw), (w_raw, w_mid))):
                    if n:
                        pool.wait_ge(w_step, n)
                    r = 1 << n
                    a = of[:, :, :].rearrange("p (q two r) n -> p q two (r n)", two=2, r=r)
                    o = to[:, :, :].rearrange("p (q two r) n -> p q two (r n)", two=2, r=r)
                    pool.tensor_tensor(o[:, :, 0, :], a[:, :, 0, :], a[:, :, 1, :], ALU.add)
                    pool.tensor_tensor(o[:, :, 1, :], a[:, :, 0, :], a[:, :, 1, :],
                                       ALU.subtract).then_inc(w_step, 1)

            @block.vector
            def _(dve):
                dve.wait_ge(small, 6 * 16)
                dve.tensor_tensor(sc_both[:, :], sc_up[:, :], su_dp[:, :], ALU.mult).then_inc(both_ready, 1)
                for k in range(KC):
                    dve.tensor_scalar(signed[:, k, :], xn[:, k, :], su_ug[:, k:k + 1], None,
                                      ALU.mult).then_inc(signed_ready, 1)
                dve.wait_ge(signed_ready, KC)
                for k, op in enumerate((ALU.add, ALU.subtract)):
                    dve.tensor_tensor(mixed[:, k, :], signed[:, 0, :], signed[:, 1, :], op).then_inc(mixed_ready, 1)
                dve.wait_ge(both_ready, 1)
                for t in range(TILES):
                    f = t // B
                    dve.wait_ge(silu_ready, t + 1)
                    if t >= 4:
                        dve.wait_ge(down_done, t - 3)
                    dve.scalar_tensor_tensor(gated[:, t % 4, :], ps[:, 2 + t % 2, :], sc_both[:, f:f + 1],
                                             act_h[:, t % 2, :], ALU.mult, ALU.mult).then_inc(gated_ready, 1)
                for b in range(B):
                    dve.wait_ge(down_done, TILES - B + b + 1)
                    for m in range(KC):
                        part = x[:, m, b * T:(b + 1) * T]
                        dve.scalar_tensor_tensor(part, ps[:, 4 + b * KC + m, :], sc_dp[:, m:m + 1], part,
                                                 ALU.mult, ALU.add).then_inc(added, 1)


KH, VPK = 16, 2
VH = KH * VPK
TAPS = 4
CH = T // P
PR = B * VPK


def delta_attention(nc, ps, d, x, xn):
    K_G, K_NBETA, K_BETA, K_NEG, K_LEFT, K_END, K_GC = range(7)
    KINDS = 7
    LEVELS = 6
    with Stage(nc, "a3") as s:
        w_ba, dt_bias, a_log = s.buf("w_ba", [P, KC, 2 * VH]), s.buf("dt_bias", [P, VH]), s.buf("a_log", [P, VH])
        taps = s.buf("taps", [P, KH, 4 * TAPS])
        nw = s.buf("nw", [P, 1])
        ident, upto, strict, floor = (s.buf(n, [P, P]) for n in ("ident", "upto", "strict", "floor"))
        ones = s.buf("ones", [P, P])
        half = s.buf("half", [P, PR])
        gates = s.buf("gates", [P, KINDS * TT, VH])
        z_a, z_b = s.buf("z_a", [P, TT, VH]), s.buf("z_b", [P, TT, VH])
        w_qkv, w_z = s.buf("w_qkv", [P, KC, 4 * P]), s.buf("w_z", [P, KC, VPK * P])
        w_out = s.buf("w_out", [P, VPK, C])
        raw = s.buf("raw", [P, 4, B, TAPS - 1 + T])
        qkv = s.buf("qkv", [P, 2, 4, B, T])
        zs = s.buf("zs", [P, 2, TT, VPK * P])
        cur = s.buf("cur", [P, 2, KINDS * TT, VPK])
        cur_taps = s.buf("cur_taps", [P, 4 * TAPS])
        low, decay, grown, rough = (s.buf(n, [P, PR, P]) for n in ("low", "decay", "grown", "rough"))
        v0, vt0 = s.buf("v0", [P, PR, P]), s.buf("vt0", [P, PR, P])
        vp, vtp = s.buf("vp", [P, 2, PR, P]), s.buf("vtp", [P, 2, PR, P])
        inv, at, qg = (s.buf(n, [P, 2, PR, P]) for n in ("inv", "at", "qg"))
        v_row, k_row = s.buf("v_row", [P, 2, PR, P]), s.buf("k_row", [P, 2, PR, P])
        state, rest, v_new = (s.buf(n, [P, PR, P]) for n in ("state", "rest", "v_new"))
        xf, sq, xnorm, out_t = (s.buf(n, [P, PR, P]) for n in ("xf", "sq", "xnorm", "out_t"))
        var, rstd = s.buf("var", [P, PR]), s.buf("rstd", [P, PR])

        def sems(*names):
            return [s.sem(n) for n in names]

        (small, filled, w1_loaded, wz_loaded, wo_loaded) = sems(
            "small", "filled", "w1_loaded", "wz_loaded", "wo_loaded")
        (filled_raw,) = sems("filled_raw")
        (ba_ready, g_act, g_step, sums_ready, gates_ready) = sems(
            "ba_ready", "g_act", "g_step", "sums_ready", "gates_ready")
        (proj_ready, raw_ready, conv_step, conv_ready, taps_ready, qkv_ready, z_ready, zs_ready) = sems(
            "proj_ready", "raw_ready", "conv_step", "conv_ready", "taps_ready", "qkv_ready", "z_ready",
            "zs_ready")
        (cur_ready, gc_ready, kq_ready, vrow_psum, krow_psum, low_ready, decay_ready, grown_ready) = sems(
            "cur_ready", "gc_ready", "kq_ready", "vrow_psum", "krow_psum", "low_ready", "decay_ready",
            "grown_ready")
        (at_ready, rough_ready, v0_ready, inv_ready, qg_ready, vrow_ready, krow_ready, vt0_psum, vt0_ready) = sems(
            "at_ready", "rough_ready", "v0_ready", "inv_ready", "qg_ready", "vrow_ready", "krow_ready",
            "vt0_psum", "vt0_ready")
        (sq_psum, sqt_psum, v_ready, vt_ready, v_by_dve, vt_by_dve, upd_psum) = sems(
            "sq_psum", "sqt_psum", "v_ready", "vt_ready", "v_by_dve", "vt_by_dve", "upd_psum")
        (ks_psum, rest_ready, x_psum, vnew_ready, o_psum, ds_psum, state_ready) = sems(
            "ks_psum", "rest_ready", "x_psum", "vnew_ready", "o_psum", "ds_psum", "state_ready")
        (xf_ready, sq_ready, var_ready, var_step, rstd_ready, xnorm_ready, ot_psum, ot_ready, y_psum, added) = sems(
            "xf_ready", "sq_ready", "var_ready", "var_step", "rstd_ready", "xnorm_ready", "ot_psum",
            "ot_ready", "y_psum", "added")
        SMALL = 10
        BG, BK, BT, BO, BSQ, BSQT, BUP, BR = range(8)
        PROJ = (BSQ, BSQT, BUP)

        def bank(n):
            return ps[:, n, :].rearrange("p (r t) -> p r t", r=PR)

        def gate(kind, hp, c, r):
            tt = r // VPK * CH + c
            return cur[:, hp, kind * TT + tt, r % VPK:r % VPK + 1]

        def chunk(hp, mt, b, c):
            return qkv[:, hp, mt, b, c * P:(c + 1) * P]

        PARTS = {0: (0, 1, 2), 1: (3, 4, 5), 2: (6, 7), 3: ()}
        BY_DVE = (2, 3, 4)

        def copied(per_head, h, c, n):
            return (per_head * CH - len(BY_DVE)) * h + per_head * c + n - (
                sum(m <= n for m in BY_DVE) if c == CH - 1 else 0)

        def wait_v(eng, h, c, n):
            if c == CH - 1 and n in BY_DVE:
                eng.wait_ge(v_by_dve, len(BY_DVE) * h + n - 1)
            else:
                eng.wait_ge(v_ready, copied(LEVELS - 1, h, c, n))

        def wait_vt(eng, h, c, n):
            if c == CH - 1 and n in BY_DVE:
                eng.wait_ge(vt_by_dve, len(BY_DVE) * h + n - 1)
            else:
                eng.wait_ge(vt_ready, copied(LEVELS, h, c, n))

        def run_heads(fori, waves):
            waves(0, 0, (0,), first=True)
            with fori(0, KH // 2 - 1) as i:
                for hp in range(2):
                    waves(i * 2 + hp, hp, (1, 2, 3))
                    waves(i * 2 + hp + 1, 1 - hp, (0,))
            waves(KH - 2, 0, (1, 2, 3))
            waves(KH - 1, 1, (0, 1, 2, 3), prepares=False)

        with nc.Block() as block:

            def load_qkv(eng, h):
                eng.dma_start(w_qkv[:, :, :], d["a3_w"][h, :, 0:4 * P].rearrange("(k p) n -> p k n", p=P)
                              ).then_inc(w1_loaded, 16)

            def load_z(eng, h):
                eng.dma_start(w_z[:, :, :], d["a3_w"][h, :, 4 * P:].rearrange("(k p) n -> p k n", p=P)
                              ).then_inc(wz_loaded, 16)

            def load_out(eng, h):
                eng.dma_start(w_out[:, :, :], d["a3_wo"][h, :, :].rearrange("(v p) n -> p v n", p=P)
                              ).then_inc(wo_loaded, 16)

            @block.sync
            def _(sp):
                sp.dma_start(w_ba[:, :, :], d["a3_w_ba"].rearrange("(k p) n -> p k n", p=P)).then_inc(small, 16)
                sp.dma_start(dt_bias[:, :], d["a3_dt"].partition_broadcast(P)).then_inc(small, 16)
                sp.dma_start(a_log[:, :], d["a3_a_log"].partition_broadcast(P)).then_inc(small, 16)
                sp.dma_start(taps[:, :, :], d["a3_taps"]).then_inc(small, 16)
                sp.dma_start(nw[:, :], d["a3_nw"]).then_inc(small, 16)
                for to, of in ((ident, "ident"), (upto, "upto"), (strict, "strict"), (floor, "floor"),
                               (ones, "ones")):
                    sp.dma_start(to[:, :], d[of]).then_inc(small, 16)
                load_qkv(sp, 0)
                load_z(sp, 0)
                load_out(sp, 0)
                sp.wait_ge(proj_ready, 8)
                load_qkv(sp, 1)
                sp.wait_ge(z_ready, 4)
                load_z(sp, 1)
                with sp.Fori(0, KH - 2) as i:
                    sp.wait_ge(proj_ready, 8 * i + 16)
                    load_qkv(sp, i + 2)
                    sp.wait_ge(z_ready, 4 * i + 8)
                    load_z(sp, i + 2)
                    sp.wait_ge(y_psum, CH * i + CH)
                    load_out(sp, i + 1)
                sp.wait_ge(y_psum, CH * (KH - 1))
                load_out(sp, KH - 1)

            @block.tensor
            def _(pe):
                def project(g, t, to):
                    mt, b = t // B, t % B
                    if t == 0:
                        pe.wait_ge(w1_loaded, 16 * g + 16)
                    for k in range(KC):
                        mm = pe.matmul(ps[:, to, :], w_qkv[:, k, mt * P:(mt + 1) * P],
                                       xn[:, k, b * T:(b + 1) * T], start=k == 0, stop=k == KC - 1)
                    mm.then_inc(proj_ready, 1)

                def project_z(g, n, to):
                    if n == 0:
                        pe.wait_ge(wz_loaded, 16 * g + 16)
                    for i in range(2):
                        tt = 2 * n + i
                        for k in range(KC):
                            mm = pe.matmul(ps[:, to, i * 256:(i + 1) * 256],
                                           xn[:, k, tt * P:(tt + 1) * P], w_z[:, k, :],
                                           start=k == 0, stop=k == KC - 1)
                    mm.then_inc(z_ready, 1)

                def part(h, w, c, n):
                    parts = PARTS[c]
                    if n >= (len(parts) if c < CH - 1 else 4):
                        return
                    if n == 0:
                        pe.wait_ge(low_ready, PR * w + 2 * PR)
                        pe.wait_ge(grown_ready, w + 2)
                    elif n == 1:
                        pe.wait_ge(rough_ready, w + 2)
                    elif c < CH - 1:
                        pe.wait_ge(raw_ready, 8 * h + 8 + parts[n - 2] + 1)
                    else:
                        pe.wait_ge(zs_ready, 4 * h + 4 + n - 1)
                    if c < CH - 1:
                        project(h + 1, parts[n], (BG, BK)[n % 2])
                    else:
                        project_z(h + 1, n, (BG, BK)[n % 2])

                def make(h, hp, w, c):
                    if c == 0:
                        pe.wait_ge(cur_ready, h + 1)
                    pe.wait_ge(low_ready, PR * w + PR)
                    pe.wait_ge(grown_ready, w + 1)
                    for r in range(PR):
                        mm = pe.matmul(bank(BG)[:, r, :], gate(K_G, hp, c, r).to_broadcast([P, P]), upto[:, :],
                                       start=True, stop=True)
                    mm.then_inc(gc_ready, 1)
                    pe.wait_ge(rough_ready, w + 1)
                    if c == 0:
                        pe.wait_ge(qkv_ready, 4 * h + 4)
                    for b in range(B):
                        pe.matmul(bank(BK)[:, b, :], chunk(hp, 1, b, c), chunk(hp, 1, b, c), start=True, stop=True)
                    for b in range(B):
                        mm = pe.matmul(bank(BK)[:, B + b, :], chunk(hp, 1, b, c), chunk(hp, 0, b, c),
                                       start=True, stop=True)
                    mm.then_inc(kq_ready, 1)
                    pe.wait_ge(vt0_ready, w + 1)
                    for r in range(PR):
                        mm = pe.transpose(bank(BT)[:, r, :], chunk(hp, 2 + r % VPK, r // VPK, c), ident[:, :])
                    mm.then_inc(vrow_psum, 1)

                def make_keys(hp, w, c):
                    pe.wait_ge(vrow_ready, w + 1)
                    for b in range(B):
                        mm = pe.transpose(bank(BT)[:, b, :], chunk(hp, 1, b, c), ident[:, :])
                    mm.then_inc(krow_psum, 1)

                def turn(w):
                    pe.wait_ge(krow_ready, PR * w + PR)
                    pe.wait_ge(v0_ready, PR * w + PR)
                    for r in range(PR):
                        mm = pe.transpose(bank(BT)[:, r, :], v0[:, r, :], ident[:, :])
                    mm.then_inc(vt0_psum, 1)

                def level(h, w, c, n):
                    if n == 1:
                        pe.wait_ge(vt0_ready, w + 1 + 1)
                        a, a_t = v0[:, :, :], vt0[:, :, :]
                    else:
                        wait_v(pe, h, c, n - 1)
                        wait_vt(pe, h, c, n - 1)
                        a, a_t = vp[:, (n - 1) % 2, :, :], vtp[:, (n - 1) % 2, :, :]
                    if n < LEVELS:
                        for r in range(PR):
                            mm = pe.matmul(bank(BSQ)[:, r, :], a_t[:, r, :], a[:, r, :], start=True, stop=True)
                        mm.then_inc(sq_psum, 1)
                    for r in range(PR):
                        mm = pe.matmul(bank(BSQT)[:, r, :], a[:, r, :], a_t[:, r, :], start=True, stop=True)
                    mm.then_inc(sqt_psum, 1)

                def update(h, w, c, n):
                    wait_vt(pe, h, c, n)
                    pe.wait_ge(inv_ready, (LEVELS + 1) * w + n)
                    for r in range(PR):
                        mm = pe.matmul(bank(BUP)[:, r, :], vtp[:, n % 2, r, :], inv[:, c % 2, r, :],
                                       start=True, stop=True)
                    mm.then_inc(upd_psum, 1)

                def recall(hp, w, c):
                    pe.wait_ge(ot_ready, w + 1)
                    pe.wait_ge(state_ready, PR * w + PR)
                    for b in range(B):
                        mm = pe.matmul(bank(BR)[:, VPK * b:VPK * (b + 1), :], chunk(hp, 1, b, c),
                                       state[:, VPK * b:VPK * (b + 1), :], start=True, stop=True)
                    mm.then_inc(ks_psum, 1)

                def solve(w, c):
                    pe.wait_ge(rest_ready, PR * w + PR)
                    pe.wait_ge(inv_ready, (LEVELS + 1) * (w + 1))
                    for r in range(PR):
                        mm = pe.matmul(bank(BR)[:, r, :], inv[:, c % 2, r, :], rest[:, r, :],
                                       start=True, stop=True)
                    mm.then_inc(x_psum, 1)

                def answer(w, c):
                    pe.wait_ge(vnew_ready, PR * w + PR)
                    pe.wait_ge(at_ready, w + 1)
                    pe.wait_ge(qg_ready, w + 1)
                    pe.wait_ge(added, w + 1)
                    for r in range(PR):
                        pe.matmul(bank(BO)[:, r, :], qg[:, c % 2, r, :], state[:, r, :], start=True, stop=False)
                        mm = pe.matmul(bank(BO)[:, r, :], at[:, c % 2, r, :], v_new[:, r, :],
                                       start=False, stop=True)
                    mm.then_inc(o_psum, 1)
                    if c == CH - 1:
                        return
                    for r in range(PR):
                        mm = pe.matmul(bank(BR)[:, r, :], k_row[:, c % 2, r, :], v_new[:, r, :],
                                       start=True, stop=True)
                    mm.then_inc(ds_psum, 1)

                def turn_out(w):
                    pe.wait_ge(state_ready, PR * w + 2 * PR)
                    pe.wait_ge(xnorm_ready, w + 1)
                    for r in range(PR):
                        mm = pe.transpose(bank(BR)[:, r, :], xnorm[:, r, :], ident[:, :])
                    mm.then_inc(ot_psum, 1)

                def project_out(h, w, c):
                    if c == 0:
                        pe.wait_ge(wo_loaded, 16 * h + 16)
                    pe.wait_ge(ot_ready, w + 1 + 1)
                    for m in range(KC):
                        for v in range(VPK):
                            mm = pe.matmul(bank(BO)[:, B * m:B * (m + 1), :], w_out[:, v, m * P:(m + 1) * P],
                                           out_t[:, v::VPK, :], start=v == 0, stop=v == VPK - 1)
                    mm.then_inc(y_psum, 1)

                def waves(h, hp, chunks, first=False, prepares=True):
                    for c in chunks:
                        w = CH * h + c
                        after = prepares or c < CH - 1
                        nh, nhp, n = (h, hp, c + 1) if c < CH - 1 else (h + 1, 1 - hp, 0)
                        before = not first
                        bh, bhp, b = (h, hp, c - 1) if c else (h - 1, 1 - hp, CH - 1)
                        level(h, w, c, 1)
                        if prepares:
                            part(h, w, c, 0)
                        if before:
                            recall(bhp, w - 1, b)
                        level(h, w, c, 2)
                        update(h, w, c, 1)
                        if prepares:
                            part(h, w, c, 1)
                        if before:
                            solve(w - 1, b)
                        level(h, w, c, 3)
                        update(h, w, c, 2)
                        if prepares:
                            part(h, w, c, 2)
                        if before:
                            answer(w - 1, b)
                        if prepares:
                            part(h, w, c, 3)
                        level(h, w, c, 4)
                        update(h, w, c, 3)
                        if after:
                            if prepares and c < CH - 1:
                                pe.wait_ge(raw_ready, 8 * h + 8 + PARTS[c][-1] + 1)
                            elif prepares:
                                pe.wait_ge(zs_ready, 4 * h + 8)
                            make(nh, nhp, w + 1, n)
                        level(h, w, c, 5)
                        update(h, w, c, 4)
                        if after:
                            make_keys(nhp, w + 1, n)
                        level(h, w, c, 6)
                        if before:
                            turn_out(w - 1)
                        update(h, w, c, 5)
                        if after:
                            turn(w + 1)
                        if before:
                            project_out(bh, w - 1, b)
                        update(h, w, c, 6)

                pe.wait_ge(small, SMALL * 16)
                for tt in range(TT):
                    for k in range(KC):
                        mm = pe.matmul(ps[:, 0, tt * 2 * VH:(tt + 1) * 2 * VH], xn[:, k, tt * P:(tt + 1) * P],
                                       w_ba[:, k, :], start=k == 0, stop=k == KC - 1)
                mm.then_inc(ba_ready, 1)
                for t in range(8):
                    if t >= 3:
                        pe.wait_ge(raw_ready, t - 2)
                    project(0, t, PROJ[t % 3])
                pe.wait_ge(g_step, 4)
                g_all = gates[:, K_G * TT:(K_G + 1) * TT, :].rearrange("p t v -> p (t v)")
                pe.matmul(ps[:, 1, 0:TT * VH], upto[:, :], g_all, start=True, stop=True)
                pe.matmul(ps[:, 2, 0:TT * VH], ones[:, :], g_all, start=True, stop=True).then_inc(sums_ready, 1)
                for n in range(4):
                    pe.wait_ge(raw_ready, 8) if n < 3 else pe.wait_ge(zs_ready, n - 2)
                    project_z(0, n, PROJ[n % 3])
                make(0, 0, 0, 0)
                make_keys(0, 0, 0)
                turn(0)
                pe.wait_ge(zs_ready, 4)
                run_heads(pe.Fori, waves)
                w = CH * KH - 1
                pe.wait_ge(inv_ready, (LEVELS + 1) * (w + 1))
                recall(1, w, CH - 1)
                solve(w, CH - 1)
                answer(w, CH - 1)
                turn_out(w)
                project_out(KH - 1, w, CH - 1)

            @block.scalar
            def _(act):
                def copy_raw(g, t, of):
                    mt, b = t // B, t % B
                    act.wait_ge(proj_ready, 8 * g + t + 1)
                    if not (isinstance(g, int) and g == 0):
                        act.wait_ge(conv_ready, 4 * g - 3 + mt)
                    act.activation(raw[:, mt, b, TAPS - 1:], ps[:, of, :], ACT.Copy).then_inc(raw_ready, 1)

                def silu_z(g, gp, n, of):
                    act.wait_ge(z_ready, 4 * g + n + 1)
                    act.activation(zs[:, gp, 2 * n:2 * n + 2, :].rearrange("p t n -> p (t n)"),
                                   ps[:, of, :], ACT.Silu).then_inc(zs_ready, 1)

                def silu(g, gp, mt):
                    act.wait_ge(conv_ready, 4 * g + mt + 1)
                    act.activation(qkv[:, gp, mt, :, :], qkv[:, gp, mt, :, :], ACT.Silu).then_inc(qkv_ready, 1)

                def part(h, c, n):
                    if n < len(PARTS[c]):
                        copy_raw(h + 1, PARTS[c][n], (BG, BK)[n % 2])

                def make_rows(w, c):
                    act.wait_ge(vrow_psum, w + 1)
                    act.activation(v_row[:, c % 2, :, :], bank(BT), ACT.Copy).then_inc(vrow_ready, 1)

                def make(hp, w, c):
                    act.wait_ge(low_ready, PR * w + PR + PR)
                    act.activation(decay[:, :, :], low[:, :, :], ACT.Exp).then_inc(decay_ready, 1)
                    act.wait_ge(gc_ready, w + 1)
                    act.activation(grown[:, :, :], bank(BG), ACT.Exp).then_inc(grown_ready, 1)
                    act.wait_ge(krow_psum, w + 1)
                    for r in range(PR):
                        act.activation(k_row[:, c % 2, r, :], bank(BT)[:, r // VPK, :], ACT.Copy,
                                       scale=gate(K_LEFT, hp, c, r)).then_inc(krow_ready, 1)

                def turn(w):
                    act.wait_ge(vt0_psum, w + 1)
                    act.activation(vt0[:, :, :], bank(BT), ACT.Copy).then_inc(vt0_ready, 1)

                def level(w, n):
                    if n < LEVELS:
                        act.wait_ge(sq_psum, (LEVELS - 1) * w + n)
                        act.activation(vp[:, n % 2, :, :], bank(BSQ), ACT.Copy).then_inc(v_ready, 1)
                    act.wait_ge(sqt_psum, LEVELS * w + n)
                    act.activation(vtp[:, n % 2, :, :], bank(BSQT), ACT.Copy).then_inc(vt_ready, 1)

                def new_values(hp, w, c):
                    act.wait_ge(x_psum, w + 1)
                    for r in range(PR):
                        act.activation(v_new[:, r, :], bank(BR)[:, r, :], ACT.Copy,
                                       scale=gate(K_BETA, hp, c, r)).then_inc(vnew_ready, 1)

                def square(w):
                    act.wait_ge(xf_ready, w + 1)
                    act.activation(sq[:, :, :], xf[:, :, :], ACT.Square).then_inc(sq_ready, 1)

                def copy_out(w):
                    act.wait_ge(ot_psum, w + 1)
                    act.activation(out_t[:, :, :], bank(BR), ACT.Copy, scale=nw[:, 0:1]).then_inc(ot_ready, 1)

                def waves(h, hp, chunks, first=False, prepares=True):
                    for c in chunks:
                        w = CH * h + c
                        after = prepares or c < CH - 1
                        nhp, n = (hp, c + 1) if c < CH - 1 else (1 - hp, 0)
                        before = not first
                        bhp, b = (hp, c - 1) if c else (1 - hp, CH - 1)
                        level(w, 1)
                        if c < CH - 1:
                            if prepares:
                                part(h, c, 0)
                            level(w, 2)
                            if prepares:
                                part(h, c, 1)
                            if before:
                                new_values(bhp, w - 1, b)
                            level(w, 3)
                            if prepares:
                                part(h, c, 2)
                            level(w, 4)
                        elif prepares:
                            for m in range(4):
                                silu(h + 1, 1 - hp, m)
                                if m == 1:
                                    new_values(bhp, w - 1, b)
                                silu_z(h + 1, 1 - hp, m, (BG, BK)[m % 2])
                        else:
                            new_values(bhp, w - 1, b)
                        if before:
                            square(w - 1)
                        if after:
                            make_rows(w + 1, n)
                        level(w, 5)
                        if after:
                            make(nhp, w + 1, n)
                        level(w, 6)
                        if before:
                            copy_out(w - 1)
                        if after:
                            turn(w + 1)

                act.wait_ge(small, SMALL * 16)
                act.wait_ge(ba_ready, 1)
                ba = ps[:, 0, :].rearrange("p (t n) -> p t n", t=TT)
                act.activation(gates[:, K_BETA * TT:(K_BETA + 1) * TT, :], ba[:, :, 0:VH],
                               ACT.Sigmoid).then_inc(g_act, 1)
                for t in range(8):
                    copy_raw(0, t, PROJ[t % 3])
                act.wait_ge(g_step, 1)
                act.activation(z_b[:, :, :], z_a[:, :, :], ACT.Abs).then_inc(g_act, 1)
                act.wait_ge(g_act, 2)
                act.activation(z_b[:, :, :], z_b[:, :, :], ACT.Exp, scale=-1.0).then_inc(g_act, 1)
                act.wait_ge(g_act, 3)
                act.activation(z_b[:, :, :], z_b[:, :, :], ACT.Ln, bias=1.0).then_inc(g_act, 1)
                act.activation(a_log[:, :], a_log[:, :], ACT.Exp).then_inc(g_act, 1)
                act.wait_ge(g_step, 6)
                for kind, n in ((K_LEFT, 6), (K_NEG, 7), (K_END, 8)):
                    act.activation(gates[:, kind * TT:(kind + 1) * TT, :],
                                   gates[:, kind * TT:(kind + 1) * TT, :], ACT.Exp).then_inc(g_act, 1)
                act.sem_inc(grown_ready, 1)
                act.sem_inc(vt0_ready, 1)
                act.sem_inc(ot_ready, 1)
                for m in range(4):
                    silu(0, 0, m)
                for n in range(4):
                    silu_z(0, 0, n, PROJ[n % 3])
                act.wait_ge(cur_ready, 1)
                make_rows(0, 0)
                make(0, 0, 0)
                turn(0)
                run_heads(act.Fori, waves)
                w = CH * KH - 1
                new_values(1, w, CH - 1)
                square(w)
                copy_out(w)

            @block.gpsimd
            def _(pool):
                pool.memset(half[:, :], -0.5).then_inc(filled, 1)
                pool.wait_ge(filled, 1)

                def root(w):
                    pool.wait_ge(var_ready, w + 1)
                    pool.tensor_tensor(rstd[:, :], var[:, :], half[:, :], ALU.pow).then_inc(rstd_ready, 1)

                with pool.Fori(0, VH * 2) as w:
                    root(w)

            @block.vector
            def _(dve):
                def convolve(g, gp, mt, j):
                    if j == 0 and mt == 0:
                        dve.tensor_copy(cur_taps[:, :], taps[:, bass.ds(g, 1), :].rearrange("p h n -> p (h n)")
                                        if not isinstance(g, int) else taps[:, g, :]).then_inc(taps_ready, 1)
                        dve.wait_ge(taps_ready, g + 1)
                    tap = cur_taps[:, mt * TAPS + j:mt * TAPS + j + 1]
                    rows, to = raw[:, mt, :, j:j + T], qkv[:, gp, mt, :, :]
                    if j == 0:
                        dve.wait_ge(raw_ready, 8 * g + 2 * mt + 2)
                        dve.tensor_scalar(to, rows, tap, None, ALU.mult).then_inc(conv_step, 1)
                        return
                    dve.wait_ge(conv_step, 12 * g + 3 * mt + j)
                    dve.scalar_tensor_tensor(to, rows, tap, to, ALU.mult,
                                             ALU.add).then_inc(conv_ready if j == TAPS - 1 else conv_step, 1)

                def level(h, n):
                    w = CH * h + CH - 1
                    dve.wait_ge(sq_psum, (LEVELS - 1) * w + n)
                    dve.tensor_copy(vp[:, n % 2, :, :], bank(BSQ)).then_inc(v_by_dve, 1)
                    dve.wait_ge(sqt_psum, LEVELS * w + n)
                    dve.tensor_copy(vtp[:, n % 2, :, :], bank(BSQT)).then_inc(vt_by_dve, 1)

                def make_low(hp, w, c):
                    dve.wait_ge(gc_ready, w + 1)
                    for r in range(PR):
                        dve.scalar_tensor_tensor(low[:, r, :], bank(BG)[:, r, :], gate(K_GC, hp, c, r), floor[:, :],
                                                 ALU.subtract, ALU.min).then_inc(low_ready, 1)

                def make(hp, w, c):
                    dve.wait_ge(kq_ready, w + 1)
                    dve.wait_ge(decay_ready, w + 1)
                    kq = bank(BK)
                    for k, to in ((B, at[:, c % 2, :, :]), (0, rough[:, :, :])):
                        mm = dve.tensor_tensor(
                            to.rearrange("p (b v) t -> p b v t", b=B),
                            kq[:, k:k + B, :].unsqueeze(2).broadcast_to([P, B, VPK, P]),
                            decay[:, :, :].rearrange("p (b v) t -> p b v t", b=B), ALU.mult)
                        mm.then_inc(rough_ready if k == 0 else at_ready, 1)
                    dve.wait_ge(rough_ready, w + 1 + 1)
                    for r in range(PR):
                        dve.scalar_tensor_tensor(v0[:, r, :], rough[:, r, :], gate(K_NBETA, hp, c, r), strict[:, :],
                                                 ALU.mult, ALU.mult).then_inc(v0_ready, 1)

                def make_rest(hp, w, c):
                    dve.wait_ge(v0_ready, PR * w + PR)
                    dve.tensor_tensor(inv[:, c % 2, :, :], v0[:, :, :],
                                      ident[:, :].unsqueeze(1).broadcast_to([P, PR, P]), ALU.add
                                      ).then_inc(inv_ready, 1)
                    dve.wait_ge(grown_ready, w + 1 + 1)
                    dve.tensor_tensor(
                        qg[:, c % 2, :, :].rearrange("p (b v) t -> p b v t", b=B),
                        qkv[:, hp, 0, :, c * P:(c + 1) * P].unsqueeze(2).broadcast_to([P, B, VPK, P]),
                        grown[:, :, :].rearrange("p (b v) t -> p b v t", b=B), ALU.mult).then_inc(qg_ready, 1)

                def update(w, c, n):
                    dve.wait_ge(upd_psum, LEVELS * w + n)
                    dve.wait_ge(inv_ready, (LEVELS + 1) * w + n)
                    dve.tensor_tensor(inv[:, c % 2, :, :], inv[:, c % 2, :, :], bank(BUP), ALU.add
                                      ).then_inc(inv_ready, 1)

                def make_right(hp, w, c):
                    dve.wait_ge(ks_psum, w + 1)
                    dve.wait_ge(vrow_ready, w + 1)
                    for r in range(PR):
                        dve.scalar_tensor_tensor(rest[:, r, :], bank(BR)[:, r, :], gate(K_NEG, hp, c, r),
                                                 v_row[:, c % 2, r, :], ALU.mult, ALU.add).then_inc(rest_ready, 1)

                def gated(h, hp, w, c):
                    dve.wait_ge(o_psum, w + 1)
                    if c == 0:
                        dve.wait_ge(zs_ready, 4 * h + 4)
                    dve.scalar_tensor_tensor(xf[:, :, :].rearrange("p (b v) t -> p b (v t)", b=B),
                                             bank(BO).rearrange("p (b v) t -> p b (v t)", b=B), float(P) ** -0.5,
                                             zs[:, hp, c::CH, :], ALU.mult, ALU.mult).then_inc(xf_ready, 1)
                    if c == CH - 1:
                        dve.memset(state[:, :, :], 0.0).then_inc(state_ready, PR)
                        return
                    dve.wait_ge(ds_psum, (CH - 1) * h + c + 1)
                    for r in range(PR):
                        dve.scalar_tensor_tensor(state[:, r, :], state[:, r, :], gate(K_END, hp, c, r),
                                                 bank(BR)[:, r, :], ALU.mult, ALU.add).then_inc(state_ready, 1)

                def reduce(w):
                    dve.wait_ge(sq_ready, w + 1)
                    dve.tensor_reduce(var[:, :], sq[:, :, :], AX.X, ALU.add).then_inc(var_step, 1)
                    dve.wait_ge(var_step, w + 1)
                    dve.tensor_scalar(var[:, :], var[:, :], 1.0 / P, 1e-6, ALU.mult, ALU.add).then_inc(var_ready, 1)

                def normed(w):
                    dve.wait_ge(rstd_ready, w + 1)
                    dve.tensor_tensor(xnorm[:, :, :], xf[:, :, :],
                                      rstd[:, :].unsqueeze(2).broadcast_to([P, PR, P]), ALU.mult
                                      ).then_inc(xnorm_ready, 1)

                def add_out(w, c):
                    dve.wait_ge(y_psum, w + 1)
                    part = x[:, :, :].rearrange("p m (b t) -> p m b t", b=B)[:, :, :, c * P:(c + 1) * P]
                    dve.tensor_tensor(part, part, ps[:, BO, :].rearrange("p (m b t) -> p m b t", m=KC, b=B),
                                      ALU.add).then_inc(added, 1)

                def waves(h, hp, chunks, first=False, prepares=True):
                    for c in chunks:
                        w = CH * h + c
                        after = prepares or c < CH - 1
                        nhp, n = (hp, c + 1) if c < CH - 1 else (1 - hp, 0)
                        before = not first
                        bh, bhp, b = (h, hp, c - 1) if c else (h - 1, 1 - hp, CH - 1)
                        kinds = {0: (0,), 1: (1,), 2: (2, 3), 3: ()}[c] if prepares else ()
                        todo = [(kind, j) for kind in kinds for j in range(TAPS)]

                        def taps_of(many):
                            for kind, j in todo[:many]:
                                convolve(h + 1, 1 - hp, kind, j)
                            del todo[:many]

                        if before:
                            make_right(bhp, w - 1, b)
                        if c == CH - 1:
                            if prepares:
                                take_gates(h + 1, 1 - hp)
                            level(h, 2)
                        update(w, c, 1)
                        if c == 2:
                            taps_of(2)
                        if c == CH - 1:
                            level(h, 3)
                        update(w, c, 2)
                        if c == 2:
                            taps_of(2)
                        if before:
                            gated(bh, bhp, w - 1, b)
                        if c == CH - 1:
                            level(h, 4)
                        taps_of(1)
                        update(w, c, 3)
                        if before:
                            reduce(w - 1)
                        if after:
                            make_low(nhp, w + 1, n)
                        taps_of(1)
                        update(w, c, 4)
                        if before:
                            normed(w - 1)
                        if after:
                            make(nhp, w + 1, n)
                        update(w, c, 5)
                        if after:
                            make_rest(nhp, w + 1, n)
                        taps_of(1)
                        if before:
                            add_out(w - 1, b)
                        taps_of(1)
                        update(w, c, 6)

                def take_gates(g, gp):
                    dve.tensor_copy(cur[:, gp, :, :], gates[:, :, bass.ds(g * VPK, VPK)]).then_inc(cur_ready, 1)
                    dve.wait_ge(cur_ready, g + 1)

                dve.memset(raw[:, :, :, 0:TAPS - 1], 0.0).then_inc(filled_raw, 1)
                dve.wait_ge(filled_raw, 1)
                dve.wait_ge(small, SMALL * 16)
                dve.wait_ge(ba_ready, 1)
                ba = ps[:, 0, :].rearrange("p (t n) -> p t n", t=TT)
                dve.wait_ge(g_act, 1)
                dve.tensor_tensor(z_a[:, :, :], ba[:, :, VH:], dt_bias[:, :].unsqueeze(1).broadcast_to([P, TT, VH]),
                                  ALU.add).then_inc(g_step, 1)
                dve.wait_ge(g_act, 5)

                def kind(k):
                    return gates[:, k * TT:(k + 1) * TT, :]

                dve.scalar_tensor_tensor(z_b[:, :, :], z_a[:, :, :], 0.0, z_b[:, :, :], ALU.max,
                                         ALU.add).then_inc(g_step, 1)
                dve.tensor_scalar(a_log[:, :], a_log[:, :], -1.0, None, ALU.mult).then_inc(g_step, 1)
                dve.wait_ge(g_step, 3)
                dve.tensor_tensor(kind(K_G), z_b[:, :, :], a_log[:, :].unsqueeze(1).broadcast_to([P, TT, VH]),
                                  ALU.mult).then_inc(g_step, 1)
                dve.wait_ge(sums_ready, 1)
                gc = ps[:, 1, 0:TT * VH].rearrange("p (t v) -> p t v", t=TT)
                total = ps[:, 2, 0:TT * VH].rearrange("p (t v) -> p t v", t=TT)
                dve.tensor_copy(kind(K_GC), gc).then_inc(g_step, 1)
                dve.wait_ge(g_step, 5)
                dve.tensor_copy(kind(K_NEG), kind(K_GC))
                dve.tensor_copy(kind(K_END), total)
                dve.tensor_tensor(kind(K_LEFT), total, kind(K_GC), ALU.subtract).then_inc(g_step, 1)
                dve.tensor_scalar(kind(K_NBETA), kind(K_BETA), -1.0, None, ALU.mult).then_inc(g_step, 1)
                dve.wait_ge(g_act, 8)
                dve.wait_ge(g_step, 7)
                dve.tensor_scalar(kind(K_NEG), kind(K_NEG), -1.0, None, ALU.mult).then_inc(gates_ready, 1)
                dve.wait_ge(gates_ready, 1)
                dve.sem_inc(low_ready, PR)
                dve.sem_inc(rough_ready, 1)
                dve.sem_inc(added, 1)
                dve.memset(state[:, :, :], 0.0).then_inc(state_ready, PR)
                for mt in range(4):
                    for j in range(TAPS):
                        convolve(0, 0, mt, j)
                take_gates(0, 0)
                make_low(0, 0, 0)
                make(0, 0, 0)
                make_rest(0, 0, 0)
                run_heads(dve.Fori, waves)
                w = CH * KH - 1
                make_right(1, w, CH - 1)
                gated(KH - 1, 1, w, CH - 1)
                reduce(w)
                normed(w)
                add_out(w, CH - 1)


def _heads_padded(w, copies=1):
    k = w.shape[0]
    out = np.zeros((k, w.shape[1] // HD * copies, HP), np.float32)
    out[:, :, :HD] = np.repeat(w.reshape(k, -1, HD), copies, axis=1)
    return np.ascontiguousarray(out.reshape(k, -1))


def _blocks(m):
    return m.reshape(-1, P, m.shape[1]).transpose(1, 0, 2).reshape(P, -1)


def _constants():
    f = np.float32
    half = HD // 2
    frac = np.arange(0, HD, 2, dtype=f) / f(HD)
    inv = (f(1.0) / (f(10000.0) ** frac)).astype(f)
    ang = np.arange(T, dtype=f)[:, None] * inv[None, :]
    rope = np.zeros((P, 2, T), f)
    turn = np.zeros((P, P), f)
    sums_of = np.zeros((P, P), f)
    for p in range(P):
        r = p % HP
        if r < HD:
            rope[p, 0] = np.cos(ang[:, r % half])
            rope[p, 1] = np.sin(ang[:, r % half])
            if r < half:
                turn[p + half, p] = -1.0
            else:
                turn[p - half, p] = 1.0
        sums_of[p - r + HD, p] = 1.0
    rel = (np.arange(P)[:, None] + (T - P)) - np.arange(T)[None, :]
    away = np.where(rel < 0, f(1e30), rel).astype(f)
    had = np.ones((1, 1), f)
    while len(had) < P:
        had = np.block([[had, had], [had, -had]])
    start = 2.0 ** (-8.0 / NH)
    slopes = np.asarray([start * start ** i for i in range(NH)], f)
    return {
        "rope": rope, "turn": turn, "sums_of": sums_of, "ones": np.ones((P, P), f),
        "mean_of": np.full((P, P), 1.0 / C, f),
        "upto": np.triu(np.ones((P, P), f)), "strict": np.triu(np.ones((P, P), f), 1),
        "floor": np.where(np.triu(np.ones((P, P), bool)), f(0), f(-1e30)).astype(f),
        "ident": np.eye(P, dtype=f), "hadamard": had,
        "entry": np.tile(np.arange(LUT, dtype=f), (P, 1)),
        "away": away, "slopes": np.tile(slopes, (P, 1)),
        "order": np.tile(np.arange(E_ALL, dtype=f), (P, TT, 1)),
    }


def _arrays(i):
    a = _constants()
    a["x_t"] = i["L0_attn_x"].reshape(N, C).T
    a["a0_wq"] = _heads_padded(i["L0_attn_q_kernel"])
    a["a0_wk"] = _heads_padded(i["L0_attn_k_kernel"], HG)
    a["a0_wv"] = i["L0_attn_v_kernel"]
    a["a0_wo"] = _heads_padded(i["L0_attn_out_kernel"].T).T
    def columns(v):
        return v.reshape(-1, P).T

    a["a1_wq"] = _heads_padded(i["L1_attn_wq"])
    a["a1_wk"] = _heads_padded(i["L1_attn_wk"])
    a["a1_bq"] = columns(_heads_padded(i["L1_attn_bq"][None])[0])
    a["a1_bk"] = columns(_heads_padded(i["L1_attn_bk"][None])[0])
    a["a1_wv"], a["a1_bv"] = i["L1_attn_wv"], i["L1_attn_bv"]
    a["a1_wo"] = _heads_padded(i["L1_attn_wo"].T).T
    a["a1_bo"] = columns(i["L1_attn_bo"])
    a["a2_w"] = np.stack([i["L2_attn_W" + c].T for c in "qkv"])
    a["a2_bias"] = np.stack([columns(i["L2_attn_b" + c]) for c in "qkv"], axis=1)
    a["a2_wo"], a["a2_bo"] = i["L2_attn_Wo"].T, columns(i["L2_attn_bo"])
    a["f0_wr"] = i["L0_ffn_router_w"]
    a["f0_w1"], a["f0_w3"], a["f0_w2"] = i["L0_ffn_w1"], i["L0_ffn_v1"], i["L0_ffn_w2"]
    a["f2_wr"], a["f2_bias"] = i["L2_ffn_Wg"].T, i["L2_ffn_bias"]
    for w in ("W1", "W3", "W2"):
        a["f2_" + w.lower()] = i["L2_ffn_" + w].transpose(0, 2, 1)
    a["f1_su_ug"], a["f1_su_dp"] = columns(i["L1_ffn_SU_ug"]), columns(i["L1_ffn_SU_dp"])
    a["f1_sc_up"], a["f1_sc_gate"] = (columns(v) for v in np.split(i["L1_ffn_Wscale_ug"], 2))
    a["f1_sc_dp"] = columns(i["L1_ffn_Wscale_dp"])
    for w in ("up", "gate", "down"):
        a["f1_w_" + w] = i["L1_ffn_W_" + w].T
    down = np.zeros((WF * P, C), np.int32)
    down[:WIDE] = i["L3_ffn_down_idx"].T
    a["f3_index"] = np.concatenate(
        [_blocks(i["L3_ffn_gate_idx"].T), _blocks(i["L3_ffn_up_idx"].T), _blocks(down)], axis=1)
    a["f3_lut"] = i["L3_ffn_lut"]
    a["a3_w"] = i["L3_attn_W_qkvz"].reshape(C, KH, 6 * P).transpose(1, 0, 2)
    a["a3_wo"] = i["L3_attn_W_out"].reshape(KH, VPK * P, C)
    a["a3_w_ba"] = i["L3_attn_W_ba"].reshape(C, KH, 2, VPK).transpose(0, 2, 1, 3).reshape(C, 2 * VH)
    taps = i["L3_attn_conv_kernel"].reshape(TAPS, -1)
    q_taps, k_taps = (t.reshape(TAPS, KH, 1, P) for t in (taps[:, :KH * P], taps[:, KH * P:2 * KH * P]))
    by_head = np.concatenate([q_taps, k_taps, taps[:, 2 * KH * P:].reshape(TAPS, KH, VPK, P)], axis=2)
    a["a3_taps"] = by_head.transpose(3, 1, 2, 0).reshape(P, KH, 4 * TAPS)
    a["a3_dt"], a["a3_a_log"] = i["L3_attn_dt_bias"], i["L3_attn_A_log"]
    a["a3_nw"] = i["L3_attn_norm_weight"][:, None]
    return {k: np.ascontiguousarray(v) for k, v in a.items()}


ALL = ("n0", "a0", "f0", "n1", "a1", "f1", "n2", "a2", "f2", "n3", "a3", "f3")


def build(nc, d, stages=ALL):
    with Stage(nc, "all") as s:
        x, xn, mean_of = s.buf("x", [P, KC, N]), s.buf("xn", [P, KC, N]), s.buf("mean_of", [P, P])
        looked_up = s.buf("looked_up", [P, LOOKED])
        ps = s.ctx.enter_context(nc.psum_tensor("ps", [P, 8, BANK], F32))
        arrived, stored = s.sem("arrived"), s.sem("stored")
        with nc.Block() as block:
            @block.sync
            def _(sp):
                sp.dma_start(x[:, :, :], d["x_t"].rearrange("(k p) t -> p k t", p=P)).then_inc(arrived, 16)
                sp.dma_start(mean_of[:, :], d["mean_of"]).then_inc(arrived, 16)
                sp.wait_ge(arrived, 32)
        if "n0" in stages:
            layer_norm(nc, "n0", ps, x, xn, mean_of)
        if "a0" in stages:
            rope_attention(nc, ps, d, x, xn)
        if "f0" in stages:
            expert_layer(nc, "f0", ps, d, x, xn, 512, False, looked_up)
        if "n1" in stages:
            layer_norm(nc, "n1", ps, x, xn, mean_of)
        if "a1" in stages:
            alibi_attention(nc, ps, d, x, xn)
        if "f1" in stages:
            hadamard_layer(nc, ps, d, x, xn)
        if "n2" in stages:
            layer_norm(nc, "n2", ps, x, xn, mean_of)
        if "a2" in stages:
            linear_attention(nc, ps, d, x, xn)
        if "f2" in stages:
            expert_layer(nc, "f2", ps, d, x, xn, 128, True)
        if "n3" in stages:
            layer_norm(nc, "n3", ps, x, xn, mean_of)
        if "a3" in stages:
            delta_attention(nc, ps, d, x, xn)
        if "f3" in stages:
            looked_up_layer(nc, ps, looked_up, x, xn)
        with nc.Block() as block:
            @block.sync
            def _(sp):
                sp.dma_start(d["out_t"].rearrange("(k p) t -> p k t", p=P), x[:, :, :]).then_inc(stored, 16)
                sp.wait_ge(stored, 16)


def kernel(**inputs):
    import concourse.bacc as bacc
    from concourse.bass_utils import run_bass_kernel_spmd

    nc = bacc.Bacc("TRN2", target_bir_lowering=False, num_devices=1)
    arrays = _arrays({k: np.asarray(v) for k, v in inputs.items()})
    d = {k: nc.dram_tensor(f"in_{k}", v.shape, mybir.dt.from_np(v.dtype), kind="ExternalInput").ap()
         for k, v in arrays.items()}
    d["out_t"] = nc.dram_tensor("out_t", (C, N), F32, kind="ExternalOutput").ap()
    build(nc, d)
    r = run_bass_kernel_spmd(nc, [{f"in_{k}": v for k, v in arrays.items()}], core_ids=[0])
    return np.ascontiguousarray(r.results[0]["out_t"].T).reshape(B, T, C)
```
